# Optimizing a Trainium2 kernel written in Bass

```python
import numpy as np
import jax
import jax.numpy as jnp

def _softmax(x, axis=-1):
    return jax.nn.softmax(x, axis=axis)

def _gelu(x):
    return jax.nn.gelu(x, approximate=True)

def _silu(x):
    return jax.nn.silu(x)

def _sigmoid(x):
    return jax.nn.sigmoid(x)

def _layernorm(x, axis=-1, eps=1e-05):
    m = jnp.mean(x, axis=axis, keepdims=True)
    v = jnp.var(x, axis=axis, keepdims=True)
    return (x - m) / jnp.sqrt(v + eps)

def _scatter_add(tgt, idx, src, axis=0):
    return tgt.at[idx].add(src)

def _segment_sum(src, seg, n):
    return jax.ops.segment_sum(src, seg, n)
kernel_name = 'mk_decoder_postln_d2_seqx_r8_98fb0b'

def setup_inputs(seed: int=0):
    np.random.seed(seed)
    _w = jnp.asarray

    def _rec_inputs():
        import jax
        import jax.numpy as jnp
        _rk = jax.random.key(seed)
        x = -0.0005207 + 1.001 * jax.random.normal(jax.random.fold_in(_rk, 1), (8, 128, 512), jnp.float32)
        _lenS = 128 - jax.random.randint(jax.random.fold_in(_rk, 7), (8,), 0, max(1, 128 // 4) + 1, jnp.int32)
        _lenS2 = 128 - jax.random.randint(jax.random.fold_in(_rk, 8), (8,), 0, max(1, 128 // 4) + 1, jnp.int32)
        _ctx_4096P = jax.random.normal(jax.random.fold_in(_rk, 11), (8, 16, 512), jnp.float32)
        _ctx_4096c = jax.random.dirichlet(jax.random.fold_in(_rk, 511), 0.3 * jnp.ones((16,), jnp.float32), (8, 128))
        _ctx_4096t = jnp.einsum('bsk,bkd->bsd', _ctx_4096c, _ctx_4096P)
        _ctx_4096t = _ctx_4096t * jax.lax.rsqrt(jnp.mean(jnp.square(_ctx_4096t)) + 1e-12) * 0.953939
        ctx_4096 = -0.00010331 + 0.999899 * (_ctx_4096t + 0.3 * jax.random.normal(jax.random.fold_in(_rk, 611), (8, 128, 512), jnp.float32))
        _validS = jnp.arange(128)[None, :] < _lenS[:, None]
        _validS2 = jnp.arange(128)[None, :] < _lenS2[:, None]
        _causal = jnp.tril(jnp.ones((128, 128), dtype=bool))
        mask_1x1xSxS2_ff0 = jnp.where(jnp.ones((1, 1, 128, 128), dtype=bool), 0.0, -1000000000.0).astype(jnp.float32)
        return (x, ctx_4096, mask_1x1xSxS2_ff0)
    x, ctx_4096, mask_1x1xSxS2_ff0 = _rec_inputs()

    def _L0_attn_setup():
        import jax, jax.numpy as jnp
        import numpy as np
        HID = 512
        DM = 128
        DIN = 2 * DM
        DST = 16
        HD = 64
        NH = DIN // HD
        DCONV = 7
        CONV_DIM = DIN + 2 * DST
        DIN_PROJ = 2 * DIN + 2 * DST + 2 * NH
        SEQ, BATCH = (256, 4)

        def _causal_conv(x, w, b):
            y = jax.lax.conv_general_dilated(jnp.transpose(x, (0, 2, 1)), w, (1,), [(DCONV - 1, 0)], feature_group_count=CONV_DIM, dimension_numbers=('NCH', 'OIH', 'NCH'))
            return jnp.transpose(y, (0, 2, 1)) + b

        def _ssm_scan(x, dt, A, B, C):
            dA = jnp.exp(dt * A)
            dBx = dt[..., None] * x

            def step(h, t):
                dA_t, dBx_t, B_t, C_t = t
                h = dA_t[:, :, None, None] * h + dBx_t[..., None] * B_t[:, None, None, :]
                y = jnp.einsum('bhpn,bn->bhp', h, C_t)
                return (h, y)
            h0 = jnp.zeros((x.shape[0], NH, HD, DST), x.dtype)
            _, ys = jax.lax.scan(step, h0, (jnp.moveaxis(dA, 1, 0), jnp.moveaxis(dBx, 1, 0), jnp.moveaxis(B, 1, 0), jnp.moveaxis(C, 1, 0)))
            return jnp.moveaxis(ys, 0, 1)

        def _hydra(u, in_w, conv_w, conv_b, dt_bias, A_log, D, fcD_w, norm_w, out_w):
            b, l, _ = u.shape
            zxbcdt = u @ in_w.T
            z = zxbcdt[..., :DIN]
            xBC = zxbcdt[..., DIN:DIN + CONV_DIM]
            dt2 = zxbcdt[..., DIN + CONV_DIM:]
            dt_fw = jax.nn.softplus(dt2[..., :NH] + dt_bias)
            dt_bw = jax.nn.softplus(jnp.flip(dt2[..., NH:], 1) + dt_bias)
            xBC = jax.nn.silu(_causal_conv(xBC, conv_w, conv_b))
            xs = xBC[..., :DIN]
            Bm = xBC[..., DIN:DIN + DST]
            Cm = xBC[..., DIN + DST:]
            A = -jnp.exp(A_log)
            x4 = xs.reshape(b, l, NH, HD)
            y_fw = _ssm_scan(x4, dt_fw, A, Bm, Cm).reshape(b, l, DIN)
            y_bw = jnp.flip(_ssm_scan(jnp.flip(x4, 1), dt_bw, A, jnp.flip(Bm, 1), jnp.flip(Cm, 1)).reshape(b, l, DIN), 1)
            zero = jnp.zeros((b, 1, DIN), u.dtype)
            y = jnp.concatenate([zero, y_fw[:, :-1]], 1) + jnp.concatenate([y_bw[:, 1:], zero], 1)
            y = y + xs * jnp.repeat(xs @ fcD_w.T + D, HD, axis=-1)
            yz = y * jax.nn.silu(z)
            y = yz * jax.lax.rsqrt(jnp.mean(jnp.square(yz), -1, keepdims=True) + 1e-05) * norm_w
            return y @ out_w.T
        key = jax.random.key(seed)
        ks = jax.random.split(key, 12)
        rn = lambda k, shape, s=0.02: jax.random.normal(k, shape, jnp.float32) * s
        dt = jnp.exp(jax.random.uniform(ks[5], (NH,), jnp.float32, np.log(0.001), np.log(0.1)))
        return dict(x=jax.random.normal(ks[0], (SEQ, BATCH, HID), jnp.float32), w_down=rn(ks[1], (DM, HID)), b_down=jnp.zeros((DM,), jnp.float32), w_up=rn(ks[2], (HID, DM)), b_up=jnp.zeros((HID,), jnp.float32), gate1=jnp.asarray(0.6, jnp.float32), hy_in_w=rn(ks[3], (DIN_PROJ, DM)), hy_conv_w=rn(ks[4], (CONV_DIM, 1, DCONV), 0.2), hy_conv_b=jnp.zeros((CONV_DIM,), jnp.float32), hy_dt_bias=jnp.log(jnp.expm1(dt)), hy_A_log=jnp.log(jax.random.uniform(ks[6], (NH,), jnp.float32, 1.0, 16.0)), hy_D=jnp.ones((NH,), jnp.float32), hy_fcD_w=rn(ks[7], (NH, DIN)), hy_norm_w=jnp.ones((DIN,), jnp.float32), hy_out_w=rn(ks[8], (DM, DIN)))
    _L0_attn_all = _L0_attn_setup()
    _L0_attn_in = {k: v for k, v in _L0_attn_all.items() if k in ('w_down', 'b_down', 'w_up', 'b_up', 'gate1', 'hy_in_w', 'hy_conv_w', 'hy_conv_b', 'hy_dt_bias', 'hy_A_log', 'hy_D', 'hy_fcD_w', 'hy_norm_w', 'hy_out_w')}
    del _L0_attn_all

    def _L0_xattn_setup():
        import jax, jax.numpy as jnp
        import numpy as np
        B, Q, D = (8, 64, 512)
        CTX = 512
        H, KV, HD = (16, 4, 96)
        G = H // KV
        key = jax.random.key(seed)
        ks = jax.random.split(key, 6)
        s = 0.02
        return {'latents': jax.random.normal(ks[0], (B, Q, D), jnp.float32), 'context': jax.random.normal(ks[1], (B, CTX, D), jnp.float32), 'Wq': jax.random.normal(ks[2], (H * HD, D), jnp.float32) * s, 'Wk': jax.random.normal(ks[3], (KV * HD, D), jnp.float32) * s, 'Wv': jax.random.normal(ks[4], (KV * HD, D), jnp.float32) * s, 'Wo': jax.random.normal(ks[5], (D, H * HD), jnp.float32) * s}
    _L0_xattn_all = _L0_xattn_setup()
    _L0_xattn_in = {k: v for k, v in _L0_xattn_all.items() if k in ('Wq', 'Wk', 'Wv', 'Wo')}
    del _L0_xattn_all

    def _L0_ffn_setup():
        import jax, jax.numpy as jnp
        import numpy as np
        GROUP_SIZE = 128

        def dequantize(imatrix, scales, zeros, group_size, out_dtype):
            rs = jnp.repeat(scales, group_size, axis=0)
            rz = jnp.repeat(zeros, group_size, axis=0)
            return ((imatrix.astype(rs.dtype) - rz.astype(rs.dtype)) * rs).astype(out_dtype)
        key = jax.random.key(seed)
        ks = jax.random.split(key, 10)
        H, I, G = (512, 1792, GROUP_SIZE)
        B, S = (4, 256)
        x = jax.random.normal(ks[0], (B, S, H), dtype=jnp.float32)
        gate_w = jax.random.randint(ks[1], (H, I), 0, 16, dtype=jnp.int32)
        gate_z = jax.random.randint(ks[2], (H // G, I), 0, 16, dtype=jnp.int32)
        gate_s = jax.random.uniform(ks[3], (H // G, I), dtype=jnp.float32) * 0.01
        up_w = jax.random.randint(ks[4], (H, I), 0, 16, dtype=jnp.int32)
        up_z = jax.random.randint(ks[5], (H // G, I), 0, 16, dtype=jnp.int32)
        up_s = jax.random.uniform(ks[6], (H // G, I), dtype=jnp.float32) * 0.01
        down_w = jax.random.randint(ks[7], (I, H), 0, 16, dtype=jnp.int32)
        down_z = jax.random.randint(ks[8], (I // G, H), 0, 16, dtype=jnp.int32)
        down_s = jax.random.uniform(ks[9], (I // G, H), dtype=jnp.float32) * 0.01
        return {'x': x, 'gate_w': gate_w, 'gate_z': gate_z, 'gate_s': gate_s, 'up_w': up_w, 'up_z': up_z, 'up_s': up_s, 'down_w': down_w, 'down_z': down_z, 'down_s': down_s}
    _L0_ffn_all = _L0_ffn_setup()
    _L0_ffn_in = {k: v for k, v in _L0_ffn_all.items() if k in ('gate_w', 'gate_z', 'gate_s', 'up_w', 'up_z', 'up_s', 'down_w', 'down_z', 'down_s')}
    del _L0_ffn_all

    def _L1_attn_setup():
        import math
        import jax, jax.numpy as jnp
        import numpy as np
        N_HEADS = 32
        ALIBI_BIAS_MAX = 8

        def _alibi_slopes(n_heads, alibi_bias_max=8):
            _n = 2 ** math.ceil(math.log2(n_heads))
            m = jnp.arange(1, _n + 1, dtype=jnp.float32) * (alibi_bias_max / _n)
            slopes = 1.0 / jnp.power(2.0, m)
            if _n != n_heads:
                slopes = jnp.concatenate([slopes[1::2], slopes[::2]])[:n_heads]
            return slopes
        key = jax.random.key(seed)
        k1, k2, k3 = jax.random.split(key, 3)
        B, S, D = (1, 256, 512)
        x = jax.random.normal(k1, (B, S, D), dtype=jnp.float32)
        w_qkv = jax.random.normal(k2, (3 * D, D), dtype=jnp.float32) * 0.02
        b_qkv = jnp.zeros((3 * D,), dtype=jnp.float32)
        w_out = jax.random.normal(k3, (D, D), dtype=jnp.float32) * 0.02
        b_out = jnp.zeros((D,), dtype=jnp.float32)
        return {'x': x, 'w_qkv': w_qkv, 'b_qkv': b_qkv, 'w_out': w_out, 'b_out': b_out}
    _L1_attn_all = _L1_attn_setup()
    _L1_attn_in = {k: v for k, v in _L1_attn_all.items() if k in ('w_qkv', 'b_qkv', 'w_out', 'b_out')}
    del _L1_attn_all

    def _L1_xattn_setup():
        import jax, jax.numpy as jnp
        import numpy as np
        B, Q, K, D = (1, 128, 6404, 512)
        H, KVH, HD = (32, 8, 128)
        GROUPS = H // KVH
        EPS = 1e-05

        def _rmsnorm(x, w):
            xf = x.astype(jnp.float32)
            var = jnp.mean(xf * xf, axis=-1, keepdims=True)
            return (xf * jax.lax.rsqrt(var + EPS)).astype(x.dtype) * w
        key = jax.random.key(seed)
        ks = jax.random.split(key, 8)
        s = 0.02
        return {'hidden_states': jax.random.normal(ks[0], (B, Q, D), jnp.float32), 'cross_attention_states': jax.random.normal(ks[1], (B, K, D), jnp.float32), 'attention_mask': jnp.zeros((B, 1, Q, K), jnp.float32), 'Wq': jax.random.normal(ks[2], (H * HD, D), jnp.float32) * s, 'Wk': jax.random.normal(ks[3], (KVH * HD, D), jnp.float32) * s, 'Wv': jax.random.normal(ks[4], (KVH * HD, D), jnp.float32) * s, 'Wo': jax.random.normal(ks[5], (D, H * HD), jnp.float32) * s, 'q_norm_w': jnp.ones((HD,), jnp.float32), 'k_norm_w': jnp.ones((HD,), jnp.float32)}
    _L1_xattn_all = _L1_xattn_setup()
    _L1_xattn_in = {k: v for k, v in _L1_xattn_all.items() if k in ('Wq', 'Wk', 'Wv', 'Wo', 'q_norm_w', 'k_norm_w')}
    del _L1_xattn_all

    def _L1_ffn_setup():
        import jax, jax.numpy as jnp
        import numpy as np
        IMAGE_START_POS = 34
        Q_START = IMAGE_START_POS + 72 + 1
        Q_END = -1
        LORA_ALPHA = 32
        LORA_RANK = 16
        SCALING = LORA_ALPHA / LORA_RANK
        key = jax.random.key(seed)
        ks = jax.random.split(key, 7)
        B_, S, D, O, E, R = (4, 256, 512, 512, 8, LORA_RANK)
        s = 0.02
        return {'x': jax.random.normal(ks[0], (B_, S, D), jnp.float32), 'W': jax.random.normal(ks[1], (O, D), jnp.float32) * s, 'b': jax.random.normal(ks[2], (O,), jnp.float32) * s, 'A': jax.random.normal(ks[3], (E, R, D), jnp.float32) * s, 'B': jax.random.normal(ks[4], (E, O, R), jnp.float32) * s, 'router_W': jax.random.normal(ks[5], (E, D), jnp.float32) * s, 'router_b': jax.random.normal(ks[6], (E,), jnp.float32) * s}
    _L1_ffn_all = _L1_ffn_setup()
    _L1_ffn_in = {k: v for k, v in _L1_ffn_all.items() if k in ('W', 'b', 'A', 'B', 'router_W', 'router_b')}
    del _L1_ffn_all
    return {'x': x, 'ctx_4096': ctx_4096, 'mask_1x1xSxS2_ff0': mask_1x1xSxS2_ff0, 'L0_attn_w_down': _L0_attn_in['w_down'], 'L0_attn_b_down': _L0_attn_in['b_down'], 'L0_attn_w_up': _L0_attn_in['w_up'], 'L0_attn_b_up': _L0_attn_in['b_up'], 'L0_attn_gate1': _L0_attn_in['gate1'], 'L0_attn_hy_in_w': _L0_attn_in['hy_in_w'], 'L0_attn_hy_conv_w': _L0_attn_in['hy_conv_w'], 'L0_attn_hy_conv_b': _L0_attn_in['hy_conv_b'], 'L0_attn_hy_dt_bias': _L0_attn_in['hy_dt_bias'], 'L0_attn_hy_A_log': _L0_attn_in['hy_A_log'], 'L0_attn_hy_D': _L0_attn_in['hy_D'], 'L0_attn_hy_fcD_w': _L0_attn_in['hy_fcD_w'], 'L0_attn_hy_norm_w': _L0_attn_in['hy_norm_w'], 'L0_attn_hy_out_w': _L0_attn_in['hy_out_w'], 'L0_xattn_Wq': _L0_xattn_in['Wq'], 'L0_xattn_Wk': _L0_xattn_in['Wk'], 'L0_xattn_Wv': _L0_xattn_in['Wv'], 'L0_xattn_Wo': _L0_xattn_in['Wo'], 'L0_ffn_gate_w': _L0_ffn_in['gate_w'], 'L0_ffn_gate_z': _L0_ffn_in['gate_z'], 'L0_ffn_gate_s': _L0_ffn_in['gate_s'], 'L0_ffn_up_w': _L0_ffn_in['up_w'], 'L0_ffn_up_z': _L0_ffn_in['up_z'], 'L0_ffn_up_s': _L0_ffn_in['up_s'], 'L0_ffn_down_w': _L0_ffn_in['down_w'], 'L0_ffn_down_z': _L0_ffn_in['down_z'], 'L0_ffn_down_s': _L0_ffn_in['down_s'], 'L1_attn_w_qkv': _L1_attn_in['w_qkv'], 'L1_attn_b_qkv': _L1_attn_in['b_qkv'], 'L1_attn_w_out': _L1_attn_in['w_out'], 'L1_attn_b_out': _L1_attn_in['b_out'], 'L1_xattn_Wq': _L1_xattn_in['Wq'], 'L1_xattn_Wk': _L1_xattn_in['Wk'], 'L1_xattn_Wv': _L1_xattn_in['Wv'], 'L1_xattn_Wo': _L1_xattn_in['Wo'], 'L1_xattn_q_norm_w': _L1_xattn_in['q_norm_w'], 'L1_xattn_k_norm_w': _L1_xattn_in['k_norm_w'], 'L1_ffn_W': _L1_ffn_in['W'], 'L1_ffn_b': _L1_ffn_in['b'], 'L1_ffn_A': _L1_ffn_in['A'], 'L1_ffn_B': _L1_ffn_in['B'], 'L1_ffn_router_W': _L1_ffn_in['router_W'], 'L1_ffn_router_b': _L1_ffn_in['router_b']}

def reference(x, ctx_4096, mask_1x1xSxS2_ff0, L0_attn_w_down, L0_attn_b_down, L0_attn_w_up, L0_attn_b_up, L0_attn_gate1, L0_attn_hy_in_w, L0_attn_hy_conv_w, L0_attn_hy_conv_b, L0_attn_hy_dt_bias, L0_attn_hy_A_log, L0_attn_hy_D, L0_attn_hy_fcD_w, L0_attn_hy_norm_w, L0_attn_hy_out_w, L0_xattn_Wq, L0_xattn_Wk, L0_xattn_Wv, L0_xattn_Wo, L0_ffn_gate_w, L0_ffn_gate_z, L0_ffn_gate_s, L0_ffn_up_w, L0_ffn_up_z, L0_ffn_up_s, L0_ffn_down_w, L0_ffn_down_z, L0_ffn_down_s, L1_attn_w_qkv, L1_attn_b_qkv, L1_attn_w_out, L1_attn_b_out, L1_xattn_Wq, L1_xattn_Wk, L1_xattn_Wv, L1_xattn_Wo, L1_xattn_q_norm_w, L1_xattn_k_norm_w, L1_ffn_W, L1_ffn_b, L1_ffn_A, L1_ffn_B, L1_ffn_router_W, L1_ffn_router_b):
    import jax
    import jax.numpy as jnp

    def _L0_attn_ref(x, w_down, b_down, w_up, b_up, gate1, hy_in_w, hy_conv_w, hy_conv_b, hy_dt_bias, hy_A_log, hy_D, hy_fcD_w, hy_norm_w, hy_out_w):
        import jax, jax.numpy as jnp
        import numpy as np
        HID = 512
        DM = 128
        DIN = 2 * DM
        DST = 16
        HD = 64
        NH = DIN // HD
        DCONV = 7
        CONV_DIM = DIN + 2 * DST
        DIN_PROJ = 2 * DIN + 2 * DST + 2 * NH
        SEQ, BATCH = (256, 4)

        def _causal_conv(x, w, b):
            y = jax.lax.conv_general_dilated(jnp.transpose(x, (0, 2, 1)), w, (1,), [(DCONV - 1, 0)], feature_group_count=CONV_DIM, dimension_numbers=('NCH', 'OIH', 'NCH'))
            return jnp.transpose(y, (0, 2, 1)) + b

        def _ssm_scan(x, dt, A, B, C):
            dA = jnp.exp(dt * A)
            dBx = dt[..., None] * x

            def step(h, t):
                dA_t, dBx_t, B_t, C_t = t
                h = dA_t[:, :, None, None] * h + dBx_t[..., None] * B_t[:, None, None, :]
                y = jnp.einsum('bhpn,bn->bhp', h, C_t)
                return (h, y)
            h0 = jnp.zeros((x.shape[0], NH, HD, DST), x.dtype)
            _, ys = jax.lax.scan(step, h0, (jnp.moveaxis(dA, 1, 0), jnp.moveaxis(dBx, 1, 0), jnp.moveaxis(B, 1, 0), jnp.moveaxis(C, 1, 0)))
            return jnp.moveaxis(ys, 0, 1)

        def _hydra(u, in_w, conv_w, conv_b, dt_bias, A_log, D, fcD_w, norm_w, out_w):
            b, l, _ = u.shape
            zxbcdt = u @ in_w.T
            z = zxbcdt[..., :DIN]
            xBC = zxbcdt[..., DIN:DIN + CONV_DIM]
            dt2 = zxbcdt[..., DIN + CONV_DIM:]
            dt_fw = jax.nn.softplus(dt2[..., :NH] + dt_bias)
            dt_bw = jax.nn.softplus(jnp.flip(dt2[..., NH:], 1) + dt_bias)
            xBC = jax.nn.silu(_causal_conv(xBC, conv_w, conv_b))
            xs = xBC[..., :DIN]
            Bm = xBC[..., DIN:DIN + DST]
            Cm = xBC[..., DIN + DST:]
            A = -jnp.exp(A_log)
            x4 = xs.reshape(b, l, NH, HD)
            y_fw = _ssm_scan(x4, dt_fw, A, Bm, Cm).reshape(b, l, DIN)
            y_bw = jnp.flip(_ssm_scan(jnp.flip(x4, 1), dt_bw, A, jnp.flip(Bm, 1), jnp.flip(Cm, 1)).reshape(b, l, DIN), 1)
            zero = jnp.zeros((b, 1, DIN), u.dtype)
            y = jnp.concatenate([zero, y_fw[:, :-1]], 1) + jnp.concatenate([y_bw[:, 1:], zero], 1)
            y = y + xs * jnp.repeat(xs @ fcD_w.T + D, HD, axis=-1)
            yz = y * jax.nn.silu(z)
            y = yz * jax.lax.rsqrt(jnp.mean(jnp.square(yz), -1, keepdims=True) + 1e-05) * norm_w
            return y @ out_w.T
        x_init = x
        h = x @ w_down.T + b_down
        h = jnp.transpose(h, (1, 0, 2))
        h = jax.nn.gelu(h, approximate=False)
        xmid = h
        hp = (hy_in_w, hy_conv_w, hy_conv_b, hy_dt_bias, hy_A_log, hy_D, hy_fcD_w, hy_norm_w, hy_out_w)
        h = _hydra(h, *hp)
        h = _hydra(h, *hp)
        alpha = jax.nn.sigmoid(gate1)
        h = alpha * xmid + (1.0 - alpha) * h
        h = xmid + h
        h = h @ w_up.T + b_up
        return x_init + jnp.transpose(h, (1, 0, 2))

    def _L0_xattn_ref(latents, context, Wq, Wk, Wv, Wo):
        import jax, jax.numpy as jnp
        import numpy as np
        B, Q, D = (8, 64, 512)
        CTX = 512
        H, KV, HD = (16, 4, 96)
        G = H // KV
        b, q_len, _ = latents.shape
        hidden = jnp.concatenate([context, latents], axis=1)
        s_len = hidden.shape[1]
        q = (latents @ Wq.T).reshape(b, q_len, H, HD)
        k = (hidden @ Wk.T).reshape(b, s_len, KV, HD)
        v = (hidden @ Wv.T).reshape(b, s_len, KV, HD)
        q = q.transpose(0, 2, 1, 3).reshape(b, KV, G, q_len, HD)
        k = k.transpose(0, 2, 1, 3)
        v = v.transpose(0, 2, 1, 3)
        scale = 1.0 / jnp.sqrt(jnp.asarray(HD, q.dtype))
        scores = jnp.einsum('bkgqd,bksd->bkgqs', q, k) * scale
        attn = jax.nn.softmax(scores.astype(jnp.float32), axis=-1).astype(q.dtype)
        out = jnp.einsum('bkgqs,bksd->bkgqd', attn, v)
        out = out.reshape(b, H, q_len, HD).transpose(0, 2, 1, 3).reshape(b, q_len, H * HD)
        return out @ Wo.T

    def _L0_ffn_ref(x, gate_w, gate_z, gate_s, up_w, up_z, up_s, down_w, down_z, down_s):
        import jax, jax.numpy as jnp
        import numpy as np
        GROUP_SIZE = 128

        def dequantize(imatrix, scales, zeros, group_size, out_dtype):
            rs = jnp.repeat(scales, group_size, axis=0)
            rz = jnp.repeat(zeros, group_size, axis=0)
            return ((imatrix.astype(rs.dtype) - rz.astype(rs.dtype)) * rs).astype(out_dtype)
        dt = x.dtype
        gate_proj = dequantize(gate_w, gate_s, gate_z, GROUP_SIZE, dt)
        up_proj = dequantize(up_w, up_s, up_z, GROUP_SIZE, dt)
        down_proj = dequantize(down_w, down_s, down_z, GROUP_SIZE, dt)
        gate = jax.nn.silu(jnp.dot(x, gate_proj))
        up = jnp.dot(x, up_proj)
        return jnp.dot(gate * up, down_proj)

    def _L1_attn_ref(x, w_qkv, b_qkv, w_out, b_out):
        import math
        import jax, jax.numpy as jnp
        import numpy as np
        N_HEADS = 32
        ALIBI_BIAS_MAX = 8

        def _alibi_slopes(n_heads, alibi_bias_max=8):
            _n = 2 ** math.ceil(math.log2(n_heads))
            m = jnp.arange(1, _n + 1, dtype=jnp.float32) * (alibi_bias_max / _n)
            slopes = 1.0 / jnp.power(2.0, m)
            if _n != n_heads:
                slopes = jnp.concatenate([slopes[1::2], slopes[::2]])[:n_heads]
            return slopes
        B, S, D = x.shape
        H = N_HEADS
        hd = D // H
        qkv = jnp.einsum('bsd,od->bso', x, w_qkv) + b_qkv
        q, k, v = jnp.split(qkv, 3, axis=-1)
        q = q.reshape(B, S, H, hd)
        k = k.reshape(B, S, H, hd)
        v = v.reshape(B, S, H, hd)
        scale = 1.0 / math.sqrt(hd)
        scores = jnp.einsum('bqhd,bkhd->bhqk', q, k) * scale
        slopes = _alibi_slopes(H, ALIBI_BIAS_MAX)
        positions = jnp.arange(1 - S, 1, dtype=jnp.float32)
        alibi = slopes[:, None] * positions[None, :]
        scores = scores + alibi[None, :, None, :]
        causal = jnp.arange(S)[:, None] >= jnp.arange(S)[None, :]
        scores = jnp.where(causal[None, None, :, :], scores, jnp.float32(-1000000000.0))
        attn = jax.nn.softmax(scores, axis=-1)
        out = jnp.einsum('bhqk,bkhd->bqhd', attn, v).reshape(B, S, D)
        return jnp.einsum('bsd,od->bso', out, w_out) + b_out

    def _L1_xattn_ref(hidden_states, cross_attention_states, attention_mask, Wq, Wk, Wv, Wo, q_norm_w, k_norm_w):
        import jax, jax.numpy as jnp
        import numpy as np
        B, Q, K, D = (1, 128, 6404, 512)
        H, KVH, HD = (32, 8, 128)
        GROUPS = H // KVH
        EPS = 1e-05

        def _rmsnorm(x, w):
            xf = x.astype(jnp.float32)
            var = jnp.mean(xf * xf, axis=-1, keepdims=True)
            return (xf * jax.lax.rsqrt(var + EPS)).astype(x.dtype) * w
        bsz, q_len, _ = hidden_states.shape
        kv_len = cross_attention_states.shape[1]
        q = (hidden_states @ Wq.T).reshape(bsz, q_len, H, HD).transpose(0, 2, 1, 3)
        k = (cross_attention_states @ Wk.T).reshape(bsz, kv_len, KVH, HD).transpose(0, 2, 1, 3)
        v = (cross_attention_states @ Wv.T).reshape(bsz, kv_len, KVH, HD).transpose(0, 2, 1, 3)
        q = _rmsnorm(q, q_norm_w)
        k = jnp.repeat(k, GROUPS, axis=1)
        v = jnp.repeat(v, GROUPS, axis=1)
        k = _rmsnorm(k, k_norm_w)
        scale = 1.0 / np.sqrt(HD)
        scores = jnp.einsum('bhqd,bhkd->bhqk', q, k) * scale
        scores = scores + attention_mask[:, :, :, :kv_len]
        probs = jax.nn.softmax(scores.astype(jnp.float32), axis=-1).astype(q.dtype)
        out = jnp.einsum('bhqk,bhkd->bhqd', probs, v)
        out = out.transpose(0, 2, 1, 3).reshape(bsz, q_len, H * HD)
        return out @ Wo.T

    def _L1_ffn_ref(x, W, b, A, B, router_W, router_b):
        import jax, jax.numpy as jnp
        import numpy as np
        IMAGE_START_POS = 34
        Q_START = IMAGE_START_POS + 72 + 1
        Q_END = -1
        LORA_ALPHA = 32
        LORA_RANK = 16
        SCALING = LORA_ALPHA / LORA_RANK
        x_q = x[:, Q_START:Q_END, :]
        q = x_q.mean(axis=1)
        logits = q @ router_W.T + router_b
        routing = jax.nn.softmax(logits, axis=-1)
        base = x @ W.T + b
        t = jnp.einsum('bsd,erd->bser', x, A)
        lora = jnp.einsum('bser,eor,be->bso', t, B, routing) * SCALING
        return base + lora
    x = _layernorm(x + _L0_attn_ref(x, L0_attn_w_down, L0_attn_b_down, L0_attn_w_up, L0_attn_b_up, L0_attn_gate1, L0_attn_hy_in_w, L0_attn_hy_conv_w, L0_attn_hy_conv_b, L0_attn_hy_dt_bias, L0_attn_hy_A_log, L0_attn_hy_D, L0_attn_hy_fcD_w, L0_attn_hy_norm_w, L0_attn_hy_out_w), axis=-1)
    x = _layernorm(x + _L0_xattn_ref(x, ctx_4096, L0_xattn_Wq, L0_xattn_Wk, L0_xattn_Wv, L0_xattn_Wo), axis=-1)
    x = _layernorm(x + _L0_ffn_ref(x, L0_ffn_gate_w, L0_ffn_gate_z, L0_ffn_gate_s, L0_ffn_up_w, L0_ffn_up_z, L0_ffn_up_s, L0_ffn_down_w, L0_ffn_down_z, L0_ffn_down_s), axis=-1)
    x = _layernorm(x + _L1_attn_ref(x, L1_attn_w_qkv, L1_attn_b_qkv, L1_attn_w_out, L1_attn_b_out), axis=-1)
    x = _layernorm(x + _L1_xattn_ref(x, ctx_4096, mask_1x1xSxS2_ff0, L1_xattn_Wq, L1_xattn_Wk, L1_xattn_Wv, L1_xattn_Wo, L1_xattn_q_norm_w, L1_xattn_k_norm_w), axis=-1)
    x = _layernorm(x + _L1_ffn_ref(x, L1_ffn_W, L1_ffn_b, L1_ffn_A, L1_ffn_B, L1_ffn_router_W, L1_ffn_router_b), axis=-1)
    return x

_drawn_inputs = setup_inputs


def setup_inputs(seed=0):
    import zlib

    import numpy as np

    out = dict(_drawn_inputs(seed))
    spreads = {'L0_attn_b_down': (0.0, 0.693),
     'L0_attn_b_up': (0.0, 0.1),
     'L0_attn_hy_conv_b': (0.0, 0.8),
     'L0_attn_hy_D': (1.0, 0.6),
     'L0_attn_hy_norm_w': (1.0, 0.6),
     'L1_attn_b_qkv': (0.0, 0.1),
     'L1_attn_b_out': (0.0, 0.1),
     'L1_xattn_q_norm_w': (1.0, 0.6),
     'L1_xattn_k_norm_w': (1.0, 0.6)}
    factors = {'L0_attn_hy_in_w': 8.0,
     'L0_attn_hy_conv_w': 8.0,
     'L0_attn_hy_dt_bias': 8.0,
     'L0_attn_hy_A_log': 64.0,
     'L0_attn_hy_fcD_w': 8.0,
     'L0_attn_hy_out_w': 8.0,
     'L0_xattn_Wq': 5.718,
     'L0_xattn_Wk': 5.779,
     'L1_ffn_b': 3.198,
     'L1_ffn_router_W': 8.0,
     'L1_ffn_router_b': 64.0}
    for name, (base, spread) in spreads.items():
        noise = np.random.default_rng([zlib.crc32(name.encode()), seed]).standard_normal(out[name].shape)
        drawn = base * np.exp(spread * noise) if base else spread * noise
        out[name] = jnp.asarray(drawn.astype(out[name].dtype))
    for name, factor in factors.items():
        out[name] = (out[name] * factor).astype(out[name].dtype)
    return out
```

```python
import math
from contextlib import ExitStack

import numpy as np
import concourse.bass as bass
from concourse import mybir
from concourse.alu_op_type import AluOpType as ALU

FP32 = mybir.dt.float32
F32R = mybir.dt.float32r
INT32 = mybir.dt.int32
ACT = mybir.ActivationFunctionType
AX = mybir.AxisListType.X

P = 128
B, S, D = 8, 128, 512
KC = D // P
TOK = B * S
HALF = 512
LN_EPS = 1e-5



def bc(ap, axis, shape):
    return ap.unsqueeze(axis).to_broadcast(shape)


def raw(ap):
    return ap.bitcast(FP32)


class Memory:

    def __init__(self, sb):
        self.xtok = sb("xtok", [P, B, D])
        self.xT_hi = sb("xT_hi", [P, KC, TOK], F32R)
        self.xT_lo = sb("xT_lo", [P, KC, TOK], F32R)
        self.cT_hi = sb("cT_hi", [P, KC, TOK], F32R)
        self.cT_lo = sb("cT_lo", [P, KC, TOK], F32R)
        self.ident, self.ones = sb("ident", [P, P]), sb("ones", [P, P])
        self.minus_half = sb("minus_half", [P, 32])
        self.stats, self.meanvar = sb("stats", [P, B, 6]), sb("meanvar", [P, B, 2])
        self.var, self.rstd = sb("var", [P, B]), sb("rstd", [P, B])
        self.norm_bank = None


class Chain:

    def __init__(self, eng, sem, per=0, turn=0):
        self.eng, self.sem, self.base, self.n, self.per = eng, sem, turn * per, 0, per

    def step(self, ins):
        self.n += 1
        ins.then_inc(self.sem, 1)
        self.eng.wait_ge(self.sem, self.base + self.n)

    def end(self):
        assert self.n == self.per, (self.n, self.per)


def three(pe, out, a_hi, a_lo, b_hi, b_lo, first, last):
    pe.matmul(out, a_hi, b_hi, start=first, stop=False)
    pe.matmul(out, a_lo, b_hi, start=False, stop=False)
    return pe.matmul(out, a_hi, b_lo, start=False, stop=last)



def norm_sems(sem, tag):
    return {n: sem(f"{tag}_{n}") for n in (
            "stats", "aggr", "var", "rstd", "x", "turned", "hi", "lo")}


def norm_vector(dve, m, s, transposed=True):
    for b in range(B):
        dve.bn_stats(m.stats[:, b, :], m.xtok[:, b, :]).then_inc(s["stats"], 1)
    dve.wait_ge(s["stats"], B)
    for b in range(B):
        dve.bn_aggr(m.meanvar[:, b, :], m.stats[:, b, :]).then_inc(s["aggr"], 1)
    dve.wait_ge(s["aggr"], B)
    dve.tensor_scalar(m.var[:, :], m.meanvar[:, :, 1], LN_EPS, None, ALU.add).then_inc(s["var"], 1)
    dve.wait_ge(s["rstd"], 1)
    for b in range(B + 2):
        if b < B:
            dve.tensor_scalar(m.xtok[:, b, :], m.xtok[:, b, :], m.meanvar[:, b, 0:1], m.rstd[:, b:b + 1],
                              ALU.subtract, ALU.mult).then_inc(s["x"], 1)
        if transposed and b >= 2:
            t = b - 2
            dve.wait_ge(s["hi"], t + 1)
            dve.tensor_tensor(m.xT_lo[:, :, t * P:(t + 1) * P], m.norm_bank[t % 2][:, :].rearrange("p (c n) -> p c n", c=KC),
                              raw(m.xT_hi[:, :, t * P:(t + 1) * P]), ALU.subtract).then_inc(s["lo"], 1)


def norm_gpsimd(pool, m, s):
    pool.wait_ge(s["var"], 1)
    pool.tensor_tensor(m.rstd[:, :], m.var[:, :], m.minus_half[:, 0:B], ALU.pow).then_inc(s["rstd"], 1)


def norm_tensor(pe, m, s):
    for b in range(B):
        pe.wait_ge(s["x"], b + 1)
        if b >= 2:
            pe.wait_ge(s["lo"], b - 1)
        for c in range(KC):
            last = pe.transpose(m.norm_bank[b % 2][:, c * P:(c + 1) * P], m.xtok[:, b, c * P:(c + 1) * P], m.ident[:, :])
        last.then_inc(s["turned"], 1)


def norm_scalar(act, m, s):
    for b in range(B):
        act.wait_ge(s["turned"], b + 1)
        act.activation(m.xT_hi[:, :, b * P:(b + 1) * P], m.norm_bank[b % 2][:, :].rearrange("p (c n) -> p c n", c=KC),
                       ACT.Copy).then_inc(s["hi"], 1)



DM, DIN, DST, NH, HDIM, TAPS = 128, 256, 16, 4, 64, 7
CONV = DIN + 2 * DST
ZDT = DIN + 2 * NH
L = B
DIST = L - 1
LAYERS = 2
EXP_FLOOR = -200.0
A_LOG_CEIL = 84.0


def hydra_stage(nc, m, io, sem):
    with ExitStack() as ctx:
        def sb(name, shape, dt=FP32):
            return ctx.enter_context(nc.sbuf_tensor("hy_" + name, shape, dt))

        def pb(name, n=HALF):
            return ctx.enter_context(nc.psum_tensor("hy_" + name, [P, n], FP32))

        xT0 = sb("xT0", [P, KC, TOK])
        w_down = sb("w_down", [P, KC, DM])
        b_down = sb("b_down", [P, 1])
        w_zdt = sb("w_zdt", [P, ZDT])
        w_xbc = sb("w_xbc", [P, CONV])
        taps = sb("taps", [P, TAPS, CONV])
        w_conv = sb("w_conv", [P, TAPS, CONV])
        conv_b = sb("conv_b", [P, CONV])
        dt_bias = sb("dt_bias", [P, NH])
        a_log = sb("a_log", [P, NH])
        d_skip = sb("d_skip", [P, NH])
        fcd = sb("fcd", [P, 2, NH])
        norm_w = sb("norm_w", [P, 2])
        w_out = sb("w_out", [P, 2, DM])
        w_up = sb("w_up", [P, D])
        b_up = sb("b_up", [P, D])
        gate = sb("gate", [P, 1])
        mix = sb("mix", [P, 2])
        x_mid = sb("x_mid", [P, TOK])
        uT = sb("uT", [P, TOK])
        z_act = sb("z_act", [P, L, DIN])
        xbc = sb("xbc", [P, L, CONV])
        xsT = sb("xsT", [P, 2, TOK])
        dt_raw = sb("dt_raw", [P, L, 2, NH])
        dt = sb("dt", [P, 2, L, NH])
        sp = [sb(f"sp{i}", [P, L * 2 * NH]) for i in range(6)]
        neg_a = sb("neg_a", [P, NH])
        cb_prod = sb("cb_prod", [P, L, L, DST])
        cb = sb("cb", [P, L * L + L + 1])
        seg = sb("seg", [P, 2, DIST, L, NH])
        dec = sb("dec", [P, 2, DIST, L, NH])
        mixw = sb("mixw", [P, (L * L + L + 1) * NH])
        prod = [sb(f"prod{i}", [P, L, DIN]) for i in range(2)]
        yz = sb("yz", [P, L, DIN])
        junk = sb("junk", [P, DIN])
        ssq = sb("ssq", [P, L])
        msq = sb("msq", [P, L])
        rms = sb("rms", [P, L])
        yT = sb("yT", [P, 2, TOK])
        hm = sb("hm", [P, TOK])
        bank = [pb(f"bank{i}") for i in range(6)]
        skip_bank = pb("skip_bank", L * NH)
        m.norm_bank = bank[2:4]
        n0 = norm_sems(sem, "n0")

        ld = {n: sem("hy_ld_" + n) for n in ("x", "gelu", "in", "conv", "small", "up")}
        s = {n: sem("hy_" + n) for n in (
            "ident", "consts", "mid", "mid_act", "u", "wconv", "alpha", "alpha_exp", "a_exp", "na", "z_mm",
            "z_out", "c_mm", "c_out", "xbc", "xs_tr", "xs_T", "skip", "chain", "pool", "sp_in", "sp_exp",
            "seg", "dec", "w_ok", "prod", "y_mm", "yz", "ssq", "msq", "rms", "yn", "y_tr", "y_T", "o_mm",
            "mixed", "up_mm", "xres", "resid")}

        with nc.Block() as block:
            @block.sync
            def _(sp_):
                for c in range(KC):
                    sp_.dma_start(xT0[:, c, :], io["xT"].rearrange("(c p) n -> p c n", p=P)[:, c, :]).then_inc(ld["x"], 16)
                sp_.dma_start(w_down[:, :, :], io["w_downT"].rearrange("(c p) n -> p c n", p=P)).then_inc(ld["gelu"], 16)
                sp_.dma_start(b_down[:, :], io["b_down"].rearrange("(p a) -> p a", a=1)).then_inc(ld["gelu"], 16)
                sp_.dma_start(w_zdt[:, 0:DIN], io["in_wT"][:, 0:DIN]).then_inc(ld["in"], 16)
                sp_.dma_start(w_zdt[:, DIN:ZDT], io["in_wT"][:, DIN + CONV:DIN + CONV + 2 * NH]).then_inc(ld["in"], 16)
                sp_.dma_start(w_xbc[:, :], io["in_wT"][:, DIN:DIN + CONV]).then_inc(ld["in"], 16)
                sp_.dma_start(m.xtok[:, :, :], io["x"].rearrange("b s d -> s b d")).then_inc(ld["up"], 16)
                sp_.dma_start(w_up[:, :], io["w_upT"]).then_inc(ld["up"], 16)
                sp_.dma_start(b_up[:, :], io["b_up"].partition_broadcast(P)).then_inc(ld["up"], 16)

            @block.gpsimd
            def _(pool):
                pool.dma_start(taps[:, :, :], io["conv_w"].partition_broadcast(P)).then_inc(ld["conv"], 16)
                pool.dma_start(conv_b[:, :], io["conv_b"].partition_broadcast(P)).then_inc(ld["small"], 16)
                pool.dma_start(dt_bias[:, :], io["dt_bias"].partition_broadcast(P)).then_inc(ld["small"], 16)
                pool.dma_start(a_log[:, :], io["a_log"].partition_broadcast(P)).then_inc(ld["small"], 16)
                pool.dma_start(d_skip[:, :], io["d_skip"].partition_broadcast(P)).then_inc(ld["small"], 16)
                pool.dma_start(gate[:, :], io["gate1"].partition_broadcast(P)).then_inc(ld["small"], 16)
                for c in range(2):
                    pool.dma_start(norm_w[:, c:c + 1], io["norm_w"][c * P:(c + 1) * P].rearrange("(p a) -> p a", a=1)).then_inc(ld["small"], 16)
                pool.dma_start(fcd[:, :, :], io["fcD_wT"].rearrange("(c p) n -> p c n", p=P)).then_inc(ld["small"], 16)
                pool.dma_start(w_out[:, :, :], io["out_wT"].rearrange("(c p) n -> p c n", p=P)).then_inc(ld["small"], 16)
                pool.memset(m.ident[:, :], 0.0).then_inc(s["ident"], 1)
                pool.wait_ge(s["ident"], 1)
                pool.affine_select(out=m.ident[:, :], in_=m.ident[:, :], compare_op=ALU.not_equal, fill=1.0, base=0,
                                   pattern=[[-1, P]], channel_multiplier=1).then_inc(s["ident"], 1)
                pool.memset(m.minus_half[:, :], -0.5).then_inc(s["consts"], 1)
                pool.memset(m.ones[:, :], 1.0).then_inc(s["consts"], 1)
                pool.wait_ge(ld["conv"], 16)
                pool.wait_ge(ld["in"], 48)
                pool.tensor_tensor(w_conv[:, :, :], taps[:, :, :], bc(w_xbc[:, :], 1, [P, TAPS, CONV]), ALU.mult).then_inc(s["wconv"], 1)
                pool.wait_ge(s["consts"], 2)
                with pool.Fori(0, LAYERS) as i:
                    pool.wait_ge(s["msq"], i + 1)
                    pool.tensor_tensor(rms[:, :], msq[:, :], m.minus_half[:, 0:L], ALU.pow).then_inc(s["rms"], 1)
                norm_gpsimd(pool, m, n0)

            @block.tensor
            def _(pe):
                pe.wait_ge(ld["x"], 16 * KC)
                pe.wait_ge(ld["gelu"], 32)
                for h in range(2):
                    for c in range(KC):
                        last = pe.matmul(bank[h][:, :], w_down[:, c, :], xT0[:, c, h * HALF:(h + 1) * HALF],
                                         start=c == 0, stop=c == KC - 1)
                    last.then_inc(s["mid"], 1)
                pe.wait_ge(s["wconv"], 1)
                pe.wait_ge(s["ident"], 2)
                pe.wait_ge(ld["small"], 16 * 9)
                with pe.Fori(0, LAYERS) as i:
                    pe.wait_ge(s["u"], 2 * i + 2)
                    for t in range(L):
                        if t >= 2:
                            pe.wait_ge(s["z_out"], L * i + t - 1)
                        pe.matmul(bank[t % 2][:, 0:ZDT], uT[:, t * P:(t + 1) * P], w_zdt[:, :],
                                  start=True, stop=True).then_inc(s["z_mm"], 1)
                        if t >= 2:
                            pe.wait_ge(s["c_out"], L * i + t - 1)
                        first = max(0, TAPS - 1 - t)
                        for k in range(first, TAPS):
                            src = t - (TAPS - 1) + k
                            last = pe.matmul(bank[2 + t % 2][:, 0:CONV], uT[:, src * P:(src + 1) * P], w_conv[:, k, :],
                                             start=k == first, stop=k == TAPS - 1)
                        last.then_inc(s["c_mm"], 1)
                    for t in range(L):
                        pe.wait_ge(s["xbc"], L * i + t + 1)
                        if t >= 2:
                            pe.wait_ge(s["xs_T"], L * i + t - 1)
                        for c in range(2):
                            last = pe.transpose(bank[4 + t % 2][:, c * P:(c + 1) * P], xbc[:, t, c * P:(c + 1) * P], m.ident[:, :])
                        last.then_inc(s["xs_tr"], 1)
                    for t in range(L):
                        pe.wait_ge(s["xs_T"], L * i + t + 1)
                        for c in range(2):
                            last = pe.matmul(skip_bank[:, t * NH:(t + 1) * NH], xsT[:, c, t * P:(t + 1) * P], fcd[:, c, :],
                                             start=c == 0, stop=c == 1)
                    last.then_inc(s["skip"], 1)
                    for t in range(L):
                        pe.wait_ge(s["prod"], L * i + t + 1)
                        if t >= 2:
                            pe.wait_ge(s["yz"], L * i + t - 1)
                        for src in range(L):
                            last = pe.matmul(bank[t % 2][:, 0:DIN], m.ident[:, :], prod[t % 2][:, src, :],
                                             start=src == 0, stop=src == L - 1)
                        last.then_inc(s["y_mm"], 1)
                    for t in range(L):
                        pe.wait_ge(s["yn"], L * i + t + 1)
                        if t >= 2:
                            pe.wait_ge(s["y_T"], 2 * (L * i + t - 1))
                        for c in range(2):
                            last = pe.transpose(bank[2 + t % 2][:, c * P:(c + 1) * P], yz[:, t, c * P:(c + 1) * P], m.ident[:, :])
                        last.then_inc(s["y_tr"], 1)
                    for h in range(2):
                        pe.wait_ge(s["y_T"], 2 * (L * i + L))
                        for c in range(2):
                            last = pe.matmul(bank[4 + h][:, :], w_out[:, c, :], yT[:, c, h * HALF:(h + 1) * HALF],
                                             start=c == 0, stop=c == 1)
                        last.then_inc(s["o_mm"], 1)
                pe.wait_ge(ld["up"], 48)
                for b in range(B):
                    pe.wait_ge(s["mixed"], b // 4 + 1)
                    if b >= 2:
                        pe.wait_ge(s["resid"], b - 1)
                    pe.matmul(bank[b % 2][:, :], hm[:, b * P:(b + 1) * P], w_up[:, :], start=True, stop=True).then_inc(s["up_mm"], 1)
                norm_tensor(pe, m, n0)

            @block.scalar
            def _(act):
                for h in range(2):
                    act.wait_ge(s["mid"], h + 1)
                    act.activation(x_mid[:, h * HALF:(h + 1) * HALF], bank[h][:, :], ACT.Gelu, bias=b_down[:, :]).then_inc(s["mid_act"], 1)
                for h in range(2):
                    act.wait_ge(s["mid_act"], h + 1)
                    act.activation(uT[:, h * HALF:(h + 1) * HALF], x_mid[:, h * HALF:(h + 1) * HALF], ACT.Copy).then_inc(s["u"], 1)
                act.wait_ge(ld["small"], 16 * 9)
                act.activation(sp[0][:, 0:1], gate[:, :], ACT.Exp, scale=-1.0).then_inc(s["alpha_exp"], 1)
                act.wait_ge(s["na"], 1)
                act.activation(neg_a[:, :], a_log[:, :], ACT.Exp).then_inc(s["a_exp"], 1)
                with act.Fori(0, LAYERS) as i:
                    for t in range(L):
                        act.wait_ge(s["z_mm"], L * i + t + 1)
                        act.activation(z_act[:, t, :], bank[t % 2][:, 0:DIN], ACT.Silu)
                        act.activation(dt_raw[:, t, :, :].rearrange("p a h -> p (a h)"), bank[t % 2][:, DIN:ZDT], ACT.Copy).then_inc(s["z_out"], 1)
                        act.wait_ge(s["c_out"], L * i + t + 1)
                        act.activation(xbc[:, t, :], xbc[:, t, :], ACT.Silu).then_inc(s["xbc"], 1)
                    act.wait_ge(s["sp_in"], i + 1)
                    act.activation(sp[1][:, :], sp[0][:, :], ACT.Exp).then_inc(s["sp_exp"], 1)
                    for t in range(L):
                        act.wait_ge(s["xs_tr"], L * i + t + 1)
                        act.activation(xsT[:, :, t * P:(t + 1) * P], bank[4 + t % 2][:, 0:DIN].rearrange("p (c n) -> p c n", c=2),
                                       ACT.Copy).then_inc(s["xs_T"], 1)
                    act.wait_ge(s["seg"], i + 1)
                    act.activation(dec[:, :, :, :, :], dec[:, :, :, :, :], ACT.Exp).then_inc(s["dec"], 1)
                    for t in range(L):
                        act.wait_ge(s["yz"], L * i + t + 1)
                        if t:
                            act.wait_ge(s["ssq"], L * i + t)
                        act.activation(junk[:, :], yz[:, t, :], ACT.Square, accum_out=ssq[:, t:t + 1]).then_inc(s["ssq"], 1)
                    for t in range(L):
                        act.wait_ge(s["y_tr"], L * i + t + 1)
                        for c in range(2):
                            act.activation(yT[:, c, t * P:(t + 1) * P], bank[2 + t % 2][:, c * P:(c + 1) * P], ACT.Copy,
                                           scale=norm_w[:, c:c + 1]).then_inc(s["y_T"], 1)
                    for h in range(2):
                        act.wait_ge(s["o_mm"], 2 * i + h + 1)
                        act.activation(uT[:, h * HALF:(h + 1) * HALF], bank[4 + h][:, :], ACT.Copy).then_inc(s["u"], 1)
                norm_scalar(act, m, n0)

            @block.vector
            def _(dve):
                dve.memset(seg[:, :, :, :, :], 0.0).then_inc(s["pool"], 1)
                dve.wait_ge(ld["small"], 16 * 9)
                dve.tensor_scalar(a_log[:, :], a_log[:, :], A_LOG_CEIL, None, ALU.min).then_inc(s["na"], 1)
                dve.wait_ge(s["alpha_exp"], 1)
                pre = Chain(dve, s["alpha"])
                pre.step(dve.tensor_scalar(sp[2][:, 0:1], sp[0][:, 0:1], 1.0, None, ALU.add))
                pre.step(dve.reciprocal(sp[3][:, 0:1], sp[2][:, 0:1]))
                pre.step(dve.tensor_scalar(mix[:, 0:1], sp[3][:, 0:1], 1.0, None, ALU.add))
                pre.step(dve.tensor_scalar(mix[:, 1:2], sp[3][:, 0:1], -1.0, 1.0, ALU.mult, ALU.add))
                dve.wait_ge(s["a_exp"], 1)
                pre.step(dve.tensor_scalar(neg_a[:, :], neg_a[:, :], -1.0, None, ALU.mult))
                dve.wait_ge(s["pool"], 1)
                with dve.Fori(0, LAYERS) as i:
                    ch = Chain(dve, s["chain"], 47, i)
                    for t in range(L):
                        dve.wait_ge(s["c_mm"], L * i + t + 1)
                        dve.tensor_tensor(xbc[:, t, :], bank[2 + t % 2][:, 0:CONV], conv_b[:, :], ALU.add).then_inc(s["c_out"], 1)
                    dve.wait_ge(s["z_out"], L * i + L)
                    v, e, z, z2, q = sp[2], sp[1], sp[3], sp[4], sp[5]
                    ch.step(dve.tensor_tensor(v[:, :].rearrange("p (a t h) -> p a t h", a=2, h=NH),
                                              dt_raw[:, :, :, :].rearrange("p t a h -> p a t h"),
                                              dt_bias[:, :].unsqueeze(1).unsqueeze(1).to_broadcast([P, 2, L, NH]), ALU.add))
                    dve.scalar_tensor_tensor(sp[0][:, :], v[:, :], -1.0, v[:, :], ALU.mult, ALU.min).then_inc(s["sp_in"], 1)
                    dve.wait_ge(s["sp_exp"], i + 1)
                    ch.step(dve.tensor_scalar(q[:, :], e[:, :], 2.0, None, ALU.add))
                    ch.step(dve.reciprocal(z[:, :], q[:, :]))
                    ch.step(dve.tensor_tensor(z[:, :], z[:, :], e[:, :], ALU.mult))
                    ch.step(dve.tensor_tensor(z2[:, :], z[:, :], z[:, :], ALU.mult))
                    ch.step(dve.tensor_scalar(q[:, :], z2[:, :], 1.0 / 15, None, ALU.mult))
                    for n in (13, 11, 9, 7, 5, 3):
                        ch.step(dve.scalar_tensor_tensor(q[:, :], q[:, :], 1.0 / n, z2[:, :], ALU.add, ALU.mult))
                    ch.step(dve.scalar_tensor_tensor(q[:, :], q[:, :], 1.0, z[:, :], ALU.add, ALU.mult))
                    ch.step(dve.tensor_scalar(v[:, :], v[:, :], 0.0, None, ALU.max))
                    ch.step(dve.scalar_tensor_tensor(dt[:, :, :, :].rearrange("p a t h -> p (a t h)"), q[:, :], 2.0, v[:, :],
                                                     ALU.mult, ALU.add))
                    for d in range(1, DIST):
                        n = DIST - d
                        dve.tensor_tensor(seg[:, 0, d, 0:n, :], seg[:, 0, d - 1, 0:n, :], dt[:, 0, d:d + n, :], ALU.add).then_inc(s["chain"], 1)
                        ch.n += 1
                        ch.step(dve.tensor_tensor(seg[:, 1, d, d + 1:L, :], seg[:, 1, d - 1, d + 1:L, :], dt[:, 1, 1:1 + n, :], ALU.add))
                    ch.step(dve.tensor_tensor(dec[:, :, :, :, :].rearrange("p a d s h -> p (a d s) h"),
                                              seg[:, :, :, :, :].rearrange("p a d s h -> p (a d s) h"),
                                              bc(neg_a[:, :], 1, [P, 2 * DIST * L, NH]), ALU.mult))
                    dve.tensor_scalar(dec[:, :, :, :, :], dec[:, :, :, :, :], EXP_FLOOR, None, ALU.max).then_inc(s["seg"], 1)
                    dve.wait_ge(s["xbc"], L * i + L)
                    ch.step(dve.tensor_tensor(cb_prod[:, :, :, :], bc(xbc[:, :, DIN + DST:CONV], 2, [P, L, L, DST]),
                                              bc(xbc[:, :, DIN:DIN + DST], 1, [P, L, L, DST]), ALU.mult))
                    ch.step(dve.tensor_reduce(cb[:, 0:L * L], cb_prod[:, :, :, :].rearrange("p t s n -> p (t s) n"), AX, ALU.add))
                    dve.wait_ge(s["dec"], i + 1)
                    for a in range(2):
                        ch.step(dve.tensor_tensor(dec[:, a, :, :, :], dec[:, a, :, :, :], bc(dt[:, a, :, :], 1, [P, DIST, L, NH]), ALU.mult))

                    def diag(t0, s0, n):
                        o = (L * t0 + s0) * NH
                        return mixw[:, o:o + n * (L + 1) * NH].rearrange("p (n k) -> p n k", k=(L + 1) * NH)[:, :, 0:NH]

                    def cdiag(t0, s0, n):
                        o = L * t0 + s0
                        return cb[:, o:o + n * (L + 1)].rearrange("p (n k) -> p n k", k=L + 1)[:, :, 0:1].to_broadcast([P, n, NH])

                    for d in range(DIST):
                        n = DIST - d
                        dve.tensor_tensor(diag(d + 1, 0, n), cdiag(d, 0, n), dec[:, 0, d, 0:n, :], ALU.mult).then_inc(s["chain"], 1)
                        dve.tensor_tensor(diag(0, d + 1, n), cdiag(1, d + 1, n), dec[:, 1, d, d + 1:L, :], ALU.mult).then_inc(s["chain"], 1)
                        ch.n += 2
                    dve.wait_ge(s["skip"], i + 1)
                    ch.step(dve.tensor_tensor(diag(0, 0, L), skip_bank[:, :].rearrange("p (t h) -> p t h", h=NH),
                                              bc(d_skip[:, :], 1, [P, L, NH]), ALU.add))
                    ch.end()
                    for t in range(L + 1):
                        if t < L:
                            if t >= 2:
                                dve.wait_ge(s["y_mm"], L * i + t - 1)
                            dve.tensor_tensor(prod[t % 2][:, :, :].rearrange("p s (h n) -> p s h n", h=NH),
                                              xbc[:, :, 0:DIN].rearrange("p s (h n) -> p s h n", h=NH),
                                              bc(mixw[:, t * L * NH:(t + 1) * L * NH].rearrange("p (s h) -> p s h", h=NH), 3,
                                                 [P, L, NH, HDIM]), ALU.mult).then_inc(s["prod"], 1)
                        if t:
                            dve.wait_ge(s["y_mm"], L * i + t)
                            dve.tensor_tensor(yz[:, t - 1, :], bank[(t - 1) % 2][:, 0:DIN], z_act[:, t - 1, :], ALU.mult).then_inc(s["yz"], 1)
                    dve.wait_ge(s["ssq"], L * i + L)
                    dve.tensor_scalar(msq[:, :], ssq[:, :], 1.0 / DIN, 1e-5, ALU.mult, ALU.add).then_inc(s["msq"], 1)
                    dve.wait_ge(s["rms"], i + 1)
                    for t in range(L):
                        dve.tensor_scalar(yz[:, t, :], yz[:, t, :], rms[:, t:t + 1], None, ALU.mult).then_inc(s["yn"], 1)
                dve.wait_ge(ld["up"], 48)
                dve.scalar_tensor_tensor(m.xtok[:, :, :], m.xtok[:, :, :], 2.0, bc(b_up[:, :], 1, [P, B, D]), ALU.mult, ALU.add).then_inc(s["xres"], 1)
                for h in range(2):
                    cols = slice(h * HALF, (h + 1) * HALF)
                    dve.wait_ge(s["u"], 2 * LAYERS + h + 1)
                    pre.step(dve.tensor_scalar(x_mid[:, cols], x_mid[:, cols], mix[:, 0:1], None, ALU.mult))
                    dve.scalar_tensor_tensor(hm[:, cols], uT[:, cols], mix[:, 1:2], x_mid[:, cols], ALU.mult, ALU.add).then_inc(s["mixed"], 1)
                dve.wait_ge(s["xres"], 1)
                for b in range(B):
                    dve.wait_ge(s["up_mm"], b + 1)
                    dve.tensor_tensor(m.xtok[:, b, :], m.xtok[:, b, :], bank[b % 2][:, :], ALU.add).then_inc(s["resid"], 1)
                dve.wait_ge(s["resid"], B)
                norm_vector(dve, m, n0)



class Attention:
    Q = 4

    def __init__(self, tag, groups, hd, key_tiles, normed, weights):
        self.tag, self.G, self.HD, self.KT, self.normed, self.weights = tag, groups, hd, key_tiles, normed, weights
        self.T = B * key_tiles
        self.KEYS = key_tiles * P
        self.NH = HALF // self.KEYS
        self.PARTS = self.Q // self.NH
        self.U = B * self.PARTS
        self.CH = self.T + 2 * self.Q
        self.LAG = 2


def attention_stage(nc, m, io, sem, a):
    wq, wk, wv, wo = (io[w] for w in a.weights)
    G, HD, KT, T, KEYS, NQ, PARTS, U, CH, LAG, Q = a.G, a.HD, a.KT, a.T, a.KEYS, a.NH, a.PARTS, a.U, a.CH, a.LAG, a.Q
    scale = 1.0 / math.sqrt(HD)
    with ExitStack() as ctx:
        def sb(name, shape, dt=FP32):
            return ctx.enter_context(nc.sbuf_tensor(f"{a.tag}_{name}", shape, dt))

        def pb(name):
            return ctx.enter_context(nc.psum_tensor(f"{a.tag}_{name}", [P, HALF], FP32))

        raw_q, q_hi, q_lo = (sb(n, [P, KC, Q * HD], dt) for n, dt in (("raw_q", FP32), ("q_hi", F32R), ("q_lo", F32R)))
        raw_kv, kv_hi, kv_lo = (sb(n, [P, KC, 2 * HD], dt) for n, dt in (("raw_kv", FP32), ("kv_hi", F32R), ("kv_lo", F32R)))
        raw_o, o_hi, o_lo = (sb(n, [HD, Q, D], dt) for n, dt in (("raw_o", FP32), ("o_hi", F32R), ("o_lo", F32R)))
        qT = sb("qT", [HD, Q, TOK])
        kv = sb("kv", [P, T, 2 * HD])
        kn = sb("kn", [P, T, HD]) if a.normed else None
        kT = sb("kT", [HD, T, P])
        prob = sb("prob", [P, 3, NQ, KEYS])
        prT = sb("prT", [P, 2, NQ * KT, P])
        peak = sb("peak", [P, 3, NQ])
        total = sb("total", [P, 3, NQ])
        inv = sb("inv", [P, 3, NQ])
        out_hi = sb("out_hi", [HD, 2, Q, P], F32R)
        out_lo = sb("out_lo", [HD, 2, Q, P], F32R)
        if a.normed:
            mask = sb("mask", [P, P])
            nw = sb("nw", [P, 2])
            nw2 = sb("nw2", [P, 1])
            q_sq = sb("q_sq", [P, 2, HALF])
            q_ms = sb("q_ms", [P, 2 * Q, 4])
            q_rs = sb("q_rs", [P, 2 * Q, 4])
            k_ms = sb("k_ms", [P, T])
            k_rs = sb("k_rs", [P, T])
        score = [pb(f"score{i}") for i in range(2)]
        turn = pb("turn")
        mixed = [pb(f"mixed{i}") for i in range(2)]
        rows = pb("rows")
        proj = [pb(f"proj{i}") for i in range(2)]
        m.norm_bank = proj

        s = {n: sem(f"{a.tag}_{n}") for n in (
            "ld_q", "ld_kv", "ld_o", "ld_c", "split_hi", "split_q", "split_kv", "split_o", "proj", "evac",
            "nw", "q_sq", "q_ssq", "q_ms", "q_rs", "k_sq", "k_ms", "k_rs", "kn", "k_turn", "kT", "score",
            "masked", "peak", "exp", "inv", "norm", "turn", "prT", "pv", "out_hi", "out_lo", "rows", "add")}
        n1 = norm_sems(sem, a.tag + "n")
        chunks = 4
        HI_TURN = 3 * chunks

        with nc.Block() as block:
            @block.sync
            def _(sp):
                if a.normed:
                    sp.dma_start(mask[:, :], io["mask"][0, 0, :, :]).then_inc(s["ld_c"], 16)
                    sp.dma_start(nw[:, 0:1], io["q_norm"].rearrange("(p a) -> p a", a=1)).then_inc(s["ld_c"], 16)
                    sp.dma_start(nw[:, 1:2], io["k_norm"].rearrange("(p a) -> p a", a=1)).then_inc(s["ld_c"], 16)

                def load(g):
                    sp.wait_ge(s["split_kv"], chunks * g)
                    for n, w in ((0, wk), (1, wv)):
                        sp.dma_start(raw_kv[:, :, n * HD:(n + 1) * HD],
                                     w.rearrange("(c p) n -> p c n", p=P)[:, :, bass.ds(g * HD, HD)]).then_inc(s["ld_kv"], 16)
                    sp.wait_ge(s["split_q"], chunks * g)
                    sp.dma_start(raw_q[:, :, :], wq.rearrange("(c p) n -> p c n", p=P)[:, :, bass.ds(g * Q * HD, Q * HD)]).then_inc(s["ld_q"], 16)
                    sp.wait_ge(s["split_o"], chunks * g)
                    sp.dma_start(raw_o[:, :, :], wo.rearrange("(g h d) n -> g d h n", h=Q, d=HD)[bass.ds(g, 1), :, :, :]
                                 .rearrange("a d h n -> (a d) h n")).then_inc(s["ld_o"], 16)

                load(0)
                with sp.Fori(1, G) as g:
                    load(g)

            @block.gpsimd
            def _(pool):
                def split(raw_w, hi, lo, n, done, g, slot):
                    if n == 0:
                        pass
                    one = bc(m.ones[0:raw_w.shape[0], 0:1], 2, [raw_w.shape[0], 1, raw_w.shape[2]])
                    pool.tensor_tensor(hi[:, n:n + 1, :], raw_w[:, n:n + 1, :], one, ALU.mult).then_inc(s["split_hi"], 1)
                    pool.wait_ge(s["split_hi"], g * HI_TURN + slot + 1)
                    pool.tensor_tensor(lo[:, n:n + 1, :], raw_w[:, n:n + 1, :], raw(hi[:, n:n + 1, :]), ALU.subtract).then_inc(done, 1)

                def split_inputs(g, n):
                    if n == 0:
                        pool.wait_ge(s["ld_kv"], 32 * (g + 1))
                        pool.wait_ge(s["proj"], CH * g)
                    if n == chunks:
                        pool.wait_ge(s["ld_q"], 16 * (g + 1))
                    if n < chunks:
                        split(raw_kv, kv_hi, kv_lo, n, s["split_kv"], g, n)
                    else:
                        split(raw_q, q_hi, q_lo, n - chunks, s["split_q"], g, n)

                def group(g, last):
                    pool.wait_ge(s["ld_o"], 16 * (g + 1))
                    pool.wait_ge(s["rows"], B * g)
                    for n in range(chunks):
                        split(raw_o, o_hi, o_lo, n, s["split_o"], g, 2 * chunks + n)
                    if a.normed:
                        pool.wait_ge(s["k_ms"], g + 1)
                        pool.tensor_tensor(k_rs[:, :], k_ms[:, :], m.minus_half[:, 0:T], ALU.pow).then_inc(s["k_rs"], 1)
                        for j in range(2 * Q + 2):
                            if j < 2 * Q:
                                pool.wait_ge(s["evac"], CH * g + T + j + 1)
                                if j >= 2:
                                    pool.wait_ge(s["q_ssq"], 2 * Q * g + j - 1)
                                part = qT[:, j // 2, (j % 2) * HALF:(j % 2 + 1) * HALF]
                                pool.tensor_tensor(q_sq[:, j % 2, :], part, part, ALU.mult).then_inc(s["q_sq"], 1)
                            if j >= 2:
                                pool.wait_ge(s["q_ms"], 2 * Q * g + j - 1)
                                pool.tensor_tensor(q_rs[:, j - 2, :], q_ms[:, j - 2, :], m.minus_half[:, 0:4], ALU.pow).then_inc(s["q_rs"], 1)
                    for u in range(U):
                        pool.wait_ge(s["inv"], U * g + u + 1)
                        pool.tensor_tensor(prob[:, u % 3, :, :], prob[:, u % 3, :, :], bc(inv[:, u % 3, :], 2, [P, NQ, KEYS]),
                                           ALU.mult).then_inc(s["norm"], 1)
                        if not last and u % PARTS == 0:
                            split_inputs(g + 1, u // PARTS)

                for n in range(2 * chunks):
                    split_inputs(0, n)
                group(0, False)
                with pool.Fori(1, G - 1) as g:
                    group(g, False)
                group(G - 1, True)
                norm_gpsimd(pool, m, n1)

            @block.tensor
            def _(pe):
                def source(t, c):
                    b, k = t // KT, t % KT
                    src = (m.cT_hi, m.cT_lo) if k == 0 else (m.xT_hi, m.xT_lo)
                    return [x[:, c, b * P:(b + 1) * P] for x in src]

                def group(g):
                    pe.wait_ge(s["split_kv"], chunks * (g + 1))
                    for t in range(T):
                        if t >= 2:
                            pe.wait_ge(s["evac"], CH * g + t - 1)
                        for c in range(KC):
                            last = three(pe, proj[t % 2][:, 0:2 * HD], *source(t, c), kv_hi[:, c, :], kv_lo[:, c, :], c == 0, c == KC - 1)
                        last.then_inc(s["proj"], 1)
                    pe.wait_ge(s["split_q"], chunks * (g + 1))
                    for j in range(2 * Q + 2):
                        if j < 2 * Q:
                            h, cols = j // 2, slice((j % 2) * HALF, (j % 2 + 1) * HALF)
                            pe.wait_ge(s["evac"], CH * g + T + j - 1)
                            for c in range(KC):
                                last = three(pe, proj[(T + j) % 2][0:HD, :], q_hi[:, c, h * HD:(h + 1) * HD], q_lo[:, c, h * HD:(h + 1) * HD],
                                             m.xT_hi[:, c, cols], m.xT_lo[:, c, cols], c == 0, c == KC - 1)
                            last.then_inc(s["proj"], 1)
                        if a.normed and j >= 2:
                            pe.wait_ge(s["q_sq"], 2 * Q * g + j - 1)
                            if j == 2:
                                pe.wait_ge(s["add"], B * g)
                            if j > 2:
                                pe.wait_ge(s["q_ms"], 2 * Q * g + j - 2)
                            for n in range(4):
                                last = pe.matmul(rows[:, 4 * (j - 2) + n:4 * (j - 2) + n + 1], q_sq[:, j % 2, n * P:(n + 1) * P],
                                                 m.ones[:, 0:1], start=True, stop=True)
                            last.then_inc(s["q_ssq"], 1)
                    if a.normed:
                        pe.wait_ge(s["kn"], g + 1)
                    else:
                        pe.wait_ge(s["evac"], CH * g + T)
                    for j in range(T // 4):
                        if j:
                            pe.wait_ge(s["kT"], (T // 4) * g + j)
                        for n in range(4):
                            t = 4 * j + n
                            src = kn[:, t, :] if a.normed else kv[:, t, 0:HD]
                            last = pe.transpose(turn[0:HD, n * P:(n + 1) * P], src, m.ident[:, :])
                        last.then_inc(s["k_turn"], 1)
                    pe.wait_ge(s["kT"], (T // 4) * (g + 1))
                    pe.wait_ge(s["evac"], CH * (g + 1))
                    pe.wait_ge(s["split_o"], chunks * (g + 1))

                    def out_rows(b):
                        pe.wait_ge(s["out_lo"], U * g + PARTS * (b + 1))
                        pe.wait_ge(s["add"], B * g + b)
                        for h in range(Q):
                            last = three(pe, rows[:, :], out_hi[:, b % 2, h, :], out_lo[:, b % 2, h, :], o_hi[:, h, :], o_lo[:, h, :],
                                         h == 0, h == Q - 1)
                        last.then_inc(s["rows"], 1)

                    for u in range(U + LAG + 1):
                        if u < U:
                            b, h0 = u // PARTS, (u % PARTS) * NQ
                            if u >= 2:
                                pe.wait_ge(s["masked"] if a.normed else s["exp"], U * g + u - 1)
                            for h in range(NQ):
                                last = pe.matmul(score[u % 2][:, h * KEYS:(h + 1) * KEYS], qT[:, h0 + h, b * P:(b + 1) * P],
                                                 kT[:, b * KT:(b + 1) * KT, :].rearrange("p t n -> p (t n)"), start=True, stop=True)
                            last.then_inc(s["score"], 1)
                        v = u - LAG
                        if 0 <= v < U:
                            pe.wait_ge(s["norm"], U * g + v + 1)
                            if v:
                                pe.wait_ge(s["prT"], U * g + v)
                            for n in range(NQ * KT):
                                h, k = n // KT, n % KT
                                last = pe.transpose(turn[:, n * P:(n + 1) * P], prob[:, v % 3, h, k * P:(k + 1) * P], m.ident[:, :])
                            last.then_inc(s["turn"], 1)
                        if v > 0 and v % PARTS == 0:
                            out_rows(v // PARTS - 1)
                        if 0 <= v < U:
                            b = v // PARTS
                            pe.wait_ge(s["prT"], U * g + v + 1)
                            if v >= 2:
                                pe.wait_ge(s["out_lo"], U * g + v - 1)
                            for k in range(KT):
                                last = pe.matmul(mixed[v % 2][0:HD, 0:NQ * P], kv[:, b * KT + k, HD:2 * HD],
                                                 prT[:, v % 2, :, :].rearrange("p (h t) n -> p h t n", t=KT)[:, :, k, :],
                                                 start=k == 0, stop=k == KT - 1)
                            last.then_inc(s["pv"], 1)

                group(0)
                with pe.Fori(1, G) as g:
                    group(g)
                norm_tensor(pe, m, n1)

            @block.scalar
            def _(act):
                def group(g):
                    act.wait_ge(s["pv"], U * g)
                    for t in range(T):
                        act.wait_ge(s["proj"], CH * g + t + 1)
                        act.activation(kv[:, t, :], proj[t % 2][:, 0:2 * HD], ACT.Copy).then_inc(s["evac"], 1)
                    for j in range(2 * Q):
                        act.wait_ge(s["proj"], CH * g + T + j + 1)
                        act.activation(qT[:, j // 2, (j % 2) * HALF:(j % 2 + 1) * HALF], proj[(T + j) % 2][0:HD, :], ACT.Copy,
                                       scale=1.0 if a.normed else scale).then_inc(s["evac"], 1)
                    for j in range(T // 4):
                        act.wait_ge(s["k_turn"], (T // 4) * g + j + 1)
                        act.activation(kT[:, 4 * j:4 * j + 4, :].rearrange("p t n -> p (t n)"), turn[0:HD, :], ACT.Copy,
                                       scale=nw2[:, :] if a.normed else 1.0).then_inc(s["kT"], 1)
                    for u in range(U + LAG):
                        v = u - LAG
                        if v >= 0:
                            act.wait_ge(s["turn"], U * g + v + 1)
                            act.activation(prT[:, v % 2, :, :].rearrange("p h n -> p (h n)"), turn[:, :], ACT.Copy).then_inc(s["prT"], 1)
                        if u < U:
                            act.wait_ge(s["peak"], U * g + u + 1)
                            for h in range(NQ):
                                src = prob[:, u % 3, h, :] if a.normed else score[u % 2][:, h * KEYS:(h + 1) * KEYS]
                                last = act.activation(prob[:, u % 3, h, :], src, ACT.Exp, bias=peak[:, u % 3, h:h + 1],
                                                      accum_out=total[:, u % 3, h:h + 1])
                            last.then_inc(s["exp"], 1)
                        if v >= 0:
                            b, h0 = v // PARTS, (v % PARTS) * NQ
                            act.wait_ge(s["pv"], U * g + v + 1)
                            act.wait_ge(s["rows"], B * g + max(b - 1, 0))
                            act.activation(out_hi[:, b % 2, h0:h0 + NQ, :].rearrange("p h n -> p (h n)"), mixed[v % 2][0:HD, 0:NQ * P],
                                           ACT.Copy).then_inc(s["out_hi"], 1)

                if a.normed:
                    act.wait_ge(s["nw"], 1)
                group(0)
                with act.Fori(1, G) as g:
                    group(g)
                norm_scalar(act, m, n1)

            @block.vector
            def _(dve):
                def group(g):
                    if a.normed:
                        dve.wait_ge(s["evac"], CH * g + T)
                        dve.tensor_tensor(kn[:, :, :], kv[:, :, 0:HD], kv[:, :, 0:HD], ALU.mult).then_inc(s["k_sq"], 1)
                        dve.wait_ge(s["k_sq"], 3 * g + 1)
                        dve.tensor_reduce(k_ms[:, :], kn[:, :, :], AX, ALU.add).then_inc(s["k_sq"], 1)
                        dve.wait_ge(s["k_sq"], 3 * g + 2)
                        dve.tensor_scalar(k_ms[:, :], k_ms[:, :], 1.0 / HD, 1e-5, ALU.mult, ALU.add).then_inc(s["k_ms"], 1)
                        dve.wait_ge(s["k_rs"], g + 1)
                        dve.tensor_tensor(kn[:, :, :], kv[:, :, 0:HD], bc(k_rs[:, :], 2, [P, T, HD]), ALU.mult).then_inc(s["kn"], 1)
                        dve.wait_ge(s["kn"], g + 1)
                        dve.memset(peak[:, 0, :], 0.0).then_inc(s["k_sq"], 1)
                        for j in range(2 * Q):
                            dve.wait_ge(s["q_ssq"], 2 * Q * g + j + 1)
                            dve.tensor_scalar(q_ms[:, j, :], rows[:, 4 * j:4 * j + 4], HD * 1e-5, None, ALU.add).then_inc(s["q_ms"], 1)
                    for u in range(U + LAG + 1):
                        if u < U:
                            b = u // PARTS
                            dve.wait_ge(s["score"], U * g + u + 1)
                            if a.normed:
                                if u == 0:
                                    dve.wait_ge(s["q_rs"], 2 * Q * (g + 1))
                                for h in range(NQ):
                                    last = dve.scalar_tensor_tensor(prob[:, u % 3, h, :], score[u % 2][:, h * KEYS:(h + 1) * KEYS],
                                                                    q_rs[:, 2 * h + b // 4, b % 4:b % 4 + 1], mask[:, :],
                                                                    ALU.mult, ALU.add)
                                last.then_inc(s["masked"], 1)
                                dve.wait_ge(s["masked"], U * g + u + 1)
                                src = prob[:, u % 3, :, :]
                            else:
                                src = score[u % 2][:, :].rearrange("p (h n) -> p h n", h=NQ)
                            dve.tensor_reduce(peak[:, u % 3, :], src, AX, ALU.max, negate=True).then_inc(s["peak"], 1)
                        if 0 <= u - 1 < U:
                            n = u - 1
                            dve.wait_ge(s["exp"], U * g + n + 1)
                            dve.reciprocal(inv[:, n % 3, :], total[:, n % 3, :]).then_inc(s["inv"], 1)
                        v = u - LAG
                        if v > 0 and v % PARTS == 0:
                            add_rows(g, v // PARTS - 1)
                        if 0 <= v < U:
                            b, h0 = v // PARTS, (v % PARTS) * NQ
                            dve.wait_ge(s["out_hi"], U * g + v + 1)
                            dve.tensor_tensor(out_lo[:, b % 2, h0:h0 + NQ, :].rearrange("p h n -> p (h n)"), mixed[v % 2][0:HD, 0:NQ * P],
                                              raw(out_hi[:, b % 2, h0:h0 + NQ, :]).rearrange("p h n -> p (h n)"), ALU.subtract).then_inc(s["out_lo"], 1)

                def add_rows(g, b):
                    dve.wait_ge(s["rows"], B * g + b + 1)
                    dve.wait_ge(s["add"], B * g + b)
                    dve.tensor_tensor(m.xtok[:, b, :], m.xtok[:, b, :], rows[:, :], ALU.add).then_inc(s["add"], 1)

                if a.normed:
                    dve.wait_ge(s["ld_c"], 48)
                    dve.tensor_tensor(nw2[:, :], nw[:, 0:1], nw[:, 1:2], ALU.mult).then_inc(s["nw"], 1)
                group(0)
                with dve.Fori(1, G) as g:
                    group(g)
                dve.wait_ge(s["add"], B * G)
                norm_vector(dve, m, n1)


def context_stage(nc, m, io, sem):
    with ExitStack() as ctx:
        cT = ctx.enter_context(nc.sbuf_tensor("cT", [P, KC, TOK], FP32))
        ld, hi, lo = sem("c_ld"), sem("c_hi"), sem("c_lo")
        with nc.Block() as block:
            @block.sync
            def _(sp):
                sp.dma_start(cT[:, :, :], io["ctxT"].rearrange("(c p) n -> p c n", p=P)).then_inc(ld, 16)

            @block.vector
            def _(dve):
                dve.wait_ge(ld, 16)
                dve.tensor_copy(m.cT_hi[:, :, :], cT[:, :, :]).then_inc(hi, 1)
                dve.wait_ge(hi, 1)
                dve.tensor_tensor(m.cT_lo[:, :, :], cT[:, :, :], raw(m.cT_hi[:, :, :]), ALU.subtract).then_inc(lo, 1)
                dve.wait_ge(lo, 1)


def cross0_stage(nc, m, io, sem):
    attention_stage(nc, m, io, sem, Attention("xa0", 4, 96, 2, False, ("wq0", "wk0", "wv0", "wo0")))


def cross1_stage(nc, m, io, sem):
    attention_stage(nc, m, io, sem, Attention("xa1", 8, 128, 1, True, ("wq1", "wk1", "wv1", "wo1")))



INNER = 1792
MT = 2
TURNS = INNER // (MT * P)
WIDE = MT * P


def ffn0_stage(nc, m, io, sem):
    with ExitStack() as ctx:
        def sb(name, shape, dt=FP32):
            return ctx.enter_context(nc.sbuf_tensor("ff_" + name, shape, dt))

        def pb(name):
            return ctx.enter_context(nc.psum_tensor("ff_" + name, [P, HALF], FP32))

        gu_q, gu_z = (sb(n, [P, KC, 2, WIDE], INT32) for n in ("gu_q", "gu_z"))
        gu_s, gu_w = (sb(n, [P, KC, 2, WIDE]) for n in ("gu_s", "gu_w"))
        gu_hi, gu_lo = (sb(n, [P, KC, 2, WIDE], F32R) for n in ("gu_hi", "gu_lo"))
        dn_q, dn_z = (sb(n, [P, MT, D], INT32) for n in ("dn_q", "dn_z"))
        dn_s, dn_w = (sb(n, [P, MT, D]) for n in ("dn_s", "dn_w"))
        dn_hi, dn_lo = (sb(n, [P, MT, D], F32R) for n in ("dn_hi", "dn_lo"))
        act_g = sb("act_g", [P, 2, HALF])
        h = sb("h", [P, 2, HALF])
        h_hi, h_lo = (sb(n, [P, MT, TOK], F32R) for n in ("h_hi", "h_lo"))
        gate = [pb(f"gate{i}") for i in range(2)]
        up = [pb(f"up{i}") for i in range(2)]
        rows = [pb(f"rows{i}") for i in range(2)]
        m.norm_bank = gate
        s = {n: sem("ff_" + n) for n in (
            "ld_gu", "ld_dn", "sub_gu", "sub_dn", "w_gu", "w_dn", "hi_gu", "hi_dn", "lo_gu", "lo_dn", "gate",
            "up", "silu", "h", "h_hi", "h_lo", "rows", "add")}
        n2 = norm_sems(sem, "n2")
        CHAINS = 2 * MT

        with nc.Block() as block:
            @block.sync
            def _(sp):
                def load(g):
                    sp.wait_ge(s["sub_gu"], g)
                    sp.wait_ge(s["w_gu"], g)
                    cols = bass.ds(g * WIDE, WIDE)
                    for n, w in enumerate(("gate", "up")):
                        q, z, sc = (io[f"{w}_{x}"] for x in "wzs")
                        sp.dma_start(gu_q[:, :, n, :], q.rearrange("(c p) n -> p c n", p=P)[:, :, cols]).then_inc(s["ld_gu"], 16)
                        sp.dma_start(gu_z[:, :, n, :], z[:, cols].partition_broadcast(P)).then_inc(s["ld_gu"], 16)
                        sp.dma_start(gu_s[:, :, n, :], sc[:, cols].partition_broadcast(P)).then_inc(s["ld_gu"], 16)
                    sp.wait_ge(s["sub_dn"], g)
                    sp.wait_ge(s["w_dn"], g)
                    rows_ = bass.ds(g * MT, MT)
                    sp.dma_start(dn_q[:, :, :], io["down_w"].rearrange("(m p) n -> p m n", p=P)[:, rows_, :]).then_inc(s["ld_dn"], 16)
                    sp.dma_start(dn_z[:, :, :], io["down_z"][rows_, :].partition_broadcast(P)).then_inc(s["ld_dn"], 16)
                    sp.dma_start(dn_s[:, :, :], io["down_s"][rows_, :].partition_broadcast(P)).then_inc(s["ld_dn"], 16)

                load(0)
                with sp.Fori(1, TURNS) as g:
                    load(g)

            @block.gpsimd
            def _(pool):
                def scale(g):
                    pool.wait_ge(s["sub_gu"], g + 1)
                    pool.tensor_tensor(gu_w[:, :, :, :], gu_w[:, :, :, :], gu_s[:, :, :, :], ALU.mult).then_inc(s["w_gu"], 1)
                    pool.wait_ge(s["sub_dn"], g + 1)
                    pool.tensor_tensor(dn_w[:, :, :], dn_w[:, :, :], dn_s[:, :, :], ALU.mult).then_inc(s["w_dn"], 1)

                def low(g):
                    pool.wait_ge(s["hi_gu"], g + 1)
                    pool.tensor_tensor(gu_lo[:, :, :, :], gu_w[:, :, :, :], raw(gu_hi[:, :, :, :]), ALU.subtract).then_inc(s["lo_gu"], 1)
                    pool.wait_ge(s["hi_dn"], g + 1)
                    pool.tensor_tensor(dn_lo[:, :, :], dn_w[:, :, :], raw(dn_hi[:, :, :]), ALU.subtract).then_inc(s["lo_dn"], 1)

                scale(0)
                low(0)
                with pool.Fori(1, TURNS) as g:
                    scale(g)
                    low(g)
                norm_gpsimd(pool, m, n2)

            @block.tensor
            def _(pe):
                def group(g):
                    pe.wait_ge(s["lo_gu"], g + 1)
                    for j in range(CHAINS):
                        half, k = j // MT, j % MT
                        cols = slice(half * HALF, (half + 1) * HALF)
                        pe.wait_ge(s["h"], CHAINS * g + max(j - 1, 0))
                        for n, (bank, done) in enumerate(((gate[j % 2], s["gate"]), (up[j % 2], s["up"]))):
                            for c in range(KC):
                                last = three(pe, bank[:, :], gu_hi[:, c, n, k * P:(k + 1) * P], gu_lo[:, c, n, k * P:(k + 1) * P],
                                             m.xT_hi[:, c, cols], m.xT_lo[:, c, cols], c == 0, c == KC - 1)
                            last.then_inc(done, 1)
                    pe.wait_ge(s["lo_dn"], g + 1)
                    for b in range(B):
                        pe.wait_ge(s["h_lo"], CHAINS * g + MT * (b // 4 + 1))
                        pe.wait_ge(s["add"], B * g + max(b - 1, 0))
                        for k in range(MT):
                            last = three(pe, rows[b % 2][:, :], h_hi[:, k, b * P:(b + 1) * P], h_lo[:, k, b * P:(b + 1) * P],
                                         dn_hi[:, k, :], dn_lo[:, k, :], k == 0, k == MT - 1)
                        last.then_inc(s["rows"], 1)

                group(0)
                with pe.Fori(1, TURNS) as g:
                    group(g)
                norm_tensor(pe, m, n2)

            @block.scalar
            def _(act):
                def group(g):
                    for j in range(CHAINS + 1):
                        if j < CHAINS:
                            act.wait_ge(s["gate"], CHAINS * g + j + 1)
                            act.activation(act_g[:, j % 2, :], gate[j % 2][:, :], ACT.Silu).then_inc(s["silu"], 1)
                        if j:
                            n = j - 1
                            half, k = n // MT, n % MT
                            act.wait_ge(s["h"], CHAINS * g + n + 1)
                            act.wait_ge(s["rows"], B * g)
                            act.activation(h_hi[:, k, half * HALF:(half + 1) * HALF], h[:, n % 2, :], ACT.Copy).then_inc(s["h_hi"], 1)

                group(0)
                with act.Fori(1, TURNS) as g:
                    group(g)
                norm_scalar(act, m, n2)

            @block.vector
            def _(dve):
                def subtract(g):
                    dve.wait_ge(s["ld_gu"], 96 * (g + 1))
                    dve.wait_ge(s["lo_gu"], g)
                    dve.tensor_tensor(gu_w[:, :, :, :], gu_q[:, :, :, :], gu_z[:, :, :, :], ALU.subtract).then_inc(s["sub_gu"], 1)
                    dve.wait_ge(s["ld_dn"], 48 * (g + 1))
                    dve.wait_ge(s["lo_dn"], g)
                    dve.tensor_tensor(dn_w[:, :, :], dn_q[:, :, :], dn_z[:, :, :], ALU.subtract).then_inc(s["sub_dn"], 1)

                def high_gu(g):
                    dve.wait_ge(s["w_gu"], g + 1)
                    dve.wait_ge(s["up"], CHAINS * g)
                    dve.tensor_copy(gu_hi[:, :, :, :], gu_w[:, :, :, :]).then_inc(s["hi_gu"], 1)

                def high_dn(g):
                    dve.wait_ge(s["w_dn"], g + 1)
                    dve.wait_ge(s["rows"], B * g)
                    dve.tensor_copy(dn_hi[:, :, :], dn_w[:, :, :]).then_inc(s["hi_dn"], 1)

                def group(g, last):
                    for j in range(CHAINS + 1):
                        if j < CHAINS:
                            dve.wait_ge(s["silu"], CHAINS * g + j + 1)
                            dve.wait_ge(s["up"], CHAINS * g + j + 1)
                            dve.wait_ge(s["h_lo"], CHAINS * g + max(j - 1, 0))
                            dve.tensor_tensor(h[:, j % 2, :], act_g[:, j % 2, :], up[j % 2][:, :], ALU.mult).then_inc(s["h"], 1)
                        if j:
                            n = j - 1
                            half, k = n // MT, n % MT
                            dve.wait_ge(s["h_hi"], CHAINS * g + n + 1)
                            dve.tensor_tensor(h_lo[:, k, half * HALF:(half + 1) * HALF], h[:, n % 2, :],
                                              raw(h_hi[:, k, half * HALF:(half + 1) * HALF]), ALU.subtract).then_inc(s["h_lo"], 1)
                        if j == 1 and not last:
                            subtract(g + 1)
                    if not last:
                        high_gu(g + 1)
                    for b in range(B):
                        dve.wait_ge(s["rows"], B * g + b + 1)
                        dve.wait_ge(s["add"], B * g + b)
                        dve.tensor_tensor(m.xtok[:, b, :], m.xtok[:, b, :], rows[b % 2][:, :], ALU.add).then_inc(s["add"], 1)
                    if not last:
                        high_dn(g + 1)

                subtract(0)
                high_gu(0)
                high_dn(0)
                group(0, False)
                with dve.Fori(1, TURNS - 1) as g:
                    group(g, False)
                group(TURNS - 1, True)
                dve.wait_ge(s["add"], B * TURNS)
                norm_vector(dve, m, n2)



AH = 32
AD = D // AH
HC = P // AD
AC = AH // HC
AUG = AD + 1


def self_stage(nc, m, io, sem):
    with ExitStack() as ctx:
        def sb(name, shape, dt=FP32):
            return ctx.enter_context(nc.sbuf_tensor("sa_" + name, shape, dt))

        def pb(name, n=HALF):
            return ctx.enter_context(nc.psum_tensor("sa_" + name, [P, n], FP32))

        w_raw, w_hi, w_lo = (sb(n, [P, KC, 3 * P], dt) for n, dt in (("w_raw", FP32), ("w_hi", F32R), ("w_lo", F32R)))
        o_raw, o_hi, o_lo = (sb(n, [P, KC, D], dt) for n, dt in (("o_raw", FP32), ("o_hi", F32R), ("o_lo", F32R)))
        bias_qk = sb("bias_qk", [P, 2])
        bias_v = sb("bias_v", [P, P])
        bias_o = sb("bias_o", [P, D])
        own = sb("own", [P, HC])
        alibi = sb("alibi", [P, HC, S])
        qT, kT = sb("qT", [P, TOK]), sb("kT", [P, TOK])
        k_own = sb("k_own", [P, 2, HC, S])
        v = sb("v", [P, B, HC, AUG])
        prob = sb("prob", [P, 3, HC, S])
        prT = sb("prT", [P, HC, S])
        peak = sb("peak", [P, 3, HC])
        inv = sb("inv", [P, HC])
        o_tok = sb("o_tok", [P, 2, HC, AD])
        oT_hi, oT_lo = (sb(n, [P, KC, TOK], F32R) for n in ("oT_hi", "oT_lo"))
        score = [pb(f"score{i}", HC * S) for i in range(2)]
        turn = pb("turn", HC * S)
        pv = pb("pv")
        back = pb("back")
        proj = [turn[:, 0:HALF], turn[:, HALF:2 * HALF]]
        m.norm_bank = proj
        s = {n: sem("sa_" + n) for n in (
            "ld_w", "ld_qk", "ld_v", "ld_o", "ld_own", "ld_alibi", "split_hi", "split", "o_hi", "o_lo",
            "ones", "proj", "v", "qk", "k_own", "score", "masked", "peak", "exp", "turn", "prT", "pv", "inv",
            "o_tok", "back", "oT_hi", "oT_lo", "res", "rows", "add")}
        n3 = norm_sems(sem, "n3")
        LAG = 2
        PROJ = B + 4

        with nc.Block() as block:
            @block.sync
            def _(sp):
                sp.dma_start(own[:, :], io["own"]).then_inc(s["ld_own"], 16)
                sp.dma_start(bias_o[:, :], io["b_out"].partition_broadcast(P)).then_inc(s["ld_o"], 16)
                sp.dma_start(o_raw[:, :, :], io["w_oT"].rearrange("(c p) n -> p c n", p=P)).then_inc(s["ld_o"], 16)

                def load(c):
                    sp.wait_ge(s["split"], c)
                    for n in range(3):
                        sp.dma_start(w_raw[:, :, n * P:(n + 1) * P],
                                     io["w_qkvT"].rearrange("(c p) n -> p c n", p=P)[:, :, bass.ds(c * P + n * D, P)]).then_inc(s["ld_w"], 16)
                    sp.wait_ge(s["qk"], 4 * c)
                    for n in range(2):
                        sp.dma_start(bias_qk[:, n:n + 1], io["b_qkv"][bass.ds(c * P + n * D, P)].rearrange("(p a) -> p a", a=1)).then_inc(s["ld_qk"], 16)
                    sp.dma_start(bias_v[:, :], io["b_qkv"][bass.ds(c * P + 2 * D, P)].partition_broadcast(P)).then_inc(s["ld_v"], 16)
                    sp.wait_ge(s["masked"], B * c)
                    sp.dma_start(alibi[:, :, :], io["alibi"].rearrange("(c h) q k -> c q h k", h=HC)[bass.ds(c, 1), :, :, :]
                                 .rearrange("a q h k -> (a q) h k")).then_inc(s["ld_alibi"], 16)

                load(0)
                with sp.Fori(1, AC) as c:
                    load(c)

            @block.gpsimd
            def _(pool):
                def split(c):
                    pool.wait_ge(s["ld_w"], 48 * (c + 1))
                    pool.wait_ge(s["proj"], PROJ * c)
                    pool.tensor_tensor(w_hi[:, :, :], w_raw[:, :, :], bc(m.ones[:, 0:1], 2, [P, KC, 3 * P]), ALU.mult).then_inc(s["split_hi"], 1)
                    pool.wait_ge(s["split_hi"], c + 1)
                    pool.tensor_tensor(w_lo[:, :, :], w_raw[:, :, :], raw(w_hi[:, :, :]), ALU.subtract).then_inc(s["split"], 1)

                def chunk(c, last):
                    for b in range(B):
                        if b == 0:
                            pool.wait_ge(s["qk"], 4 * c + 2)
                        pool.wait_ge(s["score"], B * c + max(b - 1, 0))
                        pool.tensor_tensor(k_own[:, b % 2, :, :], bc(kT[:, b * P:(b + 1) * P], 1, [P, HC, S]),
                                           bc(own[:, :], 2, [P, HC, S]), ALU.mult).then_inc(s["k_own"], 1)
                        if b == 3 and not last:
                            split(c + 1)

                pool.memset(v[:, :, :, :], 1.0).then_inc(s["ones"], 1)
                split(0)
                pool.wait_ge(s["ld_own"], 16)
                chunk(0, False)
                with pool.Fori(1, AC - 1) as c:
                    chunk(c, False)
                chunk(AC - 1, True)
                norm_gpsimd(pool, m, n3)

            @block.tensor
            def _(pe):
                def chunk(c):
                    pe.wait_ge(s["split"], c + 1)
                    for j in range(PROJ):
                        if j >= 2:
                            if j - 2 < B:
                                pe.wait_ge(s["v"], B * c + j - 1)
                            else:
                                pe.wait_ge(s["qk"], 4 * c + j - 2 - B + 1)
                        for k in range(KC):
                            if j < B:
                                last = three(pe, proj[j % 2][:, 0:P], m.xT_hi[:, k, j * P:(j + 1) * P], m.xT_lo[:, k, j * P:(j + 1) * P],
                                             w_hi[:, k, 2 * P:3 * P], w_lo[:, k, 2 * P:3 * P], k == 0, k == KC - 1)
                            else:
                                n, half = 1 - (j - B) // 2, (j - B) % 2
                                cols = slice(half * HALF, (half + 1) * HALF)
                                last = three(pe, proj[j % 2], w_hi[:, k, n * P:(n + 1) * P], w_lo[:, k, n * P:(n + 1) * P],
                                             m.xT_hi[:, k, cols], m.xT_lo[:, k, cols], k == 0, k == KC - 1)
                        last.then_inc(s["proj"], 1)
                    for b in range(B + LAG + 1):
                        if b < B:
                            pe.wait_ge(s["k_own"], B * c + b + 1)
                            if b == 0:
                                pe.wait_ge(s["qk"], 4 * (c + 1))
                            if b >= 2:
                                pe.wait_ge(s["masked"], B * c + b - 1)
                            for n in range(2):
                                last = pe.matmul(score[b % 2][:, n * HALF:(n + 1) * HALF], qT[:, b * P:(b + 1) * P],
                                                 k_own[:, b % 2, :, :].rearrange("p h n -> p (h n)")[:, n * HALF:(n + 1) * HALF],
                                                 start=True, stop=True)
                            last.then_inc(s["score"], 1)
                        u = b - LAG
                        if 0 <= u < B:
                            pe.wait_ge(s["exp"], B * c + u + 1)
                            for n in range(HC):
                                last = pe.transpose(turn[:, n * P:(n + 1) * P], prob[:, u % 3, n, :], m.ident[:, :])
                            last.then_inc(s["turn"], 1)
                        if u >= 1:
                            pe.wait_ge(s["o_tok"], B * c + u)
                            pe.wait_ge(s["oT_lo"], B * c + u - 1)
                            pe.transpose(back[:, 0:P], o_tok[:, (u - 1) % 2, :, :].rearrange("p h d -> p (h d)"), m.ident[:, :]).then_inc(s["back"], 1)
                        if 0 <= u < B:
                            pe.wait_ge(s["prT"], B * c + u + 1)
                            for n in range(HC):
                                last = pe.matmul(pv[:, n * AUG:(n + 1) * AUG], prT[:, n, :], v[:, u, n, :], start=True, stop=True)
                            last.then_inc(s["pv"], 1)

                chunk(0)
                with pe.Fori(1, AC) as c:
                    chunk(c)
                pe.wait_ge(s["oT_lo"], AC * B)
                pe.wait_ge(s["o_lo"], 1)
                for b in range(B):
                    if b >= 2:
                        pe.wait_ge(s["add"], b - 1)
                    for k in range(KC):
                        last = three(pe, score[b % 2][:, 0:HALF], oT_hi[:, k, b * P:(b + 1) * P], oT_lo[:, k, b * P:(b + 1) * P],
                                     o_hi[:, k, :], o_lo[:, k, :], k == 0, k == KC - 1)
                    last.then_inc(s["rows"], 1)
                norm_tensor(pe, m, n3)

            @block.scalar
            def _(act):
                def chunk(c):
                    act.wait_ge(s["ld_qk"], 32 * (c + 1))
                    act.wait_ge(s["score"], B * c)
                    act.wait_ge(s["k_own"], B * c)
                    for j in range(4):
                        n, half = 1 - j // 2, j % 2
                        act.wait_ge(s["proj"], PROJ * c + B + j + 1)
                        act.activation((kT if n else qT)[:, half * HALF:(half + 1) * HALF], proj[(B + j) % 2], ACT.Identity,
                                       bias=bias_qk[:, n:n + 1]).then_inc(s["qk"], 1)
                    for b in range(B + LAG):
                        u = b - LAG
                        if u >= 0:
                            act.wait_ge(s["turn"], B * c + u + 1)
                            act.wait_ge(s["pv"], B * c + u)
                            act.activation(prT[:, :, :].rearrange("p h n -> p (h n)"), turn[:, :], ACT.Copy).then_inc(s["prT"], 1)
                        if b < B:
                            act.wait_ge(s["peak"], B * c + b + 1)
                            for n in range(HC):
                                last = act.activation(prob[:, b % 3, n, :], prob[:, b % 3, n, :], ACT.Exp, bias=peak[:, b % 3, n:n + 1])
                            last.then_inc(s["exp"], 1)

                chunk(0)
                with act.Fori(1, AC) as c:
                    chunk(c)
                norm_scalar(act, m, n3)

            @block.vector
            def _(dve):
                dve.wait_ge(s["ld_o"], 32)
                dve.tensor_copy(o_hi[:, :, :], o_raw[:, :, :]).then_inc(s["o_hi"], 1)
                dve.wait_ge(s["o_hi"], 1)
                dve.tensor_tensor(o_lo[:, :, :], o_raw[:, :, :], raw(o_hi[:, :, :]), ALU.subtract).then_inc(s["o_lo"], 1)
                dve.tensor_tensor(m.xtok[:, :, :], m.xtok[:, :, :], bc(bias_o[:, :], 1, [P, B, D]), ALU.add).then_inc(s["res"], 1)
                dve.wait_ge(s["ones"], 1)

                def chunk(c):
                    dve.wait_ge(s["ld_v"], 16 * (c + 1))
                    dve.wait_ge(s["pv"], B * c)
                    for t in range(B):
                        dve.wait_ge(s["proj"], PROJ * c + t + 1)
                        dve.tensor_tensor(v[:, t, :, 0:AD], proj[t % 2][:, 0:P].rearrange("p (h d) -> p h d", h=HC),
                                          bias_v[:, :].rearrange("p (h d) -> p h d", h=HC), ALU.add).then_inc(s["v"], 1)
                    dve.wait_ge(s["ld_alibi"], 16 * (c + 1))
                    for b in range(B + LAG + 1):
                        if b < B:
                            dve.wait_ge(s["score"], B * c + b + 1)
                            dve.scalar_tensor_tensor(prob[:, b % 3, :, :], score[b % 2][:, :].rearrange("p (h n) -> p h n", h=HC),
                                                     1.0 / math.sqrt(AD), alibi[:, :, :], ALU.mult, ALU.add).then_inc(s["masked"], 1)
                            dve.wait_ge(s["masked"], B * c + b + 1)
                            dve.tensor_reduce(peak[:, b % 3, :], prob[:, b % 3, :, :], AX, ALU.max, negate=True).then_inc(s["peak"], 1)
                        u = b - LAG
                        if u >= 1:
                            dve.wait_ge(s["back"], B * c + u)
                            cols = oT_hi[:, bass.ds(c, 1), (u - 1) * P:u * P].rearrange("p a n -> p (a n)")
                            low = oT_lo[:, bass.ds(c, 1), (u - 1) * P:u * P].rearrange("p a n -> p (a n)")
                            dve.tensor_scalar(cols, back[:, 0:P], 1.0, None, ALU.mult).then_inc(s["oT_hi"], 1)
                            dve.wait_ge(s["oT_hi"], B * c + u)
                            dve.tensor_tensor(low, back[:, 0:P], raw(cols), ALU.subtract).then_inc(s["oT_lo"], 1)
                        if 0 <= u < B:
                            got = pv[:, 0:HC * AUG].rearrange("p (h d) -> p h d", h=HC)
                            dve.wait_ge(s["pv"], B * c + u + 1)
                            dve.reciprocal(inv[:, :], got[:, :, AD]).then_inc(s["inv"], 1)
                            dve.wait_ge(s["inv"], B * c + u + 1)
                            dve.tensor_tensor(o_tok[:, u % 2, :, :], got[:, :, 0:AD], bc(inv[:, :], 2, [P, HC, AD]), ALU.mult).then_inc(s["o_tok"], 1)

                chunk(0)
                with dve.Fori(1, AC) as c:
                    chunk(c)
                dve.wait_ge(s["res"], 1)
                for b in range(B):
                    dve.wait_ge(s["rows"], b + 1)
                    dve.tensor_tensor(m.xtok[:, b, :], m.xtok[:, b, :], score[b % 2][:, 0:HALF], ALU.add).then_inc(s["add"], 1)
                dve.wait_ge(s["add"], B)
                norm_vector(dve, m, n3)



E_, R_ = 8, 16
SCALING = 2.0
Q_FIRST, Q_END = 107, S - 1


def lora_stage(nc, m, io, sem):
    with ExitStack() as ctx:
        def sb(name, shape, dt=FP32):
            return ctx.enter_context(nc.sbuf_tensor("lo_" + name, shape, dt))

        def pb(name):
            return ctx.enter_context(nc.psum_tensor("lo_" + name, [P, HALF], FP32))

        WA = D + P
        w_raw, w_hi, w_lo = (sb(n, [P, KC, WA], dt) for n, dt in (("w_raw", FP32), ("w_hi", F32R), ("w_lo", F32R)))
        b_raw, b_hi, b_lo = (sb(n, [P, D], dt) for n, dt in (("b_raw", FP32), ("b_hi", F32R), ("b_lo", F32R)))
        bias = sb("bias", [P, D])
        r_w = sb("r_w", [P, KC, E_])
        r_b = sb("r_b", [B, E_])
        q_hi, q_lo, q = (sb(n, [P, KC, B]) for n in ("q_hi", "q_lo", "q"))
        lg, pr, wide = sb("lg", [B, E_]), sb("pr", [B, E_]), sb("wide", [B, E_, R_])
        pk, tot, inv = (sb(n, [B, 1]) for n in ("pk", "tot", "inv"))
        route = sb("route", [P, B])
        t = sb("t", [P, B, S])
        t_hi, t_lo = (sb(n, [P, B, S], F32R) for n in ("t_hi", "t_lo"))
        low = [pb(f"low{i}") for i in range(2)]
        rows = [pb(f"rows{i}") for i in range(2)]
        small = pb("small")
        s = {n: sem("lo_" + n) for n in (
            "ld_w", "ld_s", "hi", "lo", "chain", "q", "logits", "lg", "exp", "wide", "route", "low", "t_hi",
            "t_lo", "res", "rows", "add", "stored")}
        n5 = norm_sems(sem, "n5")

        with nc.Block() as block:
            @block.sync
            def _(sp):
                sp.dma_start(r_w[:, :, :], io["r_wT"].rearrange("(c p) n -> p c n", p=P)).then_inc(s["ld_s"], 16)
                sp.dma_start(r_b[:, :], io["r_b"].partition_broadcast(B)).then_inc(s["ld_s"], 16)
                sp.dma_start(bias[:, :], io["f_b"].partition_broadcast(P)).then_inc(s["ld_s"], 16)
                sp.dma_start(w_raw[:, :, D:WA], io["f_aT"].rearrange("(c p) n -> p c n", p=P)).then_inc(s["ld_w"], 16)
                sp.dma_start(w_raw[:, :, 0:D], io["f_wT"].rearrange("(c p) n -> p c n", p=P)).then_inc(s["ld_w"], 16)
                sp.dma_start(b_raw[:, :], io["f_bT"]).then_inc(s["ld_w"], 16)
                for b in range(B):
                    sp.wait_ge(n5["x"], b + 1)
                    sp.dma_start(io["out"][b, :, :], m.xtok[:, b, :]).then_inc(s["stored"], 16)
                sp.wait_ge(s["stored"], 16 * B)

            @block.gpsimd
            def _(pool):
                pool.wait_ge(s["ld_w"], 48)
                pool.wait_ge(s["hi"], 2)
                pool.tensor_tensor(w_lo[:, :, :], w_raw[:, :, :], raw(w_hi[:, :, :]), ALU.subtract).then_inc(s["lo"], 1)
                pool.tensor_tensor(b_lo[:, :], b_raw[:, :], raw(b_hi[:, :]), ALU.subtract).then_inc(s["lo"], 1)
                norm_gpsimd(pool, m, n5)

            @block.tensor
            def _(pe):
                pe.wait_ge(s["ld_s"], 48)
                pe.wait_ge(s["q"], 1)
                for c in range(KC):
                    last = pe.matmul(small[0:B, 0:E_], q[:, c, :], r_w[:, c, :], start=c == 0, stop=c == KC - 1)
                last.then_inc(s["logits"], 1)
                pe.wait_ge(s["lo"], 1)
                for n in range(2):
                    for c in range(KC):
                        last = three(pe, low[n][:, :], w_hi[:, c, D:WA], w_lo[:, c, D:WA], m.xT_hi[:, c, n * HALF:(n + 1) * HALF],
                                     m.xT_lo[:, c, n * HALF:(n + 1) * HALF], c == 0, c == KC - 1)
                    last.then_inc(s["low"], 1)
                pe.wait_ge(s["wide"], 1)
                pe.matmul(small[:, 64:64 + B], wide[:, :, :].rearrange("b e r -> b (e r)"), m.ident[0:B, 0:B], start=True, stop=True).then_inc(s["route"], 1)
                pe.wait_ge(s["lo"], 2)
                for b in range(B):
                    if b >= 2:
                        pe.wait_ge(s["add"], b - 1)
                    for c in range(KC):
                        three(pe, rows[b % 2][:, :], m.xT_hi[:, c, b * P:(b + 1) * P], m.xT_lo[:, c, b * P:(b + 1) * P],
                              w_hi[:, c, 0:D], w_lo[:, c, 0:D], c == 0, False)
                    pe.wait_ge(s["t_lo"], 1)
                    three(pe, rows[b % 2][:, :], t_hi[:, b, :], t_lo[:, b, :], b_hi[:, :], b_lo[:, :], False, True).then_inc(s["rows"], 1)

            @block.scalar
            def _(act):
                act.wait_ge(s["lg"], 1)
                act.activation(pr[:, :], lg[:, :], ACT.Exp, bias=pk[:, :], accum_out=tot[:, :]).then_inc(s["exp"], 1)

            @block.vector
            def _(dve):
                ch = Chain(dve, s["chain"])
                for src, dst in ((m.xT_hi, q_hi), (m.xT_lo, q_lo)):
                    ch.step(dve.tensor_reduce(dst[:, :, :].rearrange("p c b -> p (c b)"),
                                              raw(src[:, :, :]).rearrange("p c (b s) -> p (c b) s", s=S)[:, :, Q_FIRST:Q_END], AX, ALU.add))
                ch.step(dve.tensor_tensor(q[:, :, :], q_hi[:, :, :], q_lo[:, :, :], ALU.add))
                dve.tensor_scalar(q[:, :, :], q[:, :, :], 1.0 / (Q_END - Q_FIRST), None, ALU.mult).then_inc(s["q"], 1)
                dve.wait_ge(s["ld_w"], 48)
                dve.tensor_copy(w_hi[:, :, :], w_raw[:, :, :]).then_inc(s["hi"], 1)
                dve.tensor_copy(b_hi[:, :], b_raw[:, :]).then_inc(s["hi"], 1)
                dve.wait_ge(s["ld_s"], 48)
                dve.wait_ge(s["logits"], 1)
                ch.step(dve.tensor_tensor(lg[:, :], small[0:B, 0:E_], r_b[:, :], ALU.add))
                dve.tensor_reduce(pk[:, :], lg[:, :], AX, ALU.max, negate=True).then_inc(s["lg"], 1)
                dve.wait_ge(s["exp"], 1)
                ch.step(dve.reciprocal(inv[:, :], tot[:, :]))
                ch.step(dve.tensor_scalar(pr[:, :], pr[:, :], inv[:, :], SCALING, ALU.mult, ALU.mult))
                dve.tensor_copy(wide[:, :, :], bc(pr[:, :], 2, [B, E_, R_])).then_inc(s["wide"], 1)
                dve.wait_ge(s["route"], 1)
                ch.step(dve.tensor_copy(route[:, :], small[:, 64:64 + B]))
                dve.wait_ge(s["low"], 2)
                for n in range(2):
                    bs = slice(4 * n, 4 * n + 4)
                    ch.step(dve.tensor_tensor(t[:, bs, :], low[n][:, :].rearrange("p (b s) -> p b s", b=4), bc(route[:, bs], 2, [P, 4, S]), ALU.mult))
                dve.tensor_copy(t_hi[:, :, :], t[:, :, :]).then_inc(s["t_hi"], 1)
                dve.wait_ge(s["t_hi"], 1)
                dve.tensor_tensor(t_lo[:, :, :], t[:, :, :], raw(t_hi[:, :, :]), ALU.subtract).then_inc(s["t_lo"], 1)
                dve.tensor_tensor(m.xtok[:, :, :], m.xtok[:, :, :], bc(bias[:, :], 1, [P, B, D]), ALU.add).then_inc(s["res"], 1)
                dve.wait_ge(s["res"], 1)
                for b in range(B):
                    dve.wait_ge(s["rows"], b + 1)
                    dve.tensor_tensor(m.xtok[:, b, :], m.xtok[:, b, :], rows[b % 2][:, :], ALU.add).then_inc(s["add"], 1)
                dve.wait_ge(s["add"], B)
                norm_vector(dve, m, n5, transposed=False)



STAGES = (hydra_stage, context_stage, cross0_stage, ffn0_stage, self_stage, cross1_stage, lora_stage)


def program(nc, io):
    with ExitStack() as ctx:
        def sb(name, shape, dt=FP32):
            return ctx.enter_context(nc.sbuf_tensor(name, shape, dt))

        m = Memory(sb)
        for n, stage in enumerate(STAGES):
            used = []

            def sem(name):
                used.append(nc.alloc_semaphore(name))
                return used[-1]

            stage(nc, m, io, sem)
            if n < len(STAGES) - 1:
                nc.clear_and_free_semaphores(used)
                nc.all_engine_barrier()



def own_features():
    return np.repeat(np.eye(HC, dtype=np.float32), AD, axis=0)


def alibi_bias():
    slopes = np.float32(1.0) / np.power(np.float32(2.0), np.arange(1, AH + 1, dtype=np.float32) * np.float32(8 / AH))
    bias = slopes[:, None] * np.arange(1 - S, 1, dtype=np.float32)[None, :]
    causal = np.arange(S)[:, None] >= np.arange(S)[None, :]
    return np.where(causal[None], bias[:, None, :], np.float32(-1e9)).astype(np.float32)


def kernel(**inputs):
    import concourse.bacc as bacc
    from concourse.bass_utils import run_bass_kernel_spmd

    a = {n: np.asarray(v) for n, v in inputs.items()}

    def T(x):
        return np.ascontiguousarray(x.T)

    host = {
        "x": a["x"], "xT": T(a["x"].reshape(TOK, D)),
        "w_downT": T(a["L0_attn_w_down"]), "b_down": a["L0_attn_b_down"], "w_upT": T(a["L0_attn_w_up"]),
        "b_up": a["L0_attn_b_up"], "gate1": a["L0_attn_gate1"].reshape(1), "in_wT": T(a["L0_attn_hy_in_w"]),
        "conv_w": T(a["L0_attn_hy_conv_w"][:, 0, :]), "conv_b": a["L0_attn_hy_conv_b"],
        "dt_bias": a["L0_attn_hy_dt_bias"], "a_log": a["L0_attn_hy_A_log"], "d_skip": a["L0_attn_hy_D"],
        "fcD_wT": T(a["L0_attn_hy_fcD_w"]), "norm_w": a["L0_attn_hy_norm_w"], "out_wT": T(a["L0_attn_hy_out_w"]),
        "ctxT": T(a["ctx_4096"].reshape(TOK, D)), "mask": a["mask_1x1xSxS2_ff0"],
        **{w.lower() + n: T(a[f"L{n}_xattn_{w}"]) for n in "01" for w in ("Wq", "Wk", "Wv", "Wo")},
        **{f"{w}_{x}": a[f"L0_ffn_{w}_{x}"] for w in ("gate", "up", "down") for x in "wzs"},
        "w_qkvT": T(a["L1_attn_w_qkv"]), "b_qkv": a["L1_attn_b_qkv"], "w_oT": T(a["L1_attn_w_out"]), "b_out": a["L1_attn_b_out"],
        "own": own_features(), "alibi": alibi_bias(),
        "f_wT": T(a["L1_ffn_W"]), "f_b": a["L1_ffn_b"], "f_aT": T(a["L1_ffn_A"].reshape(E_ * R_, D)),
        "f_bT": np.ascontiguousarray(a["L1_ffn_B"].transpose(0, 2, 1)).reshape(E_ * R_, D),
        "r_wT": T(a["L1_ffn_router_W"]), "r_b": a["L1_ffn_router_b"],
        "q_norm": a["L1_xattn_q_norm_w"], "k_norm": a["L1_xattn_k_norm_w"],
    }
    nc = bacc.Bacc("TRN2", target_bir_lowering=False, num_devices=1)
    arrays, io = {}, {}
    for name, v in host.items():
        arrays["in_" + name] = v
        tensor = nc.dram_tensor("in_" + name, v.shape, mybir.dt.from_np(v.dtype), kind="ExternalInput").ap()
        io[name] = tensor
    io["out"] = nc.dram_tensor("out", (B, S, D), FP32, kind="ExternalOutput").ap()
    program(nc, io)
    r = run_bass_kernel_spmd(nc, [arrays], core_ids=[0])
    return r.results[0]["out"]
```

```python
import math
from contextlib import ExitStack

import numpy as np
import concourse.bass as bass
from concourse import mybir
from concourse.alu_op_type import AluOpType as ALU

FP32 = mybir.dt.float32
F32R = mybir.dt.float32r
INT32 = mybir.dt.int32
ACT = mybir.ActivationFunctionType
AX = mybir.AxisListType.X

P = 128
B, S, D = 8, 128, 512
KC = D // P
TOK = B * S
HALF = 512
LN_EPS = 1e-5



def bc(ap, axis, shape):
    return ap.unsqueeze(axis).to_broadcast(shape)


def raw(ap):
    return ap.bitcast(FP32)


class Memory:

    def __init__(self, sb):
        self.xtok = sb("xtok", [P, B, D])
        self.xT_hi = sb("xT_hi", [P, KC, TOK], F32R)
        self.xT_lo = sb("xT_lo", [P, KC, TOK], F32R)
        self.cT_hi = sb("cT_hi", [P, KC, TOK], F32R)
        self.cT_lo = sb("cT_lo", [P, KC, TOK], F32R)
        self.ident, self.ones = sb("ident", [P, P]), sb("ones", [P, P])
        self.minus_half = sb("minus_half", [P, 32])
        self.stats, self.meanvar = sb("stats", [P, B, 6]), sb("meanvar", [P, B, 2])
        self.var, self.rstd = sb("var", [P, B]), sb("rstd", [P, B])
        self.norm_bank = None


class Chain:

    def __init__(self, eng, sem, per=0, turn=0):
        self.eng, self.sem, self.base, self.n, self.per = eng, sem, turn * per, 0, per

    def step(self, ins):
        self.n += 1
        ins.then_inc(self.sem, 1)
        self.eng.wait_ge(self.sem, self.base + self.n)

    def end(self):
        assert self.n == self.per, (self.n, self.per)


def three(pe, out, a_hi, a_lo, b_hi, b_lo, first, last):
    pe.matmul(out, a_hi, b_hi, start=first, stop=False)
    pe.matmul(out, a_lo, b_hi, start=False, stop=False)
    return pe.matmul(out, a_hi, b_lo, start=False, stop=last)



def norm_sems(sem, tag):
    return {n: sem(f"{tag}_{n}") for n in (
            "stats", "aggr", "var", "rstd", "x", "turned", "hi", "lo")}


def norm_vector(dve, m, s, transposed=True):
    for b in range(B):
        dve.bn_stats(m.stats[:, b, :], m.xtok[:, b, :]).then_inc(s["stats"], 1)
    dve.wait_ge(s["stats"], B)
    for b in range(B):
        dve.bn_aggr(m.meanvar[:, b, :], m.stats[:, b, :]).then_inc(s["aggr"], 1)
    dve.wait_ge(s["aggr"], B)
    dve.tensor_scalar(m.var[:, :], m.meanvar[:, :, 1], LN_EPS, None, ALU.add).then_inc(s["var"], 1)
    dve.wait_ge(s["rstd"], 1)
    for b in range(B + 2):
        if b < B:
            dve.tensor_scalar(m.xtok[:, b, :], m.xtok[:, b, :], m.meanvar[:, b, 0:1], m.rstd[:, b:b + 1],
                              ALU.subtract, ALU.mult).then_inc(s["x"], 1)
        if transposed and b >= 2:
            t = b - 2
            dve.wait_ge(s["hi"], t + 1)
            dve.tensor_tensor(m.xT_lo[:, :, t * P:(t + 1) * P], m.norm_bank[t % 2][:, :].rearrange("p (c n) -> p c n", c=KC),
                              raw(m.xT_hi[:, :, t * P:(t + 1) * P]), ALU.subtract).then_inc(s["lo"], 1)


def norm_gpsimd(pool, m, s):
    pool.wait_ge(s["var"], 1)
    pool.tensor_tensor(m.rstd[:, :], m.var[:, :], m.minus_half[:, 0:B], ALU.pow).then_inc(s["rstd"], 1)


def norm_tensor(pe, m, s):
    for b in range(B):
        pe.wait_ge(s["x"], b + 1)
        if b >= 2:
            pe.wait_ge(s["lo"], b - 1)
        for c in range(KC):
            last = pe.transpose(m.norm_bank[b % 2][:, c * P:(c + 1) * P], m.xtok[:, b, c * P:(c + 1) * P], m.ident[:, :])
        last.then_inc(s["turned"], 1)


def norm_scalar(act, m, s):
    for b in range(B):
        act.wait_ge(s["turned"], b + 1)
        act.activation(m.xT_hi[:, :, b * P:(b + 1) * P], m.norm_bank[b % 2][:, :].rearrange("p (c n) -> p c n", c=KC),
                       ACT.Copy).then_inc(s["hi"], 1)



DM, DIN, DST, NH, HDIM, TAPS = 128, 256, 16, 4, 64, 7
CONV = DIN + 2 * DST
ZDT = DIN + 2 * NH
L = B
DIST = L - 1
LAYERS = 2
EXP_FLOOR = -200.0
A_LOG_CEIL = 84.0


def hydra_stage(nc, m, io, sem):
    with ExitStack() as ctx:
        def sb(name, shape, dt=FP32):
            return ctx.enter_context(nc.sbuf_tensor("hy_" + name, shape, dt))

        def pb(name, n=HALF):
            return ctx.enter_context(nc.psum_tensor("hy_" + name, [P, n], FP32))

        xT0 = sb("xT0", [P, KC, TOK])
        w_down = sb("w_down", [P, KC, DM])
        b_down = sb("b_down", [P, 1])
        w_zdt = sb("w_zdt", [P, ZDT])
        w_xbc = sb("w_xbc", [P, CONV])
        taps = sb("taps", [P, TAPS, CONV])
        w_conv = sb("w_conv", [P, TAPS, CONV])
        conv_b = sb("conv_b", [P, CONV])
        dt_bias = sb("dt_bias", [P, NH])
        a_log = sb("a_log", [P, NH])
        d_skip = sb("d_skip", [P, NH])
        fcd = sb("fcd", [P, 2, NH])
        norm_w = sb("norm_w", [P, 2])
        w_out = sb("w_out", [P, 2, DM])
        w_up = sb("w_up", [P, D])
        b_up = sb("b_up", [P, D])
        gate = sb("gate", [P, 1])
        mix = sb("mix", [P, 2])
        x_mid = sb("x_mid", [P, TOK])
        uT = sb("uT", [P, TOK])
        z_act = sb("z_act", [P, L, DIN])
        xbc = sb("xbc", [P, L, CONV])
        xsT = sb("xsT", [P, 2, TOK])
        dt_raw = sb("dt_raw", [P, L, 2, NH])
        dt = sb("dt", [P, 2, L, NH])
        sp = [sb(f"sp{i}", [P, L * 2 * NH]) for i in range(6)]
        neg_a = sb("neg_a", [P, NH])
        cb_prod = sb("cb_prod", [P, L, L, DST])
        cb = sb("cb", [P, L * L + L + 1])
        seg = sb("seg", [P, 2, DIST, L, NH])
        dec = sb("dec", [P, 2, DIST, L, NH])
        mixw = sb("mixw", [P, (L * L + L + 1) * NH])
        prod = [sb(f"prod{i}", [P, L, DIN]) for i in range(2)]
        yz = sb("yz", [P, L, DIN])
        junk = sb("junk", [P, DIN])
        ssq = sb("ssq", [P, L])
        msq = sb("msq", [P, L])
        rms = sb("rms", [P, L])
        yT = sb("yT", [P, 2, TOK])
        hm = sb("hm", [P, TOK])
        bank = [pb(f"bank{i}") for i in range(6)]
        skip_bank = pb("skip_bank", L * NH)
        m.norm_bank = bank[2:4]
        n0 = norm_sems(sem, "n0")

        ld = {n: sem("hy_ld_" + n) for n in ("x", "gelu", "in", "conv", "small", "up")}
        s = {n: sem("hy_" + n) for n in (
            "ident", "consts", "mid", "mid_act", "u", "wconv", "alpha", "alpha_exp", "a_exp", "na", "z_mm",
            "z_out", "c_mm", "c_out", "xbc", "xs_tr", "xs_T", "skip", "chain", "pool", "sp_in", "sp_exp",
            "seg", "dec", "w_ok", "prod", "y_mm", "yz", "ssq", "msq", "rms", "yn", "y_tr", "y_T", "o_mm",
            "mixed", "up_mm", "xres", "resid")}

        with nc.Block() as block:
            @block.sync
            def _(sp_):
                for c in range(KC):
                    sp_.dma_start(xT0[:, c, :], io["xT"].rearrange("(c p) n -> p c n", p=P)[:, c, :]).then_inc(ld["x"], 16)
                sp_.dma_start(w_down[:, :, :], io["w_downT"].rearrange("(c p) n -> p c n", p=P)).then_inc(ld["gelu"], 16)
                sp_.dma_start(b_down[:, :], io["b_down"].rearrange("(p a) -> p a", a=1)).then_inc(ld["gelu"], 16)
                sp_.dma_start(w_zdt[:, 0:DIN], io["in_wT"][:, 0:DIN]).then_inc(ld["in"], 16)
                sp_.dma_start(w_zdt[:, DIN:ZDT], io["in_wT"][:, DIN + CONV:DIN + CONV + 2 * NH]).then_inc(ld["in"], 16)
                sp_.dma_start(w_xbc[:, :], io["in_wT"][:, DIN:DIN + CONV]).then_inc(ld["in"], 16)
                sp_.dma_start(m.xtok[:, :, :], io["x"].rearrange("b s d -> s b d")).then_inc(ld["up"], 16)
                sp_.dma_start(w_up[:, :], io["w_upT"]).then_inc(ld["up"], 16)
                sp_.dma_start(b_up[:, :], io["b_up"].partition_broadcast(P)).then_inc(ld["up"], 16)

            @block.gpsimd
            def _(pool):
                pool.dma_start(taps[:, :, :], io["conv_w"].partition_broadcast(P)).then_inc(ld["conv"], 16)
                pool.dma_start(conv_b[:, :], io["conv_b"].partition_broadcast(P)).then_inc(ld["small"], 16)
                pool.dma_start(dt_bias[:, :], io["dt_bias"].partition_broadcast(P)).then_inc(ld["small"], 16)
                pool.dma_start(a_log[:, :], io["a_log"].partition_broadcast(P)).then_inc(ld["small"], 16)
                pool.dma_start(d_skip[:, :], io["d_skip"].partition_broadcast(P)).then_inc(ld["small"], 16)
                pool.dma_start(gate[:, :], io["gate1"].partition_broadcast(P)).then_inc(ld["small"], 16)
                for c in range(2):
                    pool.dma_start(norm_w[:, c:c + 1], io["norm_w"][c * P:(c + 1) * P].rearrange("(p a) -> p a", a=1)).then_inc(ld["small"], 16)
                pool.dma_start(fcd[:, :, :], io["fcD_wT"].rearrange("(c p) n -> p c n", p=P)).then_inc(ld["small"], 16)
                pool.dma_start(w_out[:, :, :], io["out_wT"].rearrange("(c p) n -> p c n", p=P)).then_inc(ld["small"], 16)
                pool.memset(m.ident[:, :], 0.0).then_inc(s["ident"], 1)
                pool.wait_ge(s["ident"], 1)
                pool.affine_select(out=m.ident[:, :], in_=m.ident[:, :], compare_op=ALU.not_equal, fill=1.0, base=0,
                                   pattern=[[-1, P]], channel_multiplier=1).then_inc(s["ident"], 1)
                pool.memset(m.minus_half[:, :], -0.5).then_inc(s["consts"], 1)
                pool.memset(m.ones[:, :], 1.0).then_inc(s["consts"], 1)
                pool.wait_ge(ld["conv"], 16)
                pool.wait_ge(ld["in"], 48)
                pool.tensor_tensor(w_conv[:, :, :], taps[:, :, :], bc(w_xbc[:, :], 1, [P, TAPS, CONV]), ALU.mult).then_inc(s["wconv"], 1)
                pool.wait_ge(s["consts"], 2)
                with pool.Fori(0, LAYERS) as i:
                    pool.wait_ge(s["msq"], i + 1)
                    pool.tensor_tensor(rms[:, :], msq[:, :], m.minus_half[:, 0:L], ALU.pow).then_inc(s["rms"], 1)
                norm_gpsimd(pool, m, n0)

            @block.tensor
            def _(pe):
                pe.wait_ge(ld["x"], 16 * KC)
                pe.wait_ge(ld["gelu"], 32)
                for h in range(2):
                    for c in range(KC):
                        last = pe.matmul(bank[h][:, :], w_down[:, c, :], xT0[:, c, h * HALF:(h + 1) * HALF],
                                         start=c == 0, stop=c == KC - 1)
                    last.then_inc(s["mid"], 1)
                pe.wait_ge(s["wconv"], 1)
                pe.wait_ge(s["ident"], 2)
                pe.wait_ge(ld["small"], 16 * 9)
                with pe.Fori(0, LAYERS) as i:
                    pe.wait_ge(s["u"], 2 * i + 2)
                    for t in range(L):
                        if t >= 2:
                            pe.wait_ge(s["z_out"], L * i + t - 1)
                        pe.matmul(bank[t % 2][:, 0:ZDT], uT[:, t * P:(t + 1) * P], w_zdt[:, :],
                                  start=True, stop=True).then_inc(s["z_mm"], 1)
                        if t >= 2:
                            pe.wait_ge(s["c_out"], L * i + t - 1)
                        first = max(0, TAPS - 1 - t)
                        for k in range(first, TAPS):
                            src = t - (TAPS - 1) + k
                            last = pe.matmul(bank[2 + t % 2][:, 0:CONV], uT[:, src * P:(src + 1) * P], w_conv[:, k, :],
                                             start=k == first, stop=k == TAPS - 1)
                        last.then_inc(s["c_mm"], 1)
                    for t in range(L):
                        pe.wait_ge(s["xbc"], L * i + t + 1)
                        if t >= 2:
                            pe.wait_ge(s["xs_T"], L * i + t - 1)
                        for c in range(2):
                            last = pe.transpose(bank[4 + t % 2][:, c * P:(c + 1) * P], xbc[:, t, c * P:(c + 1) * P], m.ident[:, :])
                        last.then_inc(s["xs_tr"], 1)
                    for t in range(L):
                        pe.wait_ge(s["xs_T"], L * i + t + 1)
                        for c in range(2):
                            last = pe.matmul(skip_bank[:, t * NH:(t + 1) * NH], xsT[:, c, t * P:(t + 1) * P], fcd[:, c, :],
                                             start=c == 0, stop=c == 1)
                    last.then_inc(s["skip"], 1)
                    for t in range(L):
                        pe.wait_ge(s["prod"], L * i + t + 1)
                        if t >= 2:
                            pe.wait_ge(s["yz"], L * i + t - 1)
                        for src in range(L):
                            last = pe.matmul(bank[t % 2][:, 0:DIN], m.ident[:, :], prod[t % 2][:, src, :],
                                             start=src == 0, stop=src == L - 1)
                        last.then_inc(s["y_mm"], 1)
                    for t in range(L):
                        pe.wait_ge(s["yn"], L * i + t + 1)
                        if t >= 2:
                            pe.wait_ge(s["y_T"], 2 * (L * i + t - 1))
                        for c in range(2):
                            last = pe.transpose(bank[2 + t % 2][:, c * P:(c + 1) * P], yz[:, t, c * P:(c + 1) * P], m.ident[:, :])
                        last.then_inc(s["y_tr"], 1)
                    for h in range(2):
                        pe.wait_ge(s["y_T"], 2 * (L * i + L))
                        for c in range(2):
                            last = pe.matmul(bank[4 + h][:, :], w_out[:, c, :], yT[:, c, h * HALF:(h + 1) * HALF],
                                             start=c == 0, stop=c == 1)
                        last.then_inc(s["o_mm"], 1)
                pe.wait_ge(ld["up"], 48)
                for b in range(B):
                    pe.wait_ge(s["mixed"], b // 4 + 1)
                    if b >= 2:
                        pe.wait_ge(s["resid"], b - 1)
                    pe.matmul(bank[b % 2][:, :], hm[:, b * P:(b + 1) * P], w_up[:, :], start=True, stop=True).then_inc(s["up_mm"], 1)
                norm_tensor(pe, m, n0)

            @block.scalar
            def _(act):
                for h in range(2):
                    act.wait_ge(s["mid"], h + 1)
                    act.activation(x_mid[:, h * HALF:(h + 1) * HALF], bank[h][:, :], ACT.Gelu, bias=b_down[:, :]).then_inc(s["mid_act"], 1)
                for h in range(2):
                    act.wait_ge(s["mid_act"], h + 1)
                    act.activation(uT[:, h * HALF:(h + 1) * HALF], x_mid[:, h * HALF:(h + 1) * HALF], ACT.Copy).then_inc(s["u"], 1)
                act.wait_ge(ld["small"], 16 * 9)
                act.activation(sp[0][:, 0:1], gate[:, :], ACT.Exp, scale=-1.0).then_inc(s["alpha_exp"], 1)
                act.wait_ge(s["na"], 1)
                act.activation(neg_a[:, :], a_log[:, :], ACT.Exp).then_inc(s["a_exp"], 1)
                with act.Fori(0, LAYERS) as i:
                    for t in range(L):
                        act.wait_ge(s["z_mm"], L * i + t + 1)
                        act.activation(z_act[:, t, :], bank[t % 2][:, 0:DIN], ACT.Silu)
                        act.activation(dt_raw[:, t, :, :].rearrange("p a h -> p (a h)"), bank[t % 2][:, DIN:ZDT], ACT.Copy).then_inc(s["z_out"], 1)
                        act.wait_ge(s["c_out"], L * i + t + 1)
                        act.activation(xbc[:, t, :], xbc[:, t, :], ACT.Silu).then_inc(s["xbc"], 1)
                    act.wait_ge(s["sp_in"], i + 1)
                    act.activation(sp[1][:, :], sp[0][:, :], ACT.Exp).then_inc(s["sp_exp"], 1)
                    for t in range(L):
                        act.wait_ge(s["xs_tr"], L * i + t + 1)
                        act.activation(xsT[:, :, t * P:(t + 1) * P], bank[4 + t % 2][:, 0:DIN].rearrange("p (c n) -> p c n", c=2),
                                       ACT.Copy).then_inc(s["xs_T"], 1)
                    act.wait_ge(s["seg"], i + 1)
                    act.activation(dec[:, :, :, :, :], dec[:, :, :, :, :], ACT.Exp).then_inc(s["dec"], 1)
                    for t in range(L):
                        act.wait_ge(s["yz"], L * i + t + 1)
                        if t:
                            act.wait_ge(s["ssq"], L * i + t)
                        act.activation(junk[:, :], yz[:, t, :], ACT.Square, accum_out=ssq[:, t:t + 1]).then_inc(s["ssq"], 1)
                    for t in range(L):
                        act.wait_ge(s["y_tr"], L * i + t + 1)
                        for c in range(2):
                            act.activation(yT[:, c, t * P:(t + 1) * P], bank[2 + t % 2][:, c * P:(c + 1) * P], ACT.Copy,
                                           scale=norm_w[:, c:c + 1]).then_inc(s["y_T"], 1)
                    for h in range(2):
                        act.wait_ge(s["o_mm"], 2 * i + h + 1)
                        act.activation(uT[:, h * HALF:(h + 1) * HALF], bank[4 + h][:, :], ACT.Copy).then_inc(s["u"], 1)
                norm_scalar(act, m, n0)

            @block.vector
            def _(dve):
                dve.memset(seg[:, :, :, :, :], 0.0).then_inc(s["pool"], 1)
                dve.wait_ge(ld["small"], 16 * 9)
                dve.tensor_scalar(a_log[:, :], a_log[:, :], A_LOG_CEIL, None, ALU.min).then_inc(s["na"], 1)
                dve.wait_ge(s["alpha_exp"], 1)
                pre = Chain(dve, s["alpha"])
                pre.step(dve.tensor_scalar(sp[2][:, 0:1], sp[0][:, 0:1], 1.0, None, ALU.add))
                pre.step(dve.reciprocal(sp[3][:, 0:1], sp[2][:, 0:1]))
                pre.step(dve.tensor_scalar(mix[:, 0:1], sp[3][:, 0:1], 1.0, None, ALU.add))
                pre.step(dve.tensor_scalar(mix[:, 1:2], sp[3][:, 0:1], -1.0, 1.0, ALU.mult, ALU.add))
                dve.wait_ge(s["a_exp"], 1)
                pre.step(dve.tensor_scalar(neg_a[:, :], neg_a[:, :], -1.0, None, ALU.mult))
                dve.wait_ge(s["pool"], 1)
                with dve.Fori(0, LAYERS) as i:
                    ch = Chain(dve, s["chain"], 47, i)
                    for t in range(L):
                        dve.wait_ge(s["c_mm"], L * i + t + 1)
                        dve.tensor_tensor(xbc[:, t, :], bank[2 + t % 2][:, 0:CONV], conv_b[:, :], ALU.add).then_inc(s["c_out"], 1)
                    dve.wait_ge(s["z_out"], L * i + L)
                    v, e, z, z2, q = sp[2], sp[1], sp[3], sp[4], sp[5]
                    ch.step(dve.tensor_tensor(v[:, :].rearrange("p (a t h) -> p a t h", a=2, h=NH),
                                              dt_raw[:, :, :, :].rearrange("p t a h -> p a t h"),
                                              dt_bias[:, :].unsqueeze(1).unsqueeze(1).to_broadcast([P, 2, L, NH]), ALU.add))
                    dve.scalar_tensor_tensor(sp[0][:, :], v[:, :], -1.0, v[:, :], ALU.mult, ALU.min).then_inc(s["sp_in"], 1)
                    dve.wait_ge(s["sp_exp"], i + 1)
                    ch.step(dve.tensor_scalar(q[:, :], e[:, :], 2.0, None, ALU.add))
                    ch.step(dve.reciprocal(z[:, :], q[:, :]))
                    ch.step(dve.tensor_tensor(z[:, :], z[:, :], e[:, :], ALU.mult))
                    ch.step(dve.tensor_tensor(z2[:, :], z[:, :], z[:, :], ALU.mult))
                    ch.step(dve.tensor_scalar(q[:, :], z2[:, :], 1.0 / 15, None, ALU.mult))
                    for n in (13, 11, 9, 7, 5, 3):
                        ch.step(dve.scalar_tensor_tensor(q[:, :], q[:, :], 1.0 / n, z2[:, :], ALU.add, ALU.mult))
                    ch.step(dve.scalar_tensor_tensor(q[:, :], q[:, :], 1.0, z[:, :], ALU.add, ALU.mult))
                    ch.step(dve.tensor_scalar(v[:, :], v[:, :], 0.0, None, ALU.max))
                    ch.step(dve.scalar_tensor_tensor(dt[:, :, :, :].rearrange("p a t h -> p (a t h)"), q[:, :], 2.0, v[:, :],
                                                     ALU.mult, ALU.add))
                    for d in range(1, DIST):
                        n = DIST - d
                        dve.tensor_tensor(seg[:, 0, d, 0:n, :], seg[:, 0, d - 1, 0:n, :], dt[:, 0, d:d + n, :], ALU.add).then_inc(s["chain"], 1)
                        ch.n += 1
                        ch.step(dve.tensor_tensor(seg[:, 1, d, d + 1:L, :], seg[:, 1, d - 1, d + 1:L, :], dt[:, 1, 1:1 + n, :], ALU.add))
                    ch.step(dve.tensor_tensor(dec[:, :, :, :, :].rearrange("p a d s h -> p (a d s) h"),
                                              seg[:, :, :, :, :].rearrange("p a d s h -> p (a d s) h"),
                                              bc(neg_a[:, :], 1, [P, 2 * DIST * L, NH]), ALU.mult))
                    dve.tensor_scalar(dec[:, :, :, :, :], dec[:, :, :, :, :], EXP_FLOOR, None, ALU.max).then_inc(s["seg"], 1)
                    dve.wait_ge(s["xbc"], L * i + L)
                    ch.step(dve.tensor_tensor(cb_prod[:, :, :, :], bc(xbc[:, :, DIN + DST:CONV], 2, [P, L, L, DST]),
                                              bc(xbc[:, :, DIN:DIN + DST], 1, [P, L, L, DST]), ALU.mult))
                    ch.step(dve.tensor_reduce(cb[:, 0:L * L], cb_prod[:, :, :, :].rearrange("p t s n -> p (t s) n"), AX, ALU.add))
                    dve.wait_ge(s["dec"], i + 1)
                    for a in range(2):
                        ch.step(dve.tensor_tensor(dec[:, a, :, :, :], dec[:, a, :, :, :], bc(dt[:, a, :, :], 1, [P, DIST, L, NH]), ALU.mult))

                    def diag(t0, s0, n):
                        o = (L * t0 + s0) * NH
                        return mixw[:, o:o + n * (L + 1) * NH].rearrange("p (n k) -> p n k", k=(L + 1) * NH)[:, :, 0:NH]

                    def cdiag(t0, s0, n):
                        o = L * t0 + s0
                        return cb[:, o:o + n * (L + 1)].rearrange("p (n k) -> p n k", k=L + 1)[:, :, 0:1].to_broadcast([P, n, NH])

                    for d in range(DIST):
                        n = DIST - d
                        dve.tensor_tensor(diag(d + 1, 0, n), cdiag(d, 0, n), dec[:, 0, d, 0:n, :], ALU.mult).then_inc(s["chain"], 1)
                        dve.tensor_tensor(diag(0, d + 1, n), cdiag(1, d + 1, n), dec[:, 1, d, d + 1:L, :], ALU.mult).then_inc(s["chain"], 1)
                        ch.n += 2
                    dve.wait_ge(s["skip"], i + 1)
                    ch.step(dve.tensor_tensor(diag(0, 0, L), skip_bank[:, :].rearrange("p (t h) -> p t h", h=NH),
                                              bc(d_skip[:, :], 1, [P, L, NH]), ALU.add))
                    ch.end()
                    for t in range(L + 1):
                        if t < L:
                            if t >= 2:
                                dve.wait_ge(s["y_mm"], L * i + t - 1)
                            dve.tensor_tensor(prod[t % 2][:, :, :].rearrange("p s (h n) -> p s h n", h=NH),
                                              xbc[:, :, 0:DIN].rearrange("p s (h n) -> p s h n", h=NH),
                                              bc(mixw[:, t * L * NH:(t + 1) * L * NH].rearrange("p (s h) -> p s h", h=NH), 3,
                                                 [P, L, NH, HDIM]), ALU.mult).then_inc(s["prod"], 1)
                        if t:
                            dve.wait_ge(s["y_mm"], L * i + t)
                            dve.tensor_tensor(yz[:, t - 1, :], bank[(t - 1) % 2][:, 0:DIN], z_act[:, t - 1, :], ALU.mult).then_inc(s["yz"], 1)
                    dve.wait_ge(s["ssq"], L * i + L)
                    dve.tensor_scalar(msq[:, :], ssq[:, :], 1.0 / DIN, 1e-5, ALU.mult, ALU.add).then_inc(s["msq"], 1)
                    dve.wait_ge(s["rms"], i + 1)
                    for t in range(L):
                        dve.tensor_scalar(yz[:, t, :], yz[:, t, :], rms[:, t:t + 1], None, ALU.mult).then_inc(s["yn"], 1)
                dve.wait_ge(ld["up"], 48)
                dve.scalar_tensor_tensor(m.xtok[:, :, :], m.xtok[:, :, :], 2.0, bc(b_up[:, :], 1, [P, B, D]), ALU.mult, ALU.add).then_inc(s["xres"], 1)
                for h in range(2):
                    cols = slice(h * HALF, (h + 1) * HALF)
                    dve.wait_ge(s["u"], 2 * LAYERS + h + 1)
                    pre.step(dve.tensor_scalar(x_mid[:, cols], x_mid[:, cols], mix[:, 0:1], None, ALU.mult))
                    dve.scalar_tensor_tensor(hm[:, cols], uT[:, cols], mix[:, 1:2], x_mid[:, cols], ALU.mult, ALU.add).then_inc(s["mixed"], 1)
                dve.wait_ge(s["xres"], 1)
                for b in range(B):
                    dve.wait_ge(s["up_mm"], b + 1)
                    dve.tensor_tensor(m.xtok[:, b, :], m.xtok[:, b, :], bank[b % 2][:, :], ALU.add).then_inc(s["resid"], 1)
                dve.wait_ge(s["resid"], B)
                norm_vector(dve, m, n0)



class Attention:
    Q = 4

    def __init__(self, tag, groups, hd, key_tiles, normed, weights):
        self.tag, self.G, self.HD, self.KT, self.normed, self.weights = tag, groups, hd, key_tiles, normed, weights
        self.T = B * key_tiles
        self.KEYS = key_tiles * P
        self.NH = HALF // self.KEYS
        self.PARTS = self.Q // self.NH
        self.U = B * self.PARTS
        self.KCH = self.T if normed else 4
        self.CH = self.KCH + 2 * self.Q
        self.LAG = 2
        self.EARLY = (2 * self.Q - 3, 2 * self.Q - 2)
        self.QS = 2 * self.Q - 1
        self.TURN = (self.Q - 1, self.Q)


def attention_stage(nc, m, io, sem, a):
    wq, wk, wv, wo = (io[w] for w in a.weights)
    G, HD, KT, T, KEYS, NQ, PARTS, U, CH, LAG, Q = a.G, a.HD, a.KT, a.T, a.KEYS, a.NH, a.PARTS, a.U, a.CH, a.LAG, a.Q
    KCH, QS = a.KCH, a.QS
    KW = 2 * HD if a.normed else HD
    scale = 1.0 / math.sqrt(HD)
    with ExitStack() as ctx:
        def sb(name, shape, dt=FP32):
            return ctx.enter_context(nc.sbuf_tensor(f"{a.tag}_{name}", shape, dt))

        def pb(name):
            return ctx.enter_context(nc.psum_tensor(f"{a.tag}_{name}", [P, HALF], FP32))

        raw_w = sb("raw_w", [P, Q * D])
        raw_q, raw_o = raw_w[:, 0:KC * Q * HD].rearrange("p (c n) -> p c n", c=KC), raw_w[0:HD, :].rearrange("p (h n) -> p h n", h=Q)
        q_hi, q_lo = (sb(n, [P, KC, Q * HD], F32R) for n in ("q_hi", "q_lo"))
        raw_kv, kv_hi, kv_lo = (sb(n, [P, KC, KW], dt) for n, dt in (("raw_kv", FP32), ("kv_hi", F32R), ("kv_lo", F32R)))
        o_hi, o_lo = (sb(n, [HD, Q, D], F32R) for n in ("o_hi", "o_lo"))
        qT = sb("qT", [HD, Q, TOK])
        if a.normed:
            kv = sb("kv", [P, T, 2 * HD])
            kn = sb("kn", [P, T, HD])
        else:
            v_all = sb("v_all", [P, T, G * HD])
            v_g = sb("v_g", [P, T, HD])
        kT = sb("kT", [HD, T, P])
        prob = sb("prob", [P, 3, NQ, KEYS])
        prT = sb("prT", [P, 2, NQ * KT, P])
        peak = sb("peak", [P, 3, NQ])
        total = sb("total", [P, 3, NQ])
        inv = sb("inv", [P, 3, NQ])
        out_hi = sb("out_hi", [HD, 2, Q, P], F32R)
        out_lo = sb("out_lo", [HD, 2, Q, P], F32R)
        if a.normed:
            mask = sb("mask", [P, P])
            nw = sb("nw", [P, 2])
            nw2 = sb("nw2", [P, 1])
            q_sq = sb("q_sq", [P, 2, HALF])
            q_ms = sb("q_ms", [P, 2 * Q, 4])
            q_rs = sb("q_rs", [P, 2 * Q, 4])
            k_ms = sb("k_ms", [P, T])
            k_rs = sb("k_rs", [P, T])
        score = [pb(f"score{i}") for i in range(2)]
        turn = pb("turn")
        mixed = [pb(f"mixed{i}") for i in range(2)]
        rows = pb("rows")
        proj = [pb(f"proj{i}") for i in range(2)]
        m.norm_bank = proj

        s = {n: sem(f"{a.tag}_{n}") for n in (
            "ld_q", "ld_kv", "ld_o", "ld_c", "split_hi", "split_q", "split_kv", "split_o", "proj", "evac",
            "nw", "q_sq", "q_ssq", "q_ms", "q_rs", "k_sq", "k_ms", "k_rs", "kn", "k_turn", "kT", "score",
            "masked", "peak", "exp", "inv", "norm", "turn", "prT", "pv", "out_hi", "out_lo", "rows", "add",
            "ld_v", "v_hi", "v_split", "v_proj", "v_evac", "v_g")}
        n1 = norm_sems(sem, a.tag + "n")
        chunks = 4
        HI_TURN = 3 * chunks

        with nc.Block() as block:
            @block.sync
            def _(sp):
                if a.normed:
                    sp.dma_start(mask[:, :], io["mask"][0, 0, :, :]).then_inc(s["ld_c"], 16)
                    sp.dma_start(nw[:, 0:1], io["q_norm"].rearrange("(p a) -> p a", a=1)).then_inc(s["ld_c"], 16)
                    sp.dma_start(nw[:, 1:2], io["k_norm"].rearrange("(p a) -> p a", a=1)).then_inc(s["ld_c"], 16)

                def load(g):
                    sp.wait_ge(s["split_kv"], chunks * g)
                    for n, w in ((0, wk), (1, wv))[0:KW // HD]:
                        sp.dma_start(raw_kv[:, :, n * HD:(n + 1) * HD],
                                     w.rearrange("(c p) n -> p c n", p=P)[:, :, bass.ds(g * HD, HD)]).then_inc(s["ld_kv"], 16)
                    sp.wait_ge(s["split_o"], chunks * g)
                    sp.dma_start(raw_q[:, :, :], wq.rearrange("(c p) n -> p c n", p=P)[:, :, bass.ds(g * Q * HD, Q * HD)]).then_inc(s["ld_q"], 16)
                    sp.wait_ge(s["split_q"], chunks * (g + 1))
                    sp.dma_start(raw_o[:, :, :], wo.rearrange("(g h d) n -> g d h n", h=Q, d=HD)[bass.ds(g, 1), :, :, :]
                                 .rearrange("a d h n -> (a d) h n")).then_inc(s["ld_o"], 16)

                if not a.normed:
                    sp.dma_start(raw_q[:, :, :], wv.rearrange("(c p) n -> p c n", p=P)).then_inc(s["ld_v"], 16)
                    sp.wait_ge(s["v_split"], chunks)
                load(0)
                with sp.Fori(1, G) as g:
                    load(g)

            @block.gpsimd
            def _(pool):
                def split(w, hi, lo, n, done, turn, high=s["split_hi"]):
                    one = bc(m.ones[0:w.shape[0], 0:1], 2, [w.shape[0], 1, w.shape[2]])
                    pool.tensor_tensor(hi[:, n:n + 1, :], w[:, n:n + 1, :], one, ALU.mult).then_inc(high, 1)
                    pool.wait_ge(high, turn + 1)
                    pool.tensor_tensor(lo[:, n:n + 1, :], w[:, n:n + 1, :], raw(hi[:, n:n + 1, :]), ALU.subtract).then_inc(done, 1)

                def split_inputs(g, n):
                    if n == 0:
                        pool.wait_ge(s["ld_kv"], 16 * (KW // HD) * (g + 1))
                        pool.wait_ge(s["proj"], CH * g)
                    if n == chunks:
                        pool.wait_ge(s["ld_q"], 16 * (g + 1))
                    if n < chunks:
                        split(raw_kv, kv_hi, kv_lo, n, s["split_kv"], g * HI_TURN + n)
                    else:
                        split(raw_q, q_hi, q_lo, n - chunks, s["split_q"], g * HI_TURN + n)

                def norm(g, u):
                    pool.wait_ge(s["inv"], U * g + u + 1)
                    pool.tensor_tensor(prob[:, u % 3, :, :], prob[:, u % 3, :, :], bc(inv[:, u % 3, :], 2, [P, NQ, KEYS]),
                                       ALU.mult).then_inc(s["norm"], 1)

                def group(g, last):
                    pool.wait_ge(s["ld_o"], 16 * (g + 1))
                    pool.wait_ge(s["rows"], B * g)
                    for n in range(chunks):
                        split(raw_o, o_hi, o_lo, n, s["split_o"], g * HI_TURN + 2 * chunks + n)
                    if a.normed:
                        pool.wait_ge(s["k_ms"], g + 1)
                        pool.tensor_tensor(k_rs[:, :], k_ms[:, :], m.minus_half[:, 0:T], ALU.pow).then_inc(s["k_rs"], 1)
                        for j in range(2 * Q):
                            if j == 2 * Q - 1:
                                norm(g, 0)
                            pool.wait_ge(s["evac"], CH * g + KCH + j + 1)
                            if j >= 2:
                                pool.wait_ge(s["q_ssq"], QS * g + j - 1)
                            part = qT[:, j % Q, (j // Q) * HALF:(j // Q + 1) * HALF]
                            pool.tensor_tensor(q_sq[:, j % 2, :], part, part, ALU.mult).then_inc(s["q_sq"], 1)
                            if j >= 2:
                                pool.wait_ge(s["q_ms"], QS * g + j - 1)
                                pool.tensor_tensor(q_rs[:, j - 2, :], q_ms[:, j - 2, :], m.minus_half[:, 0:4], ALU.pow).then_inc(s["q_rs"], 1)
                    for u in range(U):
                        if u or not a.normed:
                            norm(g, u)
                        if a.normed and u == 1:
                            pool.wait_ge(s["q_ms"], QS * (g + 1))
                            pool.tensor_tensor(q_rs[:, QS - 1:QS + 1, :].rearrange("p a n -> p (a n)"),
                                               q_ms[:, QS - 1:QS + 1, :].rearrange("p a n -> p (a n)"), m.minus_half[:, 0:8],
                                               ALU.pow).then_inc(s["q_rs"], 1)
                        if not last and u % PARTS == 0:
                            split_inputs(g + 1, u // PARTS)

                if not a.normed:
                    pool.wait_ge(s["ld_v"], 16)
                    for n in range(chunks):
                        split(raw_q, q_hi, q_lo, n, s["v_split"], n, s["v_hi"])
                for n in range(2 * chunks):
                    if n == chunks and not a.normed:
                        pool.wait_ge(s["v_proj"], T)
                    split_inputs(0, n)
                group(0, False)
                with pool.Fori(1, G - 1) as g:
                    group(g, False)
                group(G - 1, True)
                norm_gpsimd(pool, m, n1)

            @block.tensor
            def _(pe):
                def source(t, c):
                    b, k = t // KT, t % KT
                    src = (m.cT_hi, m.cT_lo) if k == 0 else (m.xT_hi, m.xT_lo)
                    return [x[:, c, b * P:(b + 1) * P] for x in src]

                def group(g):
                    pe.wait_ge(s["split_kv"], chunks * (g + 1))
                    if a.normed:
                        pe.wait_ge(s["q_ms"], QS * g)
                    for t in range(KCH):
                        if t >= 2:
                            pe.wait_ge(s["evac"], CH * g + t - 1)
                        for c in range(KC):
                            if a.normed:
                                last = three(pe, proj[t % 2][:, 0:KW], *source(t, c), kv_hi[:, c, :], kv_lo[:, c, :], c == 0, c == KC - 1)
                            else:
                                cols = slice((t % 2) * HALF, (t % 2 + 1) * HALF)
                                src = (m.xT_hi, m.xT_lo) if t // 2 else (m.cT_hi, m.cT_lo)
                                last = three(pe, proj[t % 2][0:HD, :], kv_hi[:, c, :], kv_lo[:, c, :], src[0][:, c, cols], src[1][:, c, cols],
                                             c == 0, c == KC - 1)
                        last.then_inc(s["proj"], 1)
                    def scores(u):
                        b, h0 = u // PARTS, (u % PARTS) * NQ
                        if u >= 2:
                            pe.wait_ge(s["masked"] if a.normed else s["exp"], U * g + u - 1)
                        for h in range(NQ):
                            last = pe.matmul(score[u % 2][:, h * KEYS:(h + 1) * KEYS], qT[:, h0 + h, b * P:(b + 1) * P],
                                             kT[:, b * KT:(b + 1) * KT, :].rearrange("p t n -> p (t n)"), start=True, stop=True)
                        last.then_inc(s["score"], 1)

                    pe.wait_ge(s["split_q"], chunks * (g + 1))
                    def squares(bank, col, j):
                        for n in range(4):
                            last = pe.matmul(bank[:, col + n:col + n + 1], q_sq[:, j % 2, n * P:(n + 1) * P], m.ones[:, 0:1],
                                             start=True, stop=True)
                        return last

                    for j in range(2 * Q):
                        h, cols = j % Q, slice((j // Q) * HALF, (j // Q + 1) * HALF)
                        pe.wait_ge(s["evac"], CH * g + KCH + j - 1)
                        for c in range(KC):
                            last = three(pe, proj[(KCH + j) % 2][0:HD, :], q_hi[:, c, h * HD:(h + 1) * HD], q_lo[:, c, h * HD:(h + 1) * HD],
                                         m.xT_hi[:, c, cols], m.xT_lo[:, c, cols], c == 0, c == KC - 1)
                        last.then_inc(s["proj"], 1)
                        if a.normed and j >= 2:
                            pe.wait_ge(s["q_sq"], 2 * Q * g + j - 1)
                            if j == 2:
                                pe.wait_ge(s["add"], B * g)
                            if j > 2:
                                pe.wait_ge(s["q_ms"], QS * g + j - 2)
                            squares(rows, 4 * (j - 2), j - 2).then_inc(s["q_ssq"], 1)
                        if a.normed and j in a.TURN:
                            i = a.TURN.index(j)
                            pe.wait_ge(s["kn"], g + 1)
                            if i:
                                pe.wait_ge(s["kT"], 2 * g + 1)
                            for n in range(4):
                                last = pe.transpose(turn[0:HD, n * P:(n + 1) * P], kn[:, 4 * i + n, :], m.ident[:, :])
                            last.then_inc(s["k_turn"], 1)
                        if j in a.EARLY:
                            pe.wait_ge(s["evac"], CH * g + KCH + Q)
                            if a.normed:
                                pe.wait_ge(s["kT"], 2 * (g + 1))
                            scores(a.EARLY.index(j))
                    if not a.normed:
                        pe.wait_ge(s["v_g"], g + 1)
                    pe.wait_ge(s["evac"], CH * (g + 1))
                    pe.wait_ge(s["split_o"], chunks * (g + 1))

                    def out_rows(b):
                        pe.wait_ge(s["out_lo"], U * g + PARTS * (b + 1))
                        pe.wait_ge(s["add"], B * g + b)
                        for h in range(Q):
                            last = three(pe, rows[:, :], out_hi[:, b % 2, h, :], out_lo[:, b % 2, h, :], o_hi[:, h, :], o_lo[:, h, :],
                                         h == 0, h == Q - 1)
                        last.then_inc(s["rows"], 1)

                    for u in range(LAG, U + LAG + 1):
                        v = u - LAG
                        if v < U:
                            pe.wait_ge(s["norm"], U * g + v + 1)
                            if v:
                                pe.wait_ge(s["prT"], U * g + v)
                            for n in range(NQ * KT):
                                h, k = n // KT, n % KT
                                last = pe.transpose(turn[:, n * P:(n + 1) * P], prob[:, v % 3, h, k * P:(k + 1) * P], m.ident[:, :])
                            last.then_inc(s["turn"], 1)
                        if u < U:
                            scores(u)
                        if a.normed and u == LAG:
                            pe.wait_ge(s["q_sq"], 2 * Q * (g + 1))
                            for i in range(2):
                                last = squares(proj[0], 4 * i, QS - 1 + i)
                            last.then_inc(s["q_ssq"], 1)
                        if v > 0 and v % PARTS == 0:
                            out_rows(v // PARTS - 1)
                        if v < U:
                            b = v // PARTS
                            pe.wait_ge(s["prT"], U * g + v + 1)
                            if v >= 2:
                                pe.wait_ge(s["out_lo"], U * g + v - 1)
                            for k in range(KT):
                                vs = kv[:, b * KT + k, HD:2 * HD] if a.normed else v_g[:, b * KT + k, :]
                                last = pe.matmul(mixed[v % 2][0:HD, 0:NQ * P], vs,
                                                 prT[:, v % 2, :, :].rearrange("p (h t) n -> p h t n", t=KT)[:, :, k, :],
                                                 start=k == 0, stop=k == KT - 1)
                            last.then_inc(s["pv"], 1)

                if not a.normed:
                    pe.wait_ge(s["v_split"], chunks)
                    for t in range(T):
                        if t >= 2:
                            pe.wait_ge(s["v_evac"], t - 1)
                        for c in range(KC):
                            last = three(pe, proj[t % 2][:, 0:G * HD], *source(t, c), q_hi[:, c, :], q_lo[:, c, :], c == 0, c == KC - 1)
                        last.then_inc(s["v_proj"], 1)
                    pe.wait_ge(s["v_evac"], T)
                group(0)
                with pe.Fori(1, G) as g:
                    group(g)
                norm_tensor(pe, m, n1)

            @block.scalar
            def _(act):
                def group(g):
                    act.wait_ge(s["pv"], U * g)
                    for t in range(KCH):
                        act.wait_ge(s["proj"], CH * g + t + 1)
                        if a.normed:
                            act.activation(kv[:, t, :], proj[t % 2][:, 0:KW], ACT.Copy).then_inc(s["evac"], 1)
                        else:
                            half = t % 2
                            act.activation(kT[:, :, :].rearrange("p (b k) n -> p k b n", k=KT)[:, t // 2, half * B // 2:(half + 1) * B // 2, :],
                                           proj[half][0:HD, :].rearrange("p (b n) -> p b n", n=P), ACT.Copy).then_inc(s["evac"], 1)

                    def exps(u):
                        act.wait_ge(s["peak"], U * g + u + 1)
                        for h in range(NQ):
                            src = prob[:, u % 3, h, :] if a.normed else score[u % 2][:, h * KEYS:(h + 1) * KEYS]
                            last = act.activation(prob[:, u % 3, h, :], src, ACT.Exp, bias=peak[:, u % 3, h:h + 1],
                                                  accum_out=total[:, u % 3, h:h + 1])
                        last.then_inc(s["exp"], 1)

                    for j in range(2 * Q):
                        act.wait_ge(s["proj"], CH * g + KCH + j + 1)
                        act.activation(qT[:, j % Q, (j // Q) * HALF:(j // Q + 1) * HALF], proj[(KCH + j) % 2][0:HD, :], ACT.Copy,
                                       scale=1.0 if a.normed else scale).then_inc(s["evac"], 1)
                        if a.normed and j in a.TURN:
                            i = a.TURN.index(j)
                            act.wait_ge(s["k_turn"], 2 * g + i + 1)
                            act.activation(kT[:, 4 * i:4 * i + 4, :].rearrange("p t n -> p (t n)"), turn[0:HD, :], ACT.Copy,
                                           scale=nw2[:, :]).then_inc(s["kT"], 1)
                        if j - 1 in a.EARLY:
                            exps(a.EARLY.index(j - 1))
                    for u in range(LAG, U + LAG):
                        v = u - LAG
                        act.wait_ge(s["turn"], U * g + v + 1)
                        act.activation(prT[:, v % 2, :, :].rearrange("p h n -> p (h n)"), turn[:, :], ACT.Copy).then_inc(s["prT"], 1)
                        if u < U:
                            exps(u)
                        b, h0 = v // PARTS, (v % PARTS) * NQ
                        act.wait_ge(s["pv"], U * g + v + 1)
                        act.wait_ge(s["rows"], B * g + max(b - 1, 0))
                        act.activation(out_hi[:, b % 2, h0:h0 + NQ, :].rearrange("p h n -> p (h n)"), mixed[v % 2][0:HD, 0:NQ * P],
                                       ACT.Copy).then_inc(s["out_hi"], 1)

                if a.normed:
                    act.wait_ge(s["nw"], 1)
                else:
                    for t in range(T):
                        act.wait_ge(s["v_proj"], t + 1)
                        act.activation(v_all[:, t, :], proj[t % 2][:, 0:G * HD], ACT.Copy).then_inc(s["v_evac"], 1)
                group(0)
                with act.Fori(1, G) as g:
                    group(g)
                norm_scalar(act, m, n1)

            @block.vector
            def _(dve):
                def peaks(g, u):
                    b = u // PARTS
                    dve.wait_ge(s["score"], U * g + u + 1)
                    if a.normed:
                        if u in (0, B // 2):
                            dve.wait_ge(s["q_rs"], QS * g + (QS if u else Q))
                        for h in range(NQ):
                            last = dve.scalar_tensor_tensor(prob[:, u % 3, h, :], score[u % 2][:, h * KEYS:(h + 1) * KEYS],
                                                            q_rs[:, b // 4 * Q + h, b % 4:b % 4 + 1], mask[:, :],
                                                            ALU.mult, ALU.add)
                        last.then_inc(s["masked"], 1)
                        dve.wait_ge(s["masked"], U * g + u + 1)
                        src = prob[:, u % 3, :, :]
                    else:
                        src = score[u % 2][:, :].rearrange("p (h n) -> p h n", h=NQ)
                    dve.tensor_reduce(peak[:, u % 3, :], src, AX, ALU.max, negate=True).then_inc(s["peak"], 1)

                def inverse(g, u):
                    dve.wait_ge(s["exp"], U * g + u + 1)
                    dve.reciprocal(inv[:, u % 3, :], total[:, u % 3, :]).then_inc(s["inv"], 1)

                def group(g):
                    if a.normed:
                        dve.wait_ge(s["evac"], CH * g + T)
                        dve.tensor_tensor(kn[:, :, :], kv[:, :, 0:HD], kv[:, :, 0:HD], ALU.mult).then_inc(s["k_sq"], 1)
                        dve.wait_ge(s["k_sq"], 3 * g + 1)
                        dve.tensor_reduce(k_ms[:, :], kn[:, :, :], AX, ALU.add).then_inc(s["k_sq"], 1)
                        dve.wait_ge(s["k_sq"], 3 * g + 2)
                        dve.tensor_scalar(k_ms[:, :], k_ms[:, :], 1.0 / HD, 1e-5, ALU.mult, ALU.add).then_inc(s["k_ms"], 1)
                        dve.wait_ge(s["k_rs"], g + 1)
                        dve.tensor_tensor(kn[:, :, :], kv[:, :, 0:HD], bc(k_rs[:, :], 2, [P, T, HD]), ALU.mult).then_inc(s["kn"], 1)
                        dve.wait_ge(s["kn"], g + 1)
                        dve.memset(peak[:, 0, :], 0.0).then_inc(s["k_sq"], 1)
                        for j in range(QS - 1):
                            dve.wait_ge(s["q_ssq"], QS * g + j + 1)
                            dve.tensor_scalar(q_ms[:, j, :], rows[:, 4 * j:4 * j + 4], HD * 1e-5, None, ALU.add).then_inc(s["q_ms"], 1)
                            if j - Q + 1 in (0, 1):
                                peaks(g, j - Q + 1)
                            if j == QS - 3:
                                inverse(g, 0)
                        inverse(g, 1)
                    else:
                        dve.wait_ge(s["v_evac"], T)
                        dve.wait_ge(s["pv"], U * g)
                        dve.tensor_scalar(v_g[:, :, :], v_all[:, :, bass.ds(g * HD, HD)], 1.0, None, ALU.mult).then_inc(s["v_g"], 1)
                    for u in range(2 if a.normed else 0, U + LAG + 1):
                        if u < U:
                            peaks(g, u)
                        if (2 if a.normed else 0) <= u - 1 < U:
                            inverse(g, u - 1)
                        if a.normed and u == LAG:
                            dve.wait_ge(s["q_ssq"], QS * (g + 1))
                            dve.tensor_scalar(q_ms[:, QS - 1:QS + 1, :].rearrange("p a n -> p (a n)"), proj[0][:, 0:8], HD * 1e-5, None,
                                              ALU.add).then_inc(s["q_ms"], 1)
                        v = u - LAG
                        if v > 0 and v % PARTS == 0:
                            add_rows(g, v // PARTS - 1)
                        if 0 <= v < U:
                            b, h0 = v // PARTS, (v % PARTS) * NQ
                            dve.wait_ge(s["out_hi"], U * g + v + 1)
                            dve.tensor_tensor(out_lo[:, b % 2, h0:h0 + NQ, :].rearrange("p h n -> p (h n)"), mixed[v % 2][0:HD, 0:NQ * P],
                                              raw(out_hi[:, b % 2, h0:h0 + NQ, :]).rearrange("p h n -> p (h n)"), ALU.subtract).then_inc(s["out_lo"], 1)

                def add_rows(g, b):
                    dve.wait_ge(s["rows"], B * g + b + 1)
                    dve.wait_ge(s["add"], B * g + b)
                    dve.tensor_tensor(m.xtok[:, b, :], m.xtok[:, b, :], rows[:, :], ALU.add).then_inc(s["add"], 1)

                if a.normed:
                    dve.wait_ge(s["ld_c"], 48)
                    dve.tensor_tensor(nw2[:, :], nw[:, 0:1], nw[:, 1:2], ALU.mult).then_inc(s["nw"], 1)
                group(0)
                with dve.Fori(1, G) as g:
                    group(g)
                dve.wait_ge(s["add"], B * G)
                norm_vector(dve, m, n1)


def context_stage(nc, m, io, sem):
    with ExitStack() as ctx:
        cT = ctx.enter_context(nc.sbuf_tensor("cT", [P, KC, TOK], FP32))
        ld, hi, lo = sem("c_ld"), sem("c_hi"), sem("c_lo")
        with nc.Block() as block:
            @block.sync
            def _(sp):
                sp.dma_start(cT[:, :, :], io["ctxT"].rearrange("(c p) n -> p c n", p=P)).then_inc(ld, 16)

            @block.vector
            def _(dve):
                dve.wait_ge(ld, 16)
                dve.tensor_copy(m.cT_hi[:, :, :], cT[:, :, :]).then_inc(hi, 1)
                dve.wait_ge(hi, 1)
                dve.tensor_tensor(m.cT_lo[:, :, :], cT[:, :, :], raw(m.cT_hi[:, :, :]), ALU.subtract).then_inc(lo, 1)
                dve.wait_ge(lo, 1)


def cross0_stage(nc, m, io, sem):
    attention_stage(nc, m, io, sem, Attention("xa0", 4, 96, 2, False, ("wq0", "wk0", "wv0", "wo0")))


def cross1_stage(nc, m, io, sem):
    attention_stage(nc, m, io, sem, Attention("xa1", 8, 128, 1, True, ("wq1", "wk1", "wv1", "wo1")))



INNER = 1792
MT = 2
TURNS = INNER // (MT * P)
WIDE = MT * P


def ffn0_stage(nc, m, io, sem):
    with ExitStack() as ctx:
        def sb(name, shape, dt=FP32):
            return ctx.enter_context(nc.sbuf_tensor("ff_" + name, shape, dt))

        def pb(name):
            return ctx.enter_context(nc.psum_tensor("ff_" + name, [P, HALF], FP32))

        gu_q, gu_z = (sb(n, [P, KC, 2, WIDE], INT32) for n in ("gu_q", "gu_z"))
        gu_s, gu_w = (sb(n, [P, KC, 2, WIDE]) for n in ("gu_s", "gu_w"))
        gu_hi, gu_lo = (sb(n, [P, KC, 2, WIDE], F32R) for n in ("gu_hi", "gu_lo"))
        dn_q, dn_z = (sb(n, [P, MT, D], INT32) for n in ("dn_q", "dn_z"))
        dn_s, dn_w = (sb(n, [P, MT, D]) for n in ("dn_s", "dn_w"))
        dn_hi, dn_lo = (sb(n, [P, MT, D], F32R) for n in ("dn_hi", "dn_lo"))
        act_g = sb("act_g", [P, 2, HALF])
        h = sb("h", [P, 2, HALF])
        h_hi, h_lo = (sb(n, [P, MT, TOK], F32R) for n in ("h_hi", "h_lo"))
        gate = [pb(f"gate{i}") for i in range(2)]
        up = [pb(f"up{i}") for i in range(2)]
        rows = [pb(f"rows{i}") for i in range(2)]
        m.norm_bank = gate
        s = {n: sem("ff_" + n) for n in (
            "ld_gu", "ld_dn", "sub_gu", "sub_dn", "w_gu", "w_dn", "hi_gu", "hi_dn", "lo_gu", "lo_dn", "gate",
            "up", "silu", "h", "h_hi", "h_lo", "rows", "add")}
        n2 = norm_sems(sem, "n2")
        CHAINS = 2 * MT

        with nc.Block() as block:
            @block.sync
            def _(sp):
                def load(g):
                    sp.wait_ge(s["sub_gu"], g)
                    sp.wait_ge(s["w_gu"], g)
                    cols = bass.ds(g * WIDE, WIDE)
                    for n, w in enumerate(("gate", "up")):
                        q, z, sc = (io[f"{w}_{x}"] for x in "wzs")
                        sp.dma_start(gu_q[:, :, n, :], q.rearrange("(c p) n -> p c n", p=P)[:, :, cols]).then_inc(s["ld_gu"], 16)
                        sp.dma_start(gu_z[:, :, n, :], z[:, cols].partition_broadcast(P)).then_inc(s["ld_gu"], 16)
                        sp.dma_start(gu_s[:, :, n, :], sc[:, cols].partition_broadcast(P)).then_inc(s["ld_gu"], 16)
                    sp.wait_ge(s["sub_dn"], g)
                    sp.wait_ge(s["w_dn"], g)
                    rows_ = bass.ds(g * MT, MT)
                    sp.dma_start(dn_q[:, :, :], io["down_w"].rearrange("(m p) n -> p m n", p=P)[:, rows_, :]).then_inc(s["ld_dn"], 16)
                    sp.dma_start(dn_z[:, :, :], io["down_z"][rows_, :].partition_broadcast(P)).then_inc(s["ld_dn"], 16)
                    sp.dma_start(dn_s[:, :, :], io["down_s"][rows_, :].partition_broadcast(P)).then_inc(s["ld_dn"], 16)

                load(0)
                with sp.Fori(1, TURNS) as g:
                    load(g)

            @block.gpsimd
            def _(pool):
                def scale(g):
                    pool.wait_ge(s["sub_gu"], g + 1)
                    pool.tensor_tensor(gu_w[:, :, :, :], gu_w[:, :, :, :], gu_s[:, :, :, :], ALU.mult).then_inc(s["w_gu"], 1)
                    pool.wait_ge(s["sub_dn"], g + 1)
                    pool.tensor_tensor(dn_w[:, :, :], dn_w[:, :, :], dn_s[:, :, :], ALU.mult).then_inc(s["w_dn"], 1)

                def low(g):
                    pool.wait_ge(s["hi_gu"], g + 1)
                    pool.tensor_tensor(gu_lo[:, :, :, :], gu_w[:, :, :, :], raw(gu_hi[:, :, :, :]), ALU.subtract).then_inc(s["lo_gu"], 1)
                    pool.wait_ge(s["hi_dn"], g + 1)
                    pool.tensor_tensor(dn_lo[:, :, :], dn_w[:, :, :], raw(dn_hi[:, :, :]), ALU.subtract).then_inc(s["lo_dn"], 1)

                scale(0)
                low(0)
                with pool.Fori(1, TURNS) as g:
                    scale(g)
                    low(g)
                norm_gpsimd(pool, m, n2)

            @block.tensor
            def _(pe):
                def group(g):
                    pe.wait_ge(s["lo_gu"], g + 1)
                    for j in range(CHAINS):
                        half, k = j // MT, j % MT
                        cols = slice(half * HALF, (half + 1) * HALF)
                        pe.wait_ge(s["h"], CHAINS * g + max(j - 1, 0))
                        for n, (bank, done) in enumerate(((gate[j % 2], s["gate"]), (up[j % 2], s["up"]))):
                            for c in range(KC):
                                last = three(pe, bank[:, :], gu_hi[:, c, n, k * P:(k + 1) * P], gu_lo[:, c, n, k * P:(k + 1) * P],
                                             m.xT_hi[:, c, cols], m.xT_lo[:, c, cols], c == 0, c == KC - 1)
                            last.then_inc(done, 1)
                    pe.wait_ge(s["lo_dn"], g + 1)
                    for b in range(B):
                        pe.wait_ge(s["h_lo"], CHAINS * g + MT * (b // 4 + 1))
                        pe.wait_ge(s["add"], B * g + max(b - 1, 0))
                        for k in range(MT):
                            last = three(pe, rows[b % 2][:, :], h_hi[:, k, b * P:(b + 1) * P], h_lo[:, k, b * P:(b + 1) * P],
                                         dn_hi[:, k, :], dn_lo[:, k, :], k == 0, k == MT - 1)
                        last.then_inc(s["rows"], 1)

                group(0)
                with pe.Fori(1, TURNS) as g:
                    group(g)
                norm_tensor(pe, m, n2)

            @block.scalar
            def _(act):
                def group(g):
                    for j in range(CHAINS + 1):
                        if j < CHAINS:
                            act.wait_ge(s["gate"], CHAINS * g + j + 1)
                            act.activation(act_g[:, j % 2, :], gate[j % 2][:, :], ACT.Silu).then_inc(s["silu"], 1)
                        if j:
                            n = j - 1
                            half, k = n // MT, n % MT
                            act.wait_ge(s["h"], CHAINS * g + n + 1)
                            act.wait_ge(s["rows"], B * g)
                            act.activation(h_hi[:, k, half * HALF:(half + 1) * HALF], h[:, n % 2, :], ACT.Copy).then_inc(s["h_hi"], 1)

                group(0)
                with act.Fori(1, TURNS) as g:
                    group(g)
                norm_scalar(act, m, n2)

            @block.vector
            def _(dve):
                def subtract(g):
                    dve.wait_ge(s["ld_gu"], 96 * (g + 1))
                    dve.wait_ge(s["lo_gu"], g)
                    dve.tensor_tensor(gu_w[:, :, :, :], gu_q[:, :, :, :], gu_z[:, :, :, :], ALU.subtract).then_inc(s["sub_gu"], 1)
                    dve.wait_ge(s["ld_dn"], 48 * (g + 1))
                    dve.wait_ge(s["lo_dn"], g)
                    dve.tensor_tensor(dn_w[:, :, :], dn_q[:, :, :], dn_z[:, :, :], ALU.subtract).then_inc(s["sub_dn"], 1)

                def high_gu(g):
                    dve.wait_ge(s["w_gu"], g + 1)
                    dve.wait_ge(s["up"], CHAINS * g)
                    dve.tensor_copy(gu_hi[:, :, :, :], gu_w[:, :, :, :]).then_inc(s["hi_gu"], 1)

                def high_dn(g):
                    dve.wait_ge(s["w_dn"], g + 1)
                    dve.wait_ge(s["rows"], B * g)
                    dve.tensor_copy(dn_hi[:, :, :], dn_w[:, :, :]).then_inc(s["hi_dn"], 1)

                def group(g, last):
                    for j in range(CHAINS + 1):
                        if j < CHAINS:
                            dve.wait_ge(s["silu"], CHAINS * g + j + 1)
                            dve.wait_ge(s["up"], CHAINS * g + j + 1)
                            dve.wait_ge(s["h_lo"], CHAINS * g + max(j - 1, 0))
                            dve.tensor_tensor(h[:, j % 2, :], act_g[:, j % 2, :], up[j % 2][:, :], ALU.mult).then_inc(s["h"], 1)
                        if j:
                            n = j - 1
                            half, k = n // MT, n % MT
                            dve.wait_ge(s["h_hi"], CHAINS * g + n + 1)
                            dve.tensor_tensor(h_lo[:, k, half * HALF:(half + 1) * HALF], h[:, n % 2, :],
                                              raw(h_hi[:, k, half * HALF:(half + 1) * HALF]), ALU.subtract).then_inc(s["h_lo"], 1)
                        if j == 1 and not last:
                            subtract(g + 1)
                    if not last:
                        high_gu(g + 1)
                    for b in range(B):
                        dve.wait_ge(s["rows"], B * g + b + 1)
                        dve.wait_ge(s["add"], B * g + b)
                        dve.tensor_tensor(m.xtok[:, b, :], m.xtok[:, b, :], rows[b % 2][:, :], ALU.add).then_inc(s["add"], 1)
                    if not last:
                        high_dn(g + 1)

                subtract(0)
                high_gu(0)
                high_dn(0)
                group(0, False)
                with dve.Fori(1, TURNS - 1) as g:
                    group(g, False)
                group(TURNS - 1, True)
                dve.wait_ge(s["add"], B * TURNS)
                norm_vector(dve, m, n2)



AH = 32
AD = D // AH
HC = P // AD
AC = AH // HC
AUG = AD + 1


def self_stage(nc, m, io, sem):
    with ExitStack() as ctx:
        def sb(name, shape, dt=FP32):
            return ctx.enter_context(nc.sbuf_tensor("sa_" + name, shape, dt))

        def pb(name, n=HALF):
            return ctx.enter_context(nc.psum_tensor("sa_" + name, [P, n], FP32))

        w_raw, w_hi, w_lo = (sb(n, [P, KC, 2 * P], dt) for n, dt in (("w_raw", FP32), ("w_hi", F32R), ("w_lo", F32R)))
        o_raw, o_hi, o_lo = (sb(n, [P, KC, D], dt) for n, dt in (("o_raw", FP32), ("o_hi", F32R), ("o_lo", F32R)))
        bias_qk = sb("bias_qk", [P, 2])
        bias_v = sb("bias_v", [P, D])
        bias_o = sb("bias_o", [P, D])
        own = sb("own", [P, HC])
        alibi = sb("alibi", [P, HC, S])
        qT, kT = sb("qT", [P, TOK]), sb("kT", [P, TOK])
        k_own = sb("k_own", [P, 2, HC, S])
        v = sb("v", [P, B, AH, AUG])
        prob = sb("prob", [P, 3, HC, S])
        prT = sb("prT", [P, HC, S])
        peak = sb("peak", [P, 3, HC])
        inv = sb("inv", [P, HC])
        o_tok = sb("o_tok", [P, 2, HC, AD])
        oT_hi, oT_lo = (sb(n, [P, KC, TOK], F32R) for n in ("oT_hi", "oT_lo"))
        score = [pb(f"score{i}", HC * S) for i in range(2)]
        turn = pb("turn", HC * S)
        pv = pb("pv")
        back = pb("back")
        proj = [turn[:, 0:HALF], turn[:, HALF:2 * HALF]]
        m.norm_bank = proj
        s = {n: sem("sa_" + n) for n in (
            "ld_w", "ld_qk", "ld_v", "ld_o", "ld_own", "ld_alibi", "split_hi", "split", "o_hi", "o_lo",
            "ld_wv", "wv_hi", "wv_lo", "ones", "v_proj", "proj", "v", "qk", "k_own", "score", "masked", "peak", "exp", "turn", "prT", "pv", "inv",
            "o_tok", "back", "oT_hi", "oT_lo", "res", "rows", "add")}
        n3 = norm_sems(sem, "n3")
        LAG = 2
        PROJ = 4

        with nc.Block() as block:
            @block.sync
            def _(sp):
                sp.dma_start(own[:, :], io["own"]).then_inc(s["ld_own"], 16)
                sp.dma_start(o_raw[:, :, :], io["w_qkvT"].rearrange("(c p) n -> p c n", p=P)[:, :, 2 * D:3 * D]).then_inc(s["ld_wv"], 16)
                sp.dma_start(bias_v[:, :], io["b_qkv"][2 * D:3 * D].partition_broadcast(P)).then_inc(s["ld_v"], 16)
                sp.dma_start(bias_o[:, :], io["b_out"].partition_broadcast(P)).then_inc(s["ld_o"], 16)

                def load(c):
                    sp.wait_ge(s["split"], c)
                    for n in range(2):
                        sp.dma_start(w_raw[:, :, n * P:(n + 1) * P],
                                     io["w_qkvT"].rearrange("(c p) n -> p c n", p=P)[:, :, bass.ds(c * P + n * D, P)]).then_inc(s["ld_w"], 16)
                    sp.wait_ge(s["qk"], 4 * c)
                    for n in range(2):
                        sp.dma_start(bias_qk[:, n:n + 1], io["b_qkv"][bass.ds(c * P + n * D, P)].rearrange("(p a) -> p a", a=1)).then_inc(s["ld_qk"], 16)
                    sp.wait_ge(s["masked"], B * c)
                    sp.dma_start(alibi[:, :, :], io["alibi"].rearrange("(c h) q k -> c q h k", h=HC)[bass.ds(c, 1), :, :, :]
                                 .rearrange("a q h k -> (a q) h k")).then_inc(s["ld_alibi"], 16)

                load(0)
                sp.wait_ge(s["wv_lo"], 1)
                sp.dma_start(o_raw[:, :, :], io["w_oT"].rearrange("(c p) n -> p c n", p=P)).then_inc(s["ld_o"], 16)
                with sp.Fori(1, AC) as c:
                    load(c)

            @block.gpsimd
            def _(pool):
                def split(c):
                    pool.wait_ge(s["ld_w"], 32 * (c + 1))
                    pool.wait_ge(s["proj"], PROJ * c)
                    pool.tensor_tensor(w_hi[:, :, :], w_raw[:, :, :], bc(m.ones[:, 0:1], 2, [P, KC, 2 * P]), ALU.mult).then_inc(s["split_hi"], 1)
                    pool.wait_ge(s["split_hi"], c + 1)
                    pool.tensor_tensor(w_lo[:, :, :], w_raw[:, :, :], raw(w_hi[:, :, :]), ALU.subtract).then_inc(s["split"], 1)

                def chunk(c, last):
                    for b in range(B):
                        if b == 0:
                            pool.wait_ge(s["qk"], 4 * c + 2)
                        pool.wait_ge(s["score"], B * c + max(b - 1, 0))
                        pool.tensor_tensor(k_own[:, b % 2, :, :], bc(kT[:, b * P:(b + 1) * P], 1, [P, HC, S]),
                                           bc(own[:, :], 2, [P, HC, S]), ALU.mult).then_inc(s["k_own"], 1)
                        if b == 3 and not last:
                            split(c + 1)

                pool.memset(v[:, :, :, :], 1.0).then_inc(s["ones"], 1)
                split(0)
                pool.wait_ge(s["ld_own"], 16)
                chunk(0, False)
                with pool.Fori(1, AC - 1) as c:
                    chunk(c, False)
                chunk(AC - 1, True)
                norm_gpsimd(pool, m, n3)

            @block.tensor
            def _(pe):
                def chunk(c):
                    pe.wait_ge(s["split"], c + 1)
                    for j in range(PROJ):
                        if j >= 2:
                            pe.wait_ge(s["qk"], 4 * c + j - 1)
                        n, half = 1 - j // 2, j % 2
                        cols = slice(half * HALF, (half + 1) * HALF)
                        for k in range(KC):
                            last = three(pe, proj[j % 2], w_hi[:, k, n * P:(n + 1) * P], w_lo[:, k, n * P:(n + 1) * P],
                                         m.xT_hi[:, k, cols], m.xT_lo[:, k, cols], k == 0, k == KC - 1)
                        last.then_inc(s["proj"], 1)
                    for b in range(B + LAG + 1):
                        u = b - LAG
                        if 0 <= u < B:
                            pe.wait_ge(s["exp"], B * c + u + 1)
                            for n in range(HC):
                                last = pe.transpose(turn[:, n * P:(n + 1) * P], prob[:, u % 3, n, :], m.ident[:, :])
                            last.then_inc(s["turn"], 1)
                        if b < B:
                            pe.wait_ge(s["k_own"], B * c + b + 1)
                            if b == 0:
                                pe.wait_ge(s["qk"], 4 * (c + 1))
                            if b >= 2:
                                pe.wait_ge(s["masked"], B * c + b - 1)
                            for n in range(2):
                                last = pe.matmul(score[b % 2][:, n * HALF:(n + 1) * HALF], qT[:, b * P:(b + 1) * P],
                                                 k_own[:, b % 2, :, :].rearrange("p h n -> p (h n)")[:, n * HALF:(n + 1) * HALF],
                                                 start=True, stop=True)
                            last.then_inc(s["score"], 1)
                        if u >= 1:
                            pe.wait_ge(s["o_tok"], B * c + u)
                            pe.wait_ge(s["oT_lo"], B * c + u - 1)
                            pe.transpose(back[:, 0:P], o_tok[:, (u - 1) % 2, :, :].rearrange("p h d -> p (h d)"), m.ident[:, :]).then_inc(s["back"], 1)
                        if 0 <= u < B:
                            pe.wait_ge(s["prT"], B * c + u + 1)
                            for n in range(HC):
                                last = pe.matmul(pv[:, n * AUG:(n + 1) * AUG], prT[:, n, :], v[:, u, bass.ds(c * HC + n, 1), :].rearrange("p a d -> p (a d)"),
                                                 start=True, stop=True)
                            last.then_inc(s["pv"], 1)

                pe.wait_ge(s["wv_lo"], 1)
                for t in range(B):
                    if t >= 2:
                        pe.wait_ge(s["v"], t - 1)
                    for k in range(KC):
                        last = three(pe, proj[t % 2], m.xT_hi[:, k, t * P:(t + 1) * P], m.xT_lo[:, k, t * P:(t + 1) * P],
                                     o_hi[:, k, :], o_lo[:, k, :], k == 0, k == KC - 1)
                    last.then_inc(s["v_proj"], 1)
                pe.wait_ge(s["v"], B)
                chunk(0)
                with pe.Fori(1, AC) as c:
                    chunk(c)
                pe.wait_ge(s["oT_lo"], AC * B)
                pe.wait_ge(s["o_lo"], 1)
                for b in range(B):
                    if b >= 2:
                        pe.wait_ge(s["add"], b - 1)
                    for k in range(KC):
                        last = three(pe, score[b % 2][:, 0:HALF], oT_hi[:, k, b * P:(b + 1) * P], oT_lo[:, k, b * P:(b + 1) * P],
                                     o_hi[:, k, :], o_lo[:, k, :], k == 0, k == KC - 1)
                    last.then_inc(s["rows"], 1)
                norm_tensor(pe, m, n3)

            @block.scalar
            def _(act):
                def chunk(c):
                    act.wait_ge(s["ld_qk"], 32 * (c + 1))
                    act.wait_ge(s["score"], B * c)
                    act.wait_ge(s["k_own"], B * c)
                    for j in range(4):
                        n, half = 1 - j // 2, j % 2
                        act.wait_ge(s["proj"], PROJ * c + j + 1)
                        act.activation((kT if n else qT)[:, half * HALF:(half + 1) * HALF], proj[j % 2], ACT.Identity,
                                       bias=bias_qk[:, n:n + 1]).then_inc(s["qk"], 1)
                    for b in range(B + LAG):
                        u = b - LAG
                        if u >= 0:
                            act.wait_ge(s["turn"], B * c + u + 1)
                            act.wait_ge(s["pv"], B * c + u)
                            act.activation(prT[:, :, :].rearrange("p h n -> p (h n)"), turn[:, :], ACT.Copy).then_inc(s["prT"], 1)
                        if b < B:
                            act.wait_ge(s["peak"], B * c + b + 1)
                            for n in range(HC):
                                last = act.activation(prob[:, b % 3, n, :], prob[:, b % 3, n, :], ACT.Exp, bias=peak[:, b % 3, n:n + 1])
                            last.then_inc(s["exp"], 1)

                chunk(0)
                with act.Fori(1, AC) as c:
                    chunk(c)
                norm_scalar(act, m, n3)

            @block.vector
            def _(dve):
                dve.wait_ge(s["ld_wv"], 16)
                dve.tensor_copy(o_hi[:, :, :], o_raw[:, :, :]).then_inc(s["wv_hi"], 1)
                dve.wait_ge(s["wv_hi"], 1)
                dve.tensor_tensor(o_lo[:, :, :], o_raw[:, :, :], raw(o_hi[:, :, :]), ALU.subtract).then_inc(s["wv_lo"], 1)
                dve.wait_ge(s["ones"], 1)
                dve.wait_ge(s["ld_v"], 16)
                for t in range(B):
                    dve.wait_ge(s["v_proj"], t + 1)
                    dve.tensor_tensor(v[:, t, :, 0:AD], proj[t % 2].rearrange("p (h d) -> p h d", h=AH),
                                      bias_v[:, :].rearrange("p (h d) -> p h d", h=AH), ALU.add).then_inc(s["v"], 1)
                dve.wait_ge(s["ld_o"], 32)
                dve.tensor_copy(o_hi[:, :, :], o_raw[:, :, :]).then_inc(s["o_hi"], 1)
                dve.wait_ge(s["o_hi"], 1)
                dve.tensor_tensor(o_lo[:, :, :], o_raw[:, :, :], raw(o_hi[:, :, :]), ALU.subtract).then_inc(s["o_lo"], 1)
                dve.tensor_tensor(m.xtok[:, :, :], m.xtok[:, :, :], bc(bias_o[:, :], 1, [P, B, D]), ALU.add).then_inc(s["res"], 1)

                def chunk(c):
                    dve.wait_ge(s["ld_alibi"], 16 * (c + 1))
                    for b in range(B + LAG + 1):
                        if b < B:
                            dve.wait_ge(s["score"], B * c + b + 1)
                            dve.scalar_tensor_tensor(prob[:, b % 3, :, :], score[b % 2][:, :].rearrange("p (h n) -> p h n", h=HC),
                                                     1.0 / math.sqrt(AD), alibi[:, :, :], ALU.mult, ALU.add).then_inc(s["masked"], 1)
                            dve.wait_ge(s["masked"], B * c + b + 1)
                            dve.tensor_reduce(peak[:, b % 3, :], prob[:, b % 3, :, :], AX, ALU.max, negate=True).then_inc(s["peak"], 1)
                        u = b - LAG
                        if u >= 1:
                            dve.wait_ge(s["back"], B * c + u)
                            cols = oT_hi[:, bass.ds(c, 1), (u - 1) * P:u * P].rearrange("p a n -> p (a n)")
                            low = oT_lo[:, bass.ds(c, 1), (u - 1) * P:u * P].rearrange("p a n -> p (a n)")
                            dve.tensor_scalar(cols, back[:, 0:P], 1.0, None, ALU.mult).then_inc(s["oT_hi"], 1)
                            dve.wait_ge(s["oT_hi"], B * c + u)
                            dve.tensor_tensor(low, back[:, 0:P], raw(cols), ALU.subtract).then_inc(s["oT_lo"], 1)
                        if 0 <= u < B:
                            got = pv[:, 0:HC * AUG].rearrange("p (h d) -> p h d", h=HC)
                            dve.wait_ge(s["pv"], B * c + u + 1)
                            dve.reciprocal(inv[:, :], got[:, :, AD]).then_inc(s["inv"], 1)
                            dve.wait_ge(s["inv"], B * c + u + 1)
                            dve.tensor_tensor(o_tok[:, u % 2, :, :], got[:, :, 0:AD], bc(inv[:, :], 2, [P, HC, AD]), ALU.mult).then_inc(s["o_tok"], 1)

                chunk(0)
                with dve.Fori(1, AC) as c:
                    chunk(c)
                dve.wait_ge(s["res"], 1)
                for b in range(B):
                    dve.wait_ge(s["rows"], b + 1)
                    dve.tensor_tensor(m.xtok[:, b, :], m.xtok[:, b, :], score[b % 2][:, 0:HALF], ALU.add).then_inc(s["add"], 1)
                dve.wait_ge(s["add"], B)
                norm_vector(dve, m, n3)



E_, R_ = 8, 16
SCALING = 2.0
Q_FIRST, Q_END = 107, S - 1


def lora_stage(nc, m, io, sem):
    with ExitStack() as ctx:
        def sb(name, shape, dt=FP32):
            return ctx.enter_context(nc.sbuf_tensor("lo_" + name, shape, dt))

        def pb(name):
            return ctx.enter_context(nc.psum_tensor("lo_" + name, [P, HALF], FP32))

        WA = D + P
        w_raw, w_hi, w_lo = (sb(n, [P, KC, WA], dt) for n, dt in (("w_raw", FP32), ("w_hi", F32R), ("w_lo", F32R)))
        b_raw, b_hi, b_lo = (sb(n, [P, D], dt) for n, dt in (("b_raw", FP32), ("b_hi", F32R), ("b_lo", F32R)))
        bias = sb("bias", [P, D])
        r_w = sb("r_w", [P, KC, E_])
        r_b = sb("r_b", [B, E_])
        q_hi, q_lo, q = (sb(n, [P, KC, B]) for n in ("q_hi", "q_lo", "q"))
        lg, pr, wide = sb("lg", [B, E_]), sb("pr", [B, E_]), sb("wide", [B, E_, R_])
        pk, tot, inv = (sb(n, [B, 1]) for n in ("pk", "tot", "inv"))
        route = sb("route", [P, B])
        t = sb("t", [P, B, S])
        t_hi, t_lo = (sb(n, [P, B, S], F32R) for n in ("t_hi", "t_lo"))
        low = [pb(f"low{i}") for i in range(2)]
        rows = [pb(f"rows{i}") for i in range(2)]
        small = pb("small")
        s = {n: sem("lo_" + n) for n in (
            "ld_w", "ld_s", "hi", "lo", "chain", "q", "logits", "lg", "exp", "wide", "route", "low", "t_hi",
            "t_lo", "res", "rows", "add", "stored")}
        n5 = norm_sems(sem, "n5")

        with nc.Block() as block:
            @block.sync
            def _(sp):
                sp.dma_start(r_w[:, :, :], io["r_wT"].rearrange("(c p) n -> p c n", p=P)).then_inc(s["ld_s"], 16)
                sp.dma_start(r_b[:, :], io["r_b"].partition_broadcast(B)).then_inc(s["ld_s"], 16)
                sp.dma_start(bias[:, :], io["f_b"].partition_broadcast(P)).then_inc(s["ld_s"], 16)
                sp.dma_start(w_raw[:, :, D:WA], io["f_aT"].rearrange("(c p) n -> p c n", p=P)).then_inc(s["ld_w"], 16)
                sp.dma_start(w_raw[:, :, 0:D], io["f_wT"].rearrange("(c p) n -> p c n", p=P)).then_inc(s["ld_w"], 16)
                sp.dma_start(b_raw[:, :], io["f_bT"]).then_inc(s["ld_w"], 16)
                for b in range(B):
                    sp.wait_ge(n5["x"], b + 1)
                    sp.dma_start(io["out"][b, :, :], m.xtok[:, b, :]).then_inc(s["stored"], 16)
                sp.wait_ge(s["stored"], 16 * B)

            @block.gpsimd
            def _(pool):
                pool.wait_ge(s["ld_w"], 48)
                pool.wait_ge(s["hi"], 2)
                pool.tensor_tensor(w_lo[:, :, :], w_raw[:, :, :], raw(w_hi[:, :, :]), ALU.subtract).then_inc(s["lo"], 1)
                pool.tensor_tensor(b_lo[:, :], b_raw[:, :], raw(b_hi[:, :]), ALU.subtract).then_inc(s["lo"], 1)
                norm_gpsimd(pool, m, n5)

            @block.tensor
            def _(pe):
                pe.wait_ge(s["ld_s"], 48)
                pe.wait_ge(s["q"], 1)
                for c in range(KC):
                    last = pe.matmul(small[0:B, 0:E_], q[:, c, :], r_w[:, c, :], start=c == 0, stop=c == KC - 1)
                last.then_inc(s["logits"], 1)
                pe.wait_ge(s["lo"], 1)
                for n in range(2):
                    for c in range(KC):
                        last = three(pe, low[n][:, :], w_hi[:, c, D:WA], w_lo[:, c, D:WA], m.xT_hi[:, c, n * HALF:(n + 1) * HALF],
                                     m.xT_lo[:, c, n * HALF:(n + 1) * HALF], c == 0, c == KC - 1)
                    last.then_inc(s["low"], 1)
                pe.wait_ge(s["wide"], 1)
                pe.matmul(small[:, 64:64 + B], wide[:, :, :].rearrange("b e r -> b (e r)"), m.ident[0:B, 0:B], start=True, stop=True).then_inc(s["route"], 1)
                pe.wait_ge(s["lo"], 2)
                for b in range(B):
                    if b >= 2:
                        pe.wait_ge(s["add"], b - 1)
                    for c in range(KC):
                        three(pe, rows[b % 2][:, :], m.xT_hi[:, c, b * P:(b + 1) * P], m.xT_lo[:, c, b * P:(b + 1) * P],
                              w_hi[:, c, 0:D], w_lo[:, c, 0:D], c == 0, False)
                    pe.wait_ge(s["t_lo"], 1)
                    three(pe, rows[b % 2][:, :], t_hi[:, b, :], t_lo[:, b, :], b_hi[:, :], b_lo[:, :], False, True).then_inc(s["rows"], 1)

            @block.scalar
            def _(act):
                act.wait_ge(s["lg"], 1)
                act.activation(pr[:, :], lg[:, :], ACT.Exp, bias=pk[:, :], accum_out=tot[:, :]).then_inc(s["exp"], 1)

            @block.vector
            def _(dve):
                ch = Chain(dve, s["chain"])
                for src, dst in ((m.xT_hi, q_hi), (m.xT_lo, q_lo)):
                    ch.step(dve.tensor_reduce(dst[:, :, :].rearrange("p c b -> p (c b)"),
                                              raw(src[:, :, :]).rearrange("p c (b s) -> p (c b) s", s=S)[:, :, Q_FIRST:Q_END], AX, ALU.add))
                ch.step(dve.tensor_tensor(q[:, :, :], q_hi[:, :, :], q_lo[:, :, :], ALU.add))
                dve.tensor_scalar(q[:, :, :], q[:, :, :], 1.0 / (Q_END - Q_FIRST), None, ALU.mult).then_inc(s["q"], 1)
                dve.wait_ge(s["ld_w"], 48)
                dve.tensor_copy(w_hi[:, :, :], w_raw[:, :, :]).then_inc(s["hi"], 1)
                dve.tensor_copy(b_hi[:, :], b_raw[:, :]).then_inc(s["hi"], 1)
                dve.wait_ge(s["ld_s"], 48)
                dve.wait_ge(s["logits"], 1)
                ch.step(dve.tensor_tensor(lg[:, :], small[0:B, 0:E_], r_b[:, :], ALU.add))
                dve.tensor_reduce(pk[:, :], lg[:, :], AX, ALU.max, negate=True).then_inc(s["lg"], 1)
                dve.wait_ge(s["exp"], 1)
                ch.step(dve.reciprocal(inv[:, :], tot[:, :]))
                ch.step(dve.tensor_scalar(pr[:, :], pr[:, :], inv[:, :], SCALING, ALU.mult, ALU.mult))
                dve.tensor_copy(wide[:, :, :], bc(pr[:, :], 2, [B, E_, R_])).then_inc(s["wide"], 1)
                dve.wait_ge(s["route"], 1)
                ch.step(dve.tensor_copy(route[:, :], small[:, 64:64 + B]))
                dve.wait_ge(s["low"], 2)
                for n in range(2):
                    bs = slice(4 * n, 4 * n + 4)
                    ch.step(dve.tensor_tensor(t[:, bs, :], low[n][:, :].rearrange("p (b s) -> p b s", b=4), bc(route[:, bs], 2, [P, 4, S]), ALU.mult))
                dve.tensor_copy(t_hi[:, :, :], t[:, :, :]).then_inc(s["t_hi"], 1)
                dve.wait_ge(s["t_hi"], 1)
                dve.tensor_tensor(t_lo[:, :, :], t[:, :, :], raw(t_hi[:, :, :]), ALU.subtract).then_inc(s["t_lo"], 1)
                dve.tensor_tensor(m.xtok[:, :, :], m.xtok[:, :, :], bc(bias[:, :], 1, [P, B, D]), ALU.add).then_inc(s["res"], 1)
                dve.wait_ge(s["res"], 1)
                for b in range(B):
                    dve.wait_ge(s["rows"], b + 1)
                    dve.tensor_tensor(m.xtok[:, b, :], m.xtok[:, b, :], rows[b % 2][:, :], ALU.add).then_inc(s["add"], 1)
                dve.wait_ge(s["add"], B)
                norm_vector(dve, m, n5, transposed=False)



STAGES = (hydra_stage, context_stage, cross0_stage, ffn0_stage, self_stage, cross1_stage, lora_stage)


def program(nc, io):
    with ExitStack() as ctx:
        def sb(name, shape, dt=FP32):
            return ctx.enter_context(nc.sbuf_tensor(name, shape, dt))

        m = Memory(sb)
        for n, stage in enumerate(STAGES):
            used = []

            def sem(name):
                used.append(nc.alloc_semaphore(name))
                return used[-1]

            stage(nc, m, io, sem)
            if n < len(STAGES) - 1:
                nc.clear_and_free_semaphores(used)
                nc.all_engine_barrier()



def own_features():
    return np.repeat(np.eye(HC, dtype=np.float32), AD, axis=0)


def alibi_bias():
    slopes = np.float32(1.0) / np.power(np.float32(2.0), np.arange(1, AH + 1, dtype=np.float32) * np.float32(8 / AH))
    bias = slopes[:, None] * np.arange(1 - S, 1, dtype=np.float32)[None, :]
    causal = np.arange(S)[:, None] >= np.arange(S)[None, :]
    return np.where(causal[None], bias[:, None, :], np.float32(-1e9)).astype(np.float32)


def kernel(**inputs):
    import concourse.bacc as bacc
    from concourse.bass_utils import run_bass_kernel_spmd

    a = {n: np.asarray(v) for n, v in inputs.items()}

    def T(x):
        return np.ascontiguousarray(x.T)

    host = {
        "x": a["x"], "xT": T(a["x"].reshape(TOK, D)),
        "w_downT": T(a["L0_attn_w_down"]), "b_down": a["L0_attn_b_down"], "w_upT": T(a["L0_attn_w_up"]),
        "b_up": a["L0_attn_b_up"], "gate1": a["L0_attn_gate1"].reshape(1), "in_wT": T(a["L0_attn_hy_in_w"]),
        "conv_w": T(a["L0_attn_hy_conv_w"][:, 0, :]), "conv_b": a["L0_attn_hy_conv_b"],
        "dt_bias": a["L0_attn_hy_dt_bias"], "a_log": a["L0_attn_hy_A_log"], "d_skip": a["L0_attn_hy_D"],
        "fcD_wT": T(a["L0_attn_hy_fcD_w"]), "norm_w": a["L0_attn_hy_norm_w"], "out_wT": T(a["L0_attn_hy_out_w"]),
        "ctxT": T(a["ctx_4096"].reshape(TOK, D)), "mask": a["mask_1x1xSxS2_ff0"],
        **{w.lower() + n: T(a[f"L{n}_xattn_{w}"]) for n in "01" for w in ("Wq", "Wk", "Wv", "Wo")},
        **{f"{w}_{x}": a[f"L0_ffn_{w}_{x}"] for w in ("gate", "up", "down") for x in "wzs"},
        "w_qkvT": T(a["L1_attn_w_qkv"]), "b_qkv": a["L1_attn_b_qkv"], "w_oT": T(a["L1_attn_w_out"]), "b_out": a["L1_attn_b_out"],
        "own": own_features(), "alibi": alibi_bias(),
        "f_wT": T(a["L1_ffn_W"]), "f_b": a["L1_ffn_b"], "f_aT": T(a["L1_ffn_A"].reshape(E_ * R_, D)),
        "f_bT": np.ascontiguousarray(a["L1_ffn_B"].transpose(0, 2, 1)).reshape(E_ * R_, D),
        "r_wT": T(a["L1_ffn_router_W"]), "r_b": a["L1_ffn_router_b"],
        "q_norm": a["L1_xattn_q_norm_w"], "k_norm": a["L1_xattn_k_norm_w"],
    }
    nc = bacc.Bacc("TRN2", target_bir_lowering=False, num_devices=1)
    arrays, io = {}, {}
    for name, v in host.items():
        arrays["in_" + name] = v
        tensor = nc.dram_tensor("in_" + name, v.shape, mybir.dt.from_np(v.dtype), kind="ExternalInput").ap()
        io[name] = tensor
    io["out"] = nc.dram_tensor("out", (B, S, D), FP32, kind="ExternalOutput").ap()
    program(nc, io)
    r = run_bass_kernel_spmd(nc, [arrays], core_ids=[0])
    return r.results[0]["out"]
```
